# Optimizing a Trainium2 kernel written in Bass

```python
import numpy as np
import jax
import jax.numpy as jnp

def _softmax(x, axis=-1):
    return jax.nn.softmax(x, axis=axis)
def _gelu(x):
    return jax.nn.gelu(x, approximate=True)
def _silu(x):
    return jax.nn.silu(x)
def _sigmoid(x):
    return jax.nn.sigmoid(x)
def _layernorm(x, axis=-1, eps=1e-5):
    m = jnp.mean(x, axis=axis, keepdims=True)
    v = jnp.var(x, axis=axis, keepdims=True)
    return (x - m) / jnp.sqrt(v + eps)
def _scatter_add(tgt, idx, src, axis=0):
    return tgt.at[idx].add(src)
def _segment_sum(src, seg, n):
    return jax.ops.segment_sum(src, seg, n)

kernel_name = 'mk_conv_attn_hybrid_d2_conv_nchw128_340f67'

def setup_inputs(seed: int = 0):
    np.random.seed(seed)
    _w = jnp.asarray
    def _rec_inputs():
        import jax
        import jax.numpy as jnp
        _gk = jax.random.key(seed)
        x = -0.0002928 + 1 * jax.random.normal(jax.random.fold_in(_gk, 1), (8, 128, 64, 64), jnp.float32)
        return x
    x = _rec_inputs()
    def _L0_conv_setup():
        import jax, jax.numpy as jnp
        import numpy as np
        D_MODEL = 128
        D_STATE = 16
        D_CONV = 2
        EXPAND = 2
        D_INNER = EXPAND * D_MODEL
        DT_RANK = (D_MODEL + 15) // 16
        GROUPS = 4
        EPS = 1e-05

        def _causal_conv_k2(x, w, b):
            xp = jnp.pad(x, ((0, 0), (1, 0), (0, 0)))
            return xp[:, :-1] * w[:, 0] + xp[:, 1:] * w[:, 1] + b

        def _selective_scan(xc, dt, Bmat, Cmat, A, D):

            def step(h, inp):
                dt_t, B_t, C_t, x_t = inp
                dA = jnp.exp(dt_t[..., None] * A)
                dBx = dt_t[..., None] * B_t[:, None, :] * x_t[..., None]
                h = dA * h + dBx
                y = jnp.einsum('bdn,bn->bd', h, C_t)
                return (h, y)
            B_, L, Din = xc.shape
            h0 = jnp.zeros((B_, Din, A.shape[1]), dtype=xc.dtype)
            xs = (jnp.swapaxes(dt, 0, 1), jnp.swapaxes(Bmat, 0, 1), jnp.swapaxes(Cmat, 0, 1), jnp.swapaxes(xc, 0, 1))
            _, ys = jax.lax.scan(step, h0, xs)
            return jnp.swapaxes(ys, 0, 1) + xc * D

        def _mamba(x, W_in, conv_w, conv_b, W_x, W_dt, b_dt, A_log, D, W_out):
            xz = x @ W_in
            xh, z = jnp.split(xz, 2, axis=-1)
            xh = jax.nn.silu(_causal_conv_k2(xh, conv_w, conv_b))
            x_dbl = xh @ W_x
            dt_low = x_dbl[..., :DT_RANK]
            Bmat = x_dbl[..., DT_RANK:DT_RANK + D_STATE]
            Cmat = x_dbl[..., DT_RANK + D_STATE:]
            dt = jax.nn.softplus(dt_low @ W_dt + b_dt)
            A = -jnp.exp(A_log)
            y = _selective_scan(xh, dt, Bmat, Cmat, A, D)
            y = y * jax.nn.silu(z)
            return y @ W_out

        def _group_norm(x, gamma, beta):
            B_, C, H, W = x.shape
            xr = x.reshape(B_, GROUPS, -1)
            mean = xr.mean(-1, keepdims=True)
            var = xr.var(-1, keepdims=True)
            xn = ((xr - mean) * jax.lax.rsqrt(var + EPS)).reshape(B_, C, H, W)
            return xn * gamma[:, None, None] + beta[:, None, None]
        key = jax.random.key(seed)
        ks = jax.random.split(key, 12)
        s = lambda k, shape, sc=0.02: jax.random.normal(k, shape, dtype=jnp.float32) * sc
        inp = {'x_hsi': jax.random.normal(ks[0], (8, D_MODEL, 64, 64), dtype=jnp.float32), 'W_in': s(ks[1], (D_MODEL, 2 * D_INNER)), 'conv_w': s(ks[2], (D_INNER, D_CONV), 0.5), 'conv_b': s(ks[3], (D_INNER,), 0.1), 'W_x': s(ks[4], (D_INNER, DT_RANK + 2 * D_STATE)), 'W_dt': s(ks[5], (DT_RANK, D_INNER), 0.1), 'b_dt': s(ks[6], (D_INNER,), 0.1), 'A_log': jnp.log(jnp.broadcast_to(jnp.arange(1, D_STATE + 1, dtype=jnp.float32), (D_INNER, D_STATE))), 'D': jnp.ones((D_INNER,), dtype=jnp.float32), 'W_out': s(ks[7], (D_INNER, D_MODEL)), 'gn_gamma': jnp.ones((D_MODEL,), dtype=jnp.float32), 'gn_beta': jnp.zeros((D_MODEL,), dtype=jnp.float32)}
        return inp
    _L0_conv_all = _L0_conv_setup()
    _L0_conv_in = {k: v for k, v in _L0_conv_all.items() if k in ('W_in', 'conv_w', 'conv_b', 'W_x', 'W_dt', 'b_dt', 'A_log', 'D', 'W_out', 'gn_gamma', 'gn_beta', )}
    del _L0_conv_all

    def _L1_attn_setup():
        import jax, jax.numpy as jnp
        import numpy as np
        B, S, H, A = (8, 1024, 128, 16)
        key = jax.random.key(seed)
        ks = jax.random.split(key, 5)
        scale = 1.0 / np.sqrt(2 * H)
        return {'x': jax.random.normal(ks[0], (B, S, H), dtype=jnp.float32), 'W1': jax.random.normal(ks[1], (2 * H, A), dtype=jnp.float32) * scale, 'b1': jax.random.normal(ks[2], (A,), dtype=jnp.float32) * scale, 'w2': jax.random.normal(ks[3], (A, 1), dtype=jnp.float32) * (1.0 / np.sqrt(A)), 'b2': jax.random.normal(ks[4], (1,), dtype=jnp.float32) * (1.0 / np.sqrt(A))}
    _L1_attn_all = _L1_attn_setup()
    _L1_attn_in = {k: v for k, v in _L1_attn_all.items() if k in ('W1', 'b1', 'w2', 'b2', )}
    del _L1_attn_all

    def _L1_ffn_setup():
        import jax, jax.numpy as jnp
        import numpy as np
        B, S, D, E, H, O, K = (512, 2048, 128, 64, 512, 128, 8)
        key = jax.random.key(seed)
        k0, k1, k2, k3 = jax.random.split(key, 4)
        x = jax.random.normal(k0, (B, S, D), dtype=jnp.float32)
        gate_w = jax.random.normal(k1, (E, D), dtype=jnp.float32) * (1.0 / np.sqrt(D))
        gate_b = jnp.zeros((E,), dtype=jnp.float32)
        weight1 = jax.random.uniform(k2, (E, D + 1, H), dtype=jnp.float32, minval=-1.0, maxval=1.0) * (1.0 / np.sqrt(D + 1))
        weight2 = jax.random.uniform(k3, (E, H + 1, O), dtype=jnp.float32, minval=-1.0, maxval=1.0) * (1.0 / np.sqrt(H + 1))
        return {'x': x, 'gate_w': gate_w, 'gate_b': gate_b, 'weight1': weight1, 'weight2': weight2}
    _L1_ffn_all = _L1_ffn_setup()
    _L1_ffn_in = {k: v for k, v in _L1_ffn_all.items() if k in ('gate_w', 'gate_b', 'weight1', 'weight2', )}
    del _L1_ffn_all

    return {
        "x": x,
        "L0_conv_W_in": _L0_conv_in["W_in"],
        "L0_conv_conv_w": _L0_conv_in["conv_w"],
        "L0_conv_conv_b": _L0_conv_in["conv_b"],
        "L0_conv_W_x": _L0_conv_in["W_x"],
        "L0_conv_W_dt": _L0_conv_in["W_dt"],
        "L0_conv_b_dt": _L0_conv_in["b_dt"],
        "L0_conv_A_log": _L0_conv_in["A_log"],
        "L0_conv_D": _L0_conv_in["D"],
        "L0_conv_W_out": _L0_conv_in["W_out"],
        "L0_conv_gn_gamma": _L0_conv_in["gn_gamma"],
        "L0_conv_gn_beta": _L0_conv_in["gn_beta"],
        "L1_attn_W1": _L1_attn_in["W1"],
        "L1_attn_b1": _L1_attn_in["b1"],
        "L1_attn_w2": _L1_attn_in["w2"],
        "L1_attn_b2": _L1_attn_in["b2"],
        "L1_ffn_gate_w": _L1_ffn_in["gate_w"],
        "L1_ffn_gate_b": _L1_ffn_in["gate_b"],
        "L1_ffn_weight1": _L1_ffn_in["weight1"],
        "L1_ffn_weight2": _L1_ffn_in["weight2"],
    }

def reference(x, L0_conv_W_in, L0_conv_conv_w, L0_conv_conv_b, L0_conv_W_x, L0_conv_W_dt, L0_conv_b_dt, L0_conv_A_log, L0_conv_D, L0_conv_W_out, L0_conv_gn_gamma, L0_conv_gn_beta, L1_attn_W1, L1_attn_b1, L1_attn_w2, L1_attn_b2, L1_ffn_gate_w, L1_ffn_gate_b, L1_ffn_weight1, L1_ffn_weight2):
    import jax
    import jax.numpy as jnp
    def _L0_conv_ref(x_hsi, W_in, conv_w, conv_b, W_x, W_dt, b_dt, A_log, D, W_out, gn_gamma, gn_beta):
        import jax, jax.numpy as jnp
        import numpy as np
        D_MODEL = 128
        D_STATE = 16
        D_CONV = 2
        EXPAND = 2
        D_INNER = EXPAND * D_MODEL
        DT_RANK = (D_MODEL + 15) // 16
        GROUPS = 4
        EPS = 1e-05

        def _causal_conv_k2(x, w, b):
            xp = jnp.pad(x, ((0, 0), (1, 0), (0, 0)))
            return xp[:, :-1] * w[:, 0] + xp[:, 1:] * w[:, 1] + b

        def _selective_scan(xc, dt, Bmat, Cmat, A, D):

            def step(h, inp):
                dt_t, B_t, C_t, x_t = inp
                dA = jnp.exp(dt_t[..., None] * A)
                dBx = dt_t[..., None] * B_t[:, None, :] * x_t[..., None]
                h = dA * h + dBx
                y = jnp.einsum('bdn,bn->bd', h, C_t)
                return (h, y)
            B_, L, Din = xc.shape
            h0 = jnp.zeros((B_, Din, A.shape[1]), dtype=xc.dtype)
            xs = (jnp.swapaxes(dt, 0, 1), jnp.swapaxes(Bmat, 0, 1), jnp.swapaxes(Cmat, 0, 1), jnp.swapaxes(xc, 0, 1))
            _, ys = jax.lax.scan(step, h0, xs)
            return jnp.swapaxes(ys, 0, 1) + xc * D

        def _mamba(x, W_in, conv_w, conv_b, W_x, W_dt, b_dt, A_log, D, W_out):
            xz = x @ W_in
            xh, z = jnp.split(xz, 2, axis=-1)
            xh = jax.nn.silu(_causal_conv_k2(xh, conv_w, conv_b))
            x_dbl = xh @ W_x
            dt_low = x_dbl[..., :DT_RANK]
            Bmat = x_dbl[..., DT_RANK:DT_RANK + D_STATE]
            Cmat = x_dbl[..., DT_RANK + D_STATE:]
            dt = jax.nn.softplus(dt_low @ W_dt + b_dt)
            A = -jnp.exp(A_log)
            y = _selective_scan(xh, dt, Bmat, Cmat, A, D)
            y = y * jax.nn.silu(z)
            return y @ W_out

        def _group_norm(x, gamma, beta):
            B_, C, H, W = x.shape
            xr = x.reshape(B_, GROUPS, -1)
            mean = xr.mean(-1, keepdims=True)
            var = xr.var(-1, keepdims=True)
            xn = ((xr - mean) * jax.lax.rsqrt(var + EPS)).reshape(B_, C, H, W)
            return xn * gamma[:, None, None] + beta[:, None, None]
        B_, C, H, W = x_hsi.shape
        x = jnp.transpose(x_hsi, (0, 2, 3, 1)).reshape(B_, H * W, C)
        x = _mamba(x, W_in, conv_w, conv_b, W_x, W_dt, b_dt, A_log, D, W_out)
        x = jnp.transpose(x.reshape(B_, H, W, C), (0, 3, 1, 2))
        x = jax.nn.silu(_group_norm(x, gn_gamma, gn_beta))
        return x + x_hsi

    def _L1_attn_ref(x, W1, b1, w2, b2):
        import jax, jax.numpy as jnp
        import numpy as np
        B, S, H, A = (8, 1024, 128, 16)
        h = x.shape[-1]
        f = jnp.einsum('bih,ha->bia', x, W1[:h])
        g = jnp.einsum('bjh,ha->bja', x, W1[h:])
        t = jnp.tanh(f[:, :, None, :] + g[:, None, :, :] + b1)
        scores = jnp.einsum('bija,a->bij', t, w2[:, 0]) + b2[0]
        n_seq = x.shape[1]
        flag = jnp.tril(jnp.ones((n_seq, n_seq), dtype=x.dtype), -1)[None, :, :]
        e = jnp.exp(scores) * flag
        denom = jnp.sum(e, axis=-1, keepdims=True) + 1e-10
        w = e / denom
        return jnp.einsum('bij,bjh->bih', w, x)

    def _L1_ffn_ref(x, gate_w, gate_b, weight1, weight2):
        import jax, jax.numpy as jnp
        import numpy as np
        B, S, D, E, H, O, K = (512, 2048, 128, 64, 512, 128, 8)
        Bn, Sn, Dn = x.shape
        logits = jnp.einsum('bsd,ed->bse', x, gate_w) + gate_b
        probs = jax.nn.softmax(logits, axis=1)
        vals, idx = jax.lax.top_k(probs.transpose(0, 2, 1), K)
        topv = vals.transpose(0, 2, 1)
        topi = idx.transpose(0, 2, 1)
        flat_idx = topi.reshape(Bn, K * E)
        gathered = jnp.take_along_axis(x, flat_idx[:, :, None], axis=1)
        gathered = gathered.reshape(Bn, K, E, Dn)
        pooled = jnp.einsum('bked,bke->bed', gathered, topv)
        ones = jnp.ones((E, Bn, 1), dtype=x.dtype)
        h = jnp.concatenate([pooled.transpose(1, 0, 2), ones], axis=-1)
        h = jax.nn.gelu(jnp.einsum('ebd,edh->ebh', h, weight1), approximate=False)
        h = jnp.concatenate([h, ones], axis=-1)
        out = jnp.einsum('ebh,eho->ebo', h, weight2)
        out = out.transpose(1, 0, 2)
        weighted = jnp.einsum('beo,bke->bkeo', out, topv).reshape(Bn, K * E, O)
        outputs = jnp.zeros((Bn, Sn, O), dtype=x.dtype)
        outputs = outputs.at[jnp.arange(Bn)[:, None], flat_idx].add(weighted)
        return outputs

    def _gn(v, G=32, eps=1e-5):
        B_, C_, H_, W_ = v.shape
        g = v.reshape(B_, G, C_ // G, H_, W_)
        m = jnp.mean(g, axis=(2, 3, 4), keepdims=True)
        s = jnp.var(g, axis=(2, 3, 4), keepdims=True)
        return ((g - m) / jnp.sqrt(s + eps)).reshape(v.shape)

    def _ln_c(v, eps=1e-6):
        m = jnp.mean(v, axis=1, keepdims=True)
        s = jnp.var(v, axis=1, keepdims=True)
        return (v - m) / jnp.sqrt(s + eps)

    def _ln_t(v, eps=1e-5):
        m = jnp.mean(v, axis=-1, keepdims=True)
        s = jnp.var(v, axis=-1, keepdims=True)
        return (v - m) / jnp.sqrt(s + eps)

    def _to_tokens(v):
        B_, C_, H_, W_ = v.shape
        return v.reshape(B_, C_, H_ * W_).transpose(0, 2, 1)
    def _from_tokens(t, like):
        B_, C_, H_, W_ = like.shape
        return t.transpose(0, 2, 1).reshape(B_, C_, H_, W_)

    x = _L0_conv_ref(x, L0_conv_W_in, L0_conv_conv_w, L0_conv_conv_b, L0_conv_W_x, L0_conv_W_dt, L0_conv_b_dt, L0_conv_A_log, L0_conv_D, L0_conv_W_out, L0_conv_gn_gamma, L0_conv_gn_beta)
    t = _to_tokens(x)
    t = t + _L1_attn_ref(_ln_t(t), L1_attn_W1, L1_attn_b1, L1_attn_w2, L1_attn_b2)
    t = t + _L1_ffn_ref(_ln_t(t), L1_ffn_gate_w, L1_ffn_gate_b, L1_ffn_weight1, L1_ffn_weight2)
    x = _from_tokens(t, x)
    return x


_drawn_inputs = setup_inputs


def setup_inputs(seed=0):
    import zlib

    import numpy as np

    out = dict(_drawn_inputs(seed))
    spreads = {'L0_conv_D': (1.0, 0.2),
     'L0_conv_gn_gamma': (1.0, 0.2),
     'L0_conv_gn_beta': (0.0, 0.1),
     'L1_ffn_gate_b': (0.0, 0.8)}
    factors = {'L0_conv_W_x': 8.0,
     'L0_conv_W_dt': 8.0,
     'L0_conv_b_dt': 8.0,
     'L0_conv_A_log': 8.0,
     'L1_attn_b1': 22.028,
     'L1_ffn_gate_w': 8.0,
     'L1_ffn_weight1': 8.0,
     'L1_ffn_weight2': 8.0}
    for name, (base, spread) in spreads.items():
        noise = np.random.default_rng([zlib.crc32(name.encode()), seed]).standard_normal(out[name].shape)
        drawn = base * np.exp(spread * noise) if base else spread * noise
        out[name] = jnp.asarray(drawn.astype(out[name].dtype))
    for name, factor in factors.items():
        out[name] = (out[name] * factor).astype(out[name].dtype)
    return out
```

```python
from contextlib import ExitStack

import concourse.bass as bass
from concourse import mybir

ALU = mybir.AluOpType
ACT = mybir.ActivationFunctionType
F32 = mybir.dt.float32
BF16 = mybir.dt.bfloat16

C = 128
L = 4096
DI = 256
NS = 16
T = 1024
SUP = 2048
NA = 16
NE = 64
NH = 512
EG = 4


class Done:

    def __init__(self, sem, step):
        self.sem, self.step, self.wanted, self.value = sem, step, False, None


class Queue:

    def __init__(self, name):
        self.name, self.items = name, []

    def __call__(self, sem, fn, waits=(), step=1):
        waits = [w for w in waits if w is not None]
        for w in waits:
            w.wanted = True
        d = Done(f"{self.name}_{sem}", step)
        d.wanted = step == 16
        self.items.append((waits, fn, d))
        return d


def flush(queues, new_sem):
    sems, owner, count = {}, {}, {}
    for q in queues:
        for _, _, d in q.items:
            if d.wanted:
                assert owner.setdefault(d.sem, q.name) == q.name
                count[d.sem] = count.get(d.sem, 0) + d.step
                d.value = count[d.sem]
                if d.sem not in sems:
                    sems[d.sem] = new_sem(d.sem)

    def emit(q, eng):
        seen = {}
        for waits, fn, d in q.items:
            need = {}
            for w in waits:
                need[w.sem] = max(need.get(w.sem, 0), w.value)
            for s, v in need.items():
                if seen.get(s, 0) < v:
                    eng.wait_ge(sems[s], v)
                    seen[s] = v
            ins = fn(eng)
            if d.wanted:
                ins.then_inc(sems[d.sem], d.step)
    return emit


def hybrid_kernel(nc, NB, x, W_in, conv_w, conv_b, W_x, W_dt, b_dt, A_log, D, W_out, gn_gamma, gn_beta,
                  W1, b1, w2, b2, gate_w, gate_b, we1, we2, out):
    ctx = ExitStack()
    with ctx:
        def sb(name, shape, dt=F32):
            return ctx.enter_context(nc.sbuf_tensor(name, shape, dt))

        PE, VE, AC, PO, SP = (Queue(n) for n in ("pe", "ve", "ac", "po", "sp"))
        TR = ctx.enter_context(nc.psum_tensor("banks", [128, 8, 512], F32))

        def dram(name, shape):
            return nc.dram_tensor(name, shape, F32, kind="Internal").ap()
        t0d = dram("t0_scratch", (NB, C, L))
        t1d = dram("t1_scratch", (NB, C, L))
        xtd = dram("xt_scratch", (NB, 128, L // 128, C))
        lgd = dram("lg_scratch", (NB, NE, L))
        fd = dram("f_scratch", (NB, NA, SUP))
        xd = x.rearrange("b c h w -> b c (h w)")
        od = out.rearrange("b c h w -> b c (h w)")

        ident = sb("ident", [128, 128])
        ones = sb("ones", [128, 8])
        WinS = sb("WinS", [128, DI])
        Wc = sb("Wc", [128, 2, DI])
        Wx = sb("Wx", [128, 2, 104])
        Wdt = sb("Wdt", [128, DI])
        Wo = sb("Wo", [128, 2, C])
        sel = sb("sel", [128, 32], BF16)
        W1f = sb("W1f", [128, 8, NA])
        W1g = sb("W1g", [128, 8, 128])
        w2b = sb("w2b", [128, 4, 32])
        gw = sb("gw", [128, NE])
        gmask = sb("gmask", [128, 4, 32])
        rmask = sb("rmask", [128, 8])
        cb = sb("cb", [128, 2])
        cbh = sb("cbh", [128, 2])
        bdt = sb("bdt", [128, 2])
        Dv = sb("Dv", [128, 2])
        An = sb("An", [128, 2, NS])
        gam = sb("gam", [128, 2])
        b1r = sb("b1r", [128, 1])
        w2r = sb("w2r", [128, 1])
        b2r = sb("b2r", [128, 1])
        gb = sb("gb", [128, 1])
        mhalf = sb("mhalf", [128, 4])
        arena = sb("arena", [128, 49800])
        top = [0]

        def cut(n):
            a = top[0]
            top[0] += n
            assert top[0] <= 49800, top[0]
            return arena[:, a:a + n]

        Fq = cut(SUP)
        Gk = cut(L // 8)
        xnT = cut(L).rearrange("p (k c) -> p k c", c=C)
        TH = [cut(SUP) for _ in range(6)]
        EX = [cut(SUP) for _ in range(2)]
        acc = cut(SUP)
        esum = cut(SUP)
        U = [cut(2 * T).rearrange("p (h t) -> p h t", h=2) for _ in range(2)]
        dA = [cut(2 * T).rearrange("p (h t) -> p h t", h=2) for _ in range(2)]
        Y = cut(2 * T).rearrange("p (h t) -> p h t", h=2)
        XC = cut(2 * T).rearrange("p (h t) -> p h t", h=2)
        DT = cut(2 * T).rearrange("p (h t) -> p h t", h=2)
        BCf = cut(T // 2)
        BC = BCf.bitcast(BF16)
        XS = cut(516)
        MO = cut(L)
        EPa = cut(512)
        EPb = cut(512)
        EPc = cut(512)
        EPd = cut(512)
        ST = cut(2 * NS).rearrange("p (h n) -> p h n", h=2)
        BN = cut(8 * 6).rearrange("p (k s) -> p k s", s=6)
        GS = cut(16)
        B4 = cut(4 * 6).rearrange("p (k s) -> p k s", s=6)
        MV = cut(8).rearrange("p (k s) -> p k s", s=2)
        RS = cut(8)
        RD = cut(16)

        S = {}

        def load(key, dst, src):
            S[key] = SP("const", lambda e, dst=dst, src=src: e.dma_start(dst, src), step=16)

        cwrow = TH[2][:, 0:2 * DI]
        wxl = TH[3][:, 0:2 * 40].rearrange("p (k n) -> p k n", k=2)
        w1l = TH[4][:, 0:2 * NA].rearrange("p (k n) -> p k n", k=2)
        al = TH[5][:, 0:2 * NS].rearrange("p (h n) -> p h n", h=2)
        wil = TH[1][:, 0:2 * DI]
        if True:
            load("win", wil, W_in)
            load("cw", cwrow, conv_w.rearrange("d k -> (d k)").partition_broadcast(128))
            load("cb", cb[:, :], conv_b.rearrange("(h p) -> p h", p=128))
            load("wx", wxl, W_x.rearrange("(k p) n -> p k n", p=128))
            load("wdt", Wdt[96:104, :], W_dt)
            load("bdt", bdt[:, :], b_dt.rearrange("(h p) -> p h", p=128))
            load("D", Dv[:, :], D.rearrange("(h p) -> p h", p=128))
            load("al", al, A_log.rearrange("(h p) n -> p h n", p=128))
            load("wo", Wo[:, :, :], W_out.rearrange("(k p) n -> p k n", p=128))
            load("gg", gam[:, 0:1], gn_gamma.rearrange("(p a) -> p a", a=1))
            load("gb", gam[:, 1:2], gn_beta.rearrange("(p a) -> p a", a=1))
            load("w1", w1l, W1.rearrange("(k p) n -> p k n", p=128))
            for r in range(8):
                load("b1", b1r[16 * r:16 * r + 16, :], b1.rearrange("(p a) -> p a", a=1))
                load("w2", w2r[16 * r:16 * r + 16, :], w2)
            load("b2", b2r[:, :], b2.partition_broadcast(128))
            load("gw", EPa[0:NE, 0:C], gate_w)
            load("gb2", gb[0:NE, :], gate_b.rearrange("(p a) -> p a", a=1))
            load("gb2", gb[NE:2 * NE, :], gate_b.rearrange("(p a) -> p a", a=1))
        cst = S["gb2"]

        k = PO("k", lambda e: e.memset(ident[:, :], 0.0))
        k = PO("k", lambda e: e.affine_select(out=ident[:, :], in_=ident[:, :], compare_op=ALU.not_equal, fill=1.0,
                                              base=0, pattern=[[-1, 128]], channel_multiplier=1), [k])
        k_id = k
        k = PO("k", lambda e: e.memset(sel[:, :], 0.0))
        for j in range(3):
            k = PO("k", lambda e, j=j: e.affine_select(out=sel[:, :], in_=sel[:, :], compare_op=ALU.not_equal,
                                                       fill=1.0, base=-32 * j, pattern=[[-1, 32]],
                                                       channel_multiplier=1), [k])
        for t_, v in ((gmask, 1.0 / 32), (rmask, 1.0), (ones, 1.0), (mhalf, -0.5)):
            k = PO("k", lambda e, t_=t_, v=v: e.memset(t_[:], v))
        k = PO("k", lambda e: e.affine_select(out=gmask[:, :, :], in_=gmask[:, :, :], compare_op=ALU.is_ge, fill=0.0,
                                              base=0, pattern=[[-32, 4], [0, 32]], channel_multiplier=1), [k])
        k = PO("k", lambda e: e.affine_select(out=gmask[:, :, :], in_=gmask[:, :, :], compare_op=ALU.is_ge, fill=0.0,
                                              base=31, pattern=[[32, 4], [0, 32]], channel_multiplier=-1), [k])
        k = PO("k", lambda e: e.affine_select(out=rmask[:, :], in_=rmask[:, :], compare_op=ALU.is_ge, fill=0.0,
                                              base=0, pattern=[[-16, 8]], channel_multiplier=1), [k])
        k = PO("k", lambda e: e.affine_select(out=rmask[:, :], in_=rmask[:, :], compare_op=ALU.is_ge, fill=0.0,
                                              base=15, pattern=[[16, 8]], channel_multiplier=-1), [k])
        k_po = k
        v = VE("k", lambda e: e.tensor_copy(WinS[:, :], wil[:, DI:2 * DI]), [cst])
        cw2 = cwrow.rearrange("p (d k) -> p k d", k=2)
        wil_d = DI
        for j in range(2):
            v = VE("k", lambda e, j=j: e.tensor_tensor(Wc[:, j, :], wil[:, 0:wil_d], cw2[:, j, :], ALU.mult))
        for g in range(3):
            v = VE("k", lambda e, g=g: e.tensor_copy(Wx[:, :, 32 * g:32 * g + 32], wxl[:, :, 8:40]))
        v = VE("k", lambda e: e.tensor_copy(Wx[:, :, 96:104], wxl[:, :, 0:8]))
        v = VE("k", lambda e: e.tensor_scalar(cbh[:, :], cb[:, :], 0.5, None, ALU.mult))
        v = VE("k", lambda e: e.tensor_copy(W1f[:, :, :], w1l[:, 0:1, :].to_broadcast([128, 8, NA])))
        v = VE("k", lambda e: e.memset(W1g[:, :, :], 0.0))
        v2 = VE("k", lambda e: e.memset(w2b[:, :, :], 0.0))
        for r in range(8):
            v = VE("k", lambda e, r=r: e.tensor_copy(W1g[:, r, 16 * r:16 * r + 16], w1l[:, 1, :]), [v2])
        for m in range(4):
            v = VE("k", lambda e, m=m: e.tensor_scalar(w2b[:, m, 8 * m:8 * m + 8], rmask[:, :], w2r[:, 0:1], None,
                                                       ALU.mult), [v2, k_po])
        for j in range(4):
            v = VE("k", lambda e, j=j: e.memset(TR[:, 2 * j:2 * j + 2, :], 0.0))
        a = AC("k", lambda e: e.activation(al, al, ACT.Exp), [cst])
        v = VE("k", lambda e: e.tensor_scalar(An[:, :, :], al, -1.0, None, ALU.mult), [a])
        p = PE("k", lambda e: e.transpose(TR[:, 7, 0:NE], EPa[0:NE, 0:C], ident[0:NE, 0:NE]), [cst, k_id, v])
        v = VE("k", lambda e: e.tensor_copy(gw[:, :], TR[:, 7, 0:NE]), [p])
        ready = [v, k_po, cst]

        bank_free = {5: v, 6: v, 7: v, 4: v}
        turn = [0]

        def bank():
            i = 5 + turn[0] % 3
            turn[0] += 1
            return i

        first = {"XS": None}
        free = {}

        def mamba(b):
            xb = xd[b]

            def load_x(g0, taps):
                w = [free.get("XS")]
                if g0 == 0 and taps:
                    z = VE("xs0", lambda e: e.memset(XS[:, 0:1], 0.0), w)
                    d = SP("xs", lambda e: e.dma_start(XS[:, 1:513], xb[:, 0:512]), w + [free.get("XSl")], 16)
                    return [z, d]
                lo = 1 if not taps else 0
                d = SP("xs", lambda e: e.dma_start(XS[:, lo:513], xb[:, g0 - 1 + lo:g0 + 512]),
                       w + [free.get("XSl")], 16)
                return [d]

            scan_free = {"U": [free.get("U0"), free.get("U1")], "dA": [free.get("dA0"), free.get("dA1")]}
            for c in range(L // T):
                vx = []
                for s in range(2):
                    g0 = c * T + s * 512
                    ld = load_x(g0, True)
                    free["XSl"] = ld[-1]
                    for h in range(2):
                        i = bank()
                        for kk in range(2):
                            p = PE("xh", lambda e, i=i, kk=kk, h=h: e.matmul(
                                TR[:, i, :], Wc[:, kk, h * 128:h * 128 + 128], XS[:, kk:kk + 512],
                                start=(kk == 0), stop=(kk == 1)), ld + ready + [bank_free[i]])
                        a = AC("xth", lambda e, i=i, h=h, s=s: e.activation(
                            dA[1][:, h, s * 512:s * 512 + 512], TR[:, i, :], ACT.Tanh, bias=cbh[:, h:h + 1],
                            scale=0.5), [p, scan_free["dA"][1]])
                        v1 = VE("xb", lambda e, i=i, h=h, s=s: e.tensor_scalar(
                            U[1][:, h, s * 512:s * 512 + 512], TR[:, i, :], cb[:, h:h + 1], 0.5, ALU.add, ALU.mult),
                            [p, a, scan_free["U"][1]])
                        bank_free[i] = v1
                        v1b = VE("xc", lambda e, h=h, s=s: e.scalar_tensor_tensor(
                            out=XC[:, h, s * 512:s * 512 + 512], in0=dA[1][:, h, s * 512:s * 512 + 512], scalar=1.0,
                            in1=U[1][:, h, s * 512:s * 512 + 512], op0=ALU.add, op1=ALU.mult),
                            [a, v1, free.get("XC")])
                        vx.append(v1b)
                    free["XS"] = p
                    yield 3.5
                for h in range(2):
                    vy = VE("y0", lambda e, h=h: e.tensor_scalar(Y[:, h, :], XC[:, h, :], Dv[:, h:h + 1], None,
                                                                 ALU.mult), [vx[-1], free.get("Y")])
                vdt = []
                for s in range(2):
                    i = bank()
                    for h in range(2):
                        p = PE("xdbl", lambda e, i=i, h=h, s=s: e.matmul(
                            TR[0:104, i, :], Wx[:, h, :], XC[:, h, s * 512:s * 512 + 512],
                            start=(h == 0), stop=(h == 1)), [vx[-1], bank_free[i]])
                    R = U[1][:, 0, s * 512:s * 512 + 512]
                    DL = U[1][:, 1, s * 512:s * 512 + 512]
                    mid = dA[1][:, 0, s * 256:s * 256 + 256].bitcast(BF16)
                    bcs = BC[:, s * 512:s * 512 + 512]
                    q0 = VE("dl", lambda e, i=i, DL=DL: e.tensor_copy(DL[96:104, :], TR[96:104, i, :]), [p, vx[-1]])
                    q1 = VE("s1", lambda e, i=i, bcs=bcs: e.tensor_copy(bcs[0:96, :], TR[0:96, i, :]),
                            [p, free.get("BC")])
                    q2 = VE("s2", lambda e, i=i, bcs=bcs, R=R: e.tensor_tensor(
                        R[0:96, :], TR[0:96, i, :], bcs[0:96, :], ALU.subtract), [q1])
                    bank_free[i] = q2
                    q3 = VE("s3", lambda e, mid=mid, R=R: e.tensor_copy(mid[0:96, :], R[0:96, :]), [q2])
                    q4 = VE("s4", lambda e, mid=mid, R=R: e.tensor_tensor(
                        R[0:96, :], R[0:96, :], mid[0:96, :], ALU.subtract), [q3])
                    q5 = VE("s5", lambda e, mid=mid, bcs=bcs: e.tensor_copy(bcs[32:64, :], mid[32:64, :]), [q3])
                    q6 = VE("s6", lambda e, R=R, bcs=bcs: e.tensor_copy(bcs[64:96, :], R[64:96, :]), [q4])
                    vbc = q6
                    for h in range(2):
                        i = bank()
                        p = PE("dt", lambda e, i=i, h=h, DL=DL: e.matmul(
                            TR[:, i, :], Wdt[96:104, h * 128:h * 128 + 128], DL[96:104, :], start=True, stop=True),
                            [q0, bank_free[i]])
                        ab = AC("dta", lambda e, i=i, h=h, s=s: e.activation(
                            U[0][:, h, s * 512:s * 512 + 512], TR[:, i, :], ACT.Abs, bias=bdt[:, h:h + 1]),
                            [p, scan_free["U"][0]])
                        w = VE("dtm", lambda e, i=i, h=h, s=s: e.tensor_scalar(
                            DT[:, h, s * 512:s * 512 + 512], TR[:, i, :], bdt[:, h:h + 1], 0.0, ALU.add, ALU.max),
                            [ab, free.get("DT")])
                        bank_free[i] = w
                        vdt.append(w)
                    yield 6
                a1 = AC("sp1", lambda e: e.activation(dA[0], U[0], ACT.Exp, scale=-1.0),
                        [ab, scan_free["dA"][0]])
                yield 4
                a2 = AC("sp2", lambda e: e.activation(U[0], dA[0], ACT.Ln, bias=1.0), [a1])
                g1 = PO("sp3", lambda e: e.tensor_scalar(dA[1], dA[0], 1.0, None, ALU.add), [a1, q5])
                g2 = PO("sp4", lambda e: e.tensor_scalar(dA[1], dA[1], -1.0, None, ALU.add), [g1])
                g3 = PO("sp5", lambda e: e.tensor_tensor(dA[1], dA[0], dA[1], ALU.subtract), [g2])
                v3 = VE("sp6", lambda e: e.tensor_tensor(DT, DT, U[0], ALU.add), [a2, vdt[-1]])
                yield 6
                v3 = VE("sp7", lambda e: e.tensor_tensor(DT, DT, dA[1], ALU.add), [v3, g3])
                v4 = VE("dtx", lambda e: e.tensor_tensor(XC, XC, DT, ALU.mult), [v3, vy])
                yield 5
                u_free = [v3, vbc]
                d_free = [g3, v3]
                for n in range(NS):
                    Un, An_ = U[n % 2], dA[n % 2]
                    ibc = []
                    for q in range(2):
                        for s in range(2):
                            i = bank()
                            col = q * NS + n
                            p = PE("bc", lambda e, i=i, col=col, s=s: e.matmul(
                                TR[:, i, :], sel[0:96, col:col + 1].to_broadcast([96, 128]),
                                BC[0:96, s * 512:s * 512 + 512], start=True, stop=True), [vbc, bank_free[i]])
                            ibc.append((i, p))
                            if q == 0:
                                w = VE("mb", lambda e, i=i, s=s, Un=Un: e.tensor_tensor(
                                    Un[:, :, s * 512:s * 512 + 512], XC[:, :, s * 512:s * 512 + 512],
                                    TR[:, i:i + 1, :].to_broadcast([128, 2, 512]), ALU.mult),
                                    [p, v4, u_free[n % 2]])
                                bank_free[i] = w
                                if s == 1:
                                    for h in range(2):
                                        a = AC("da", lambda e, h=h, n=n, An_=An_: e.activation(
                                            An_[:, h, :], DT[:, h, :], ACT.Exp, scale=An[:, h, n:n + 1]),
                                            [v3, d_free[n % 2]])
                                        ini = 0.0 if c == 0 else ST[:, h, n:n + 1]
                                        sc = VE("scan", lambda e, h=h, An_=An_, Un=Un, ini=ini:
                                                e.tensor_tensor_scan(Un[:, h, :], An_[:, h, :], Un[:, h, :], ini,
                                                                     ALU.mult, ALU.add), [a, w, free.get("ST")])
                                    d_free[n % 2] = sc
                                    st = VE("st", lambda e, n=n, Un=Un: e.tensor_copy(
                                        ST[:, :, n:n + 1], Un[:, :, T - 1:T]), [sc])
                                    free["ST"] = st
                            else:
                                w = VE("mc", lambda e, i=i, s=s, Un=Un: e.tensor_tensor(
                                    Un[:, :, s * 512:s * 512 + 512], Un[:, :, s * 512:s * 512 + 512],
                                    TR[:, i:i + 1, :].to_broadcast([128, 2, 512]), ALU.mult), [p, st])
                                bank_free[i] = w
                    g = PO("y", lambda e, Un=Un: e.tensor_tensor(Y, Y, Un, ALU.add), [w, vy, u_free[(n + 1) % 2]])
                    u_free[n % 2] = g
                    yield 8
                free["BC"] = p
                free["XC"] = w
                free["DT"] = a
                z0 = u_free[0]
                for s in range(2):
                    g0 = c * T + s * 512
                    ld = load_x(g0, False)
                    free["XSl"] = ld[-1]
                    for h in range(2):
                        i = bank()
                        p = PE("z", lambda e, i=i, h=h: e.matmul(
                            TR[:, i, :], WinS[:, h * 128:h * 128 + 128], XS[:, 1:513], start=True, stop=True),
                            ld + [bank_free[i]])
                        a = AC("zth", lambda e, i=i, h=h, s=s: e.activation(
                            dA[0][:, h, s * 512:s * 512 + 512], TR[:, i, :], ACT.Tanh, scale=0.5),
                            [p, d_free[0], d_free[1]])
                        w = VE("zz", lambda e, i=i, h=h, s=s: e.scalar_tensor_tensor(
                            out=U[0][:, h, s * 512:s * 512 + 512], in0=dA[0][:, h, s * 512:s * 512 + 512],
                            scalar=1.0, in1=TR[:, i, :], op0=ALU.add, op1=ALU.mult), [a, z0])
                        bank_free[i] = w
                    free["XS"] = p
                    yz = VE("yz", lambda e, s=s: e.scalar_tensor_tensor(
                        out=U[0][:, :, s * 512:s * 512 + 512], in0=Y[:, :, s * 512:s * 512 + 512], scalar=0.5,
                        in1=U[0][:, :, s * 512:s * 512 + 512], op0=ALU.mult, op1=ALU.mult), [w, g])
                    i = bank()
                    for h in range(2):
                        p = PE("mo", lambda e, i=i, h=h, s=s: e.matmul(
                            TR[:, i, :], Wo[:, h, :], U[0][:, h, s * 512:s * 512 + 512],
                            start=(h == 0), stop=(h == 1)), [yz, bank_free[i]])
                    w = VE("moc", lambda e, i=i, g0=g0: e.tensor_copy(MO[:, g0:g0 + 512], TR[:, i, :]),
                           [p, free.get("MO")])
                    VE("mobn", lambda e, i=i, kk=2 * c + s: e.bn_stats(BN[:, kk, :], TR[:, i, :]), [p])
                    bank_free[i] = VE.items[-1][2]
                    yield 5
                free["Y"] = yz
                scan_free = {"U": [p, u_free[1]], "dA": [w, d_free[1]]}
                free["U0"], free["U1"] = scan_free["U"]
                free["dA0"], free["dA1"] = scan_free["dA"]
            v = VE("gn", lambda e: e.bn_aggr(GS[:, 0:2], BN.rearrange("p k s -> p (k s)")), [bank_free[i]])
            v = VE("gn", lambda e: e.tensor_scalar(GS[:, 2:3], GS[:, 0:1], GS[:, 0:1], GS[:, 1:2], ALU.mult, ALU.add),
                   [v])
            v = VE("gn", lambda e: e.tensor_copy(GS[:, 1:2], GS[:, 2:3]), [v])
            i = bank()
            p = PE("gn", lambda e, i=i: e.matmul(TR[:, i, 0:2], gmask[:, :, :].rearrange("p a b -> p (a b)"),
                                                 GS[:, 0:2], start=True, stop=True), [v, bank_free[i]])
            v = VE("gn", lambda e, i=i: e.tensor_copy(GS[:, 4:6], TR[:, i, 0:2]), [p])
            bank_free[i] = v
            v = VE("gn", lambda e: e.tensor_tensor(GS[:, 6:7], GS[:, 4:5], GS[:, 4:5], ALU.mult), [v])
            v = VE("gn", lambda e: e.tensor_tensor(GS[:, 7:8], GS[:, 5:6], GS[:, 6:7], ALU.subtract), [v])
            v = VE("gn", lambda e: e.tensor_scalar(GS[:, 7:8], GS[:, 7:8], 1e-5, None, ALU.add), [v])
            g = PO("gn", lambda e: e.tensor_tensor(GS[:, 8:9], GS[:, 7:8], mhalf[:, 0:1], ALU.pow), [v, k_po])
            v = VE("gn", lambda e: e.tensor_tensor(GS[:, 9:10], GS[:, 8:9], gam[:, 0:1], ALU.mult), [g])
            v = VE("gn", lambda e: e.tensor_tensor(GS[:, 10:11], GS[:, 9:10], GS[:, 4:5], ALU.mult), [v])
            v = VE("gn", lambda e: e.tensor_tensor(GS[:, 11:12], gam[:, 1:2], GS[:, 10:11], ALU.subtract), [v])
            yield 5
            gnv = v
            for kk in range(8):
                sl = slice(kk * 512, kk * 512 + 512)
                w = VE("t0a", lambda e, sl=sl: e.tensor_scalar(MO[:, sl], MO[:, sl], GS[:, 9:10], GS[:, 11:12],
                                                               ALU.mult, ALU.add), [gnv])
                a = AC("t0b", lambda e, sl=sl, kk=kk: e.activation(dA[1][:, 0, (kk % 2) * 512:(kk % 2) * 512 + 512],
                                                                  MO[:, sl], ACT.Tanh, scale=0.5),
                       [w, free["dA1"], free.get("t0c%d" % (kk % 2))])
                d = SP("t0x%d" % (kk % 2), lambda e, sl=sl, kk=kk: e.dma_start(
                    U[1][:, 0, (kk % 2) * 512:(kk % 2) * 512 + 512], xb[:, sl]),
                    [free["U1"], free.get("t0d%d" % (kk % 2))], 16)
                w = VE("t0c", lambda e, sl=sl, kk=kk: e.scalar_tensor_tensor(
                    out=MO[:, sl], in0=dA[1][:, 0, (kk % 2) * 512:(kk % 2) * 512 + 512], scalar=1.0, in1=MO[:, sl],
                    op0=ALU.add, op1=ALU.mult), [a, w])
                free["t0c%d" % (kk % 2)] = w
                w = VE("t0d", lambda e, sl=sl, kk=kk: e.scalar_tensor_tensor(
                    out=MO[:, sl], in0=MO[:, sl], scalar=0.5,
                    in1=U[1][:, 0, (kk % 2) * 512:(kk % 2) * 512 + 512], op0=ALU.mult, op1=ALU.add), [w, d])
                free["t0d%d" % (kk % 2)] = w
                t0v[kk] = w
                d = SP("t0s", lambda e, sl=sl: e.dma_start(t0d[b][:, sl], MO[:, sl]), [w], 16)
                t0s[kk] = d
                yield 3
            free["dA1"], free["U1"] = w, w
            free["MOd"] = d

        t0v, t0s = {}, {}

        def normed(src, waits, dst, dstw, out_to=None):
            i = bank()
            for j in range(4):
                p = PE("tr", lambda e, i=i, j=j: e.transpose(TR[:, i, 128 * j:128 * j + 128],
                                                            src[:, 128 * j:128 * j + 128], ident[:, :]),
                       waits + [bank_free[i]])
            for j in range(4):
                v = VE("ln1", lambda e, i=i, j=j: e.bn_stats(B4[:, j, :], TR[:, i, 128 * j:128 * j + 128]), [p])
            for j in range(4):
                v2 = VE("ln2", lambda e, j=j: e.bn_aggr(MV[:, j, :], B4[:, j, :]), [v, free.get("MV")])
            g = PO("ln", lambda e: e.tensor_scalar(RS[:, 0:4], MV[:, :, 1], 1e-5, None, ALU.add),
                   [v2, free.get("RS")])
            g = PO("ln", lambda e: e.tensor_tensor(RS[:, 4:8], RS[:, 0:4], mhalf[:, :], ALU.pow), [g, k_po])
            for j in range(4):
                v = VE("ln3", lambda e, i=i, j=j: e.tensor_scalar(
                    dst[:, j, :], TR[:, i, 128 * j:128 * j + 128], MV[:, j, 0:1], RS[:, 4 + j:5 + j],
                    ALU.subtract, ALU.mult), [g, v2] + dstw)
            free["MV"] = free["RS"] = v
            bank_free[i] = v
            i2 = bank()
            for j in range(4):
                p = PE("tr2", lambda e, i2=i2, j=j: e.transpose(TR[:, i2, 128 * j:128 * j + 128], dst[:, j, :],
                                                               ident[:, :]), [v, bank_free[i2]])
            w = VE("ln4", lambda e, i2=i2: e.tensor_copy(EPb, TR[:, i2, :]), [p, free.get("EPb")])
            bank_free[i2] = w
            return v, p, w

        def prologue(b, kk, fwait, xtwait):
            sl = slice(kk * 512, kk * 512 + 512)
            v, p, w = normed(MO[:, sl], [t0v[kk]], xnT[:, 4 * kk:4 * kk + 4, :], [xtwait])
            free["MO"] = p
            xnv[kk] = v
            i = bank()
            p = PE("f", lambda e, i=i: e.matmul(TR[:, i, :], W1f[:, :, :].rearrange("p a b -> p (a b)"), EPb,
                                                start=True, stop=True), [w, bank_free[i]])
            if kk < 4:
                v = VE("f", lambda e, i=i, sl=sl: e.tensor_scalar(Fq[:, sl], TR[:, i, :], b1r[:, 0:1], None, ALU.add),
                       [p, fwait])
                fv[kk] = v
            else:
                v = VE("f2", lambda e, i=i: e.tensor_scalar(EPc[0:NA, :], TR[0:NA, i, :], b1r[0:NA, 0:1], None,
                                                            ALU.add), [p, free.get("EPc")])
                d = SP("fs", lambda e, kk=kk: e.dma_start(fd[b][:, (kk - 4) * 512:(kk - 4) * 512 + 512],
                                                          EPc[0:NA, :]), [v], 16)
                free["EPc"] = d
                fs[kk] = d
            bank_free[i] = v
            i = bank()
            xr = EPb.rearrange("p (o r) -> p r o", r=8)
            for r in range(8):
                p = PE("g", lambda e, i=i, r=r: e.matmul(TR[:, i, 0:64], W1g[:, r, :], xr[:, r, :],
                                                         start=(r == 0), stop=(r == 7)), [bank_free[i]])
            free["EPb"] = p
            v = VE("g", lambda e, i=i, kk=kk: e.tensor_copy(Gk[:, kk * 64:kk * 64 + 64], TR[:, i, 0:64]),
                   [p, fwait])
            bank_free[i] = v
            gv[kk] = v

        xnv, fv, gv, fs = {}, {}, {}, {}

        def epilogue(b, I, accw, denp):
            i, p = denp
            v = VE("den", lambda e, i=i: e.tensor_scalar(RD, TR[:, i, 0:16], 1e-10, None, ALU.add),
                   [p, free.get("RD")])
            bank_free[i] = v
            vr = VE("den", lambda e: e.reciprocal(RD, RD), [v])
            for kk in range(4):
                sl = slice(kk * 512, kk * 512 + 512)
                gl = slice(I * SUP + kk * 512, I * SUP + kk * 512 + 512)
                i = bank()
                for j in range(4):
                    col = 4 * kk + j
                    p = PE("rb", lambda e, i=i, j=j, col=col: e.matmul(
                        TR[:, i, 128 * j:128 * j + 128], RD[:, col:col + 1].to_broadcast([128, 128]), ident[:, :],
                        start=True, stop=True), [vr, bank_free[i]])
                free["RD"] = p
                d = SP("t0l", lambda e, gl=gl: e.dma_start(EPa, t0d[b][:, gl]),
                       [t0sb[b][4 * I + kk], free.get("EPa")], 16)
                v = VE("t1", lambda e, i=i, sl=sl: e.tensor_tensor(acc[:, sl], acc[:, sl], TR[:, i, :], ALU.mult),
                       [p, accw])
                bank_free[i] = v
                v = VE("t1", lambda e, sl=sl: e.tensor_tensor(acc[:, sl], acc[:, sl], EPa, ALU.add), [v, d])
                free["EPa"] = v
                d = SP("t1s", lambda e, gl=gl, sl=sl: e.dma_start(t1d[b][:, gl], acc[:, sl]), [v], 16)
                yield 3
                x2 = EPd.rearrange("p (k c) -> p k c", c=C)
                v, p, w = normed(acc[:, sl], [v], x2, [free.get("EPd"), free.get("EPd2")])
                free["EPd2"] = p
                dx = SP("x2s", lambda e, kk=kk: e.dma_start(xtd[b][:, 16 * I + 4 * kk:16 * I + 4 * kk + 4, :], x2),
                        [v], 16)
                free["EPd"] = dx
                i = bank()
                p = PE("lg", lambda e, i=i: e.matmul(TR[0:NE, i, :], gw[:, :], EPb, start=True, stop=True),
                       [w, bank_free[i]])
                free["EPb"] = p
                v = VE("lg", lambda e, i=i: e.tensor_scalar(EPc[0:NE, :], TR[0:NE, i, :], gb[0:NE, 0:1], None,
                                                            ALU.add), [p, free.get("EPc")])
                bank_free[i] = v
                dl = SP("lgs", lambda e, gl=gl: e.dma_start(lgd[b][:, gl], EPc[0:NE, :]), [v], 16)
                free["EPc"] = dl
                stores.append((d, dx, dl))
                free["acc"] = [d, w]
                yield 5

        stores = []

        th_free = [None] * 6
        ex_free = [None] * 2
        st8 = {"th": 0, "s": None, "av": None, "esum": None, "acc": None, "avpend": []}

        def drain_side(kind):
            while side and side[0][0] == kind:
                step_side()

        side = []

        def step_side():
            try:
                return next(side[0][1])
            except StopIteration:
                side.pop(0)
                return 0

        def attention(b, I, fw):
            nblk = 16 * (I + 1)
            pend = []

            def av_pieces(j0, css, eready):
                for c in range(css[0] // 512, 4):
                    def go(c=c):
                        lo = max(512 * c, css[0])
                        for m in range(2):
                            l = max(512 * c, css[m])
                            if l >= 512 * c + 512:
                                continue
                            last = m == 1 or css[1] >= 512 * c + 512
                            p = PE("av", lambda e, c=c, l=l, m=m, last=last: e.matmul(
                                TR[:, 4, l - 512 * c:512], xnT[:, j0 + m, :], EX[m][:, l:512 * c + 512],
                                start=(m == 0), stop=last, skip_group_check=True),
                                [eready[m], xnv[(j0 + m) // 4], bank_free[4]])
                            if last:
                                ex_av[m] = p
                        if j0 == 0:
                            drain_side("epi")
                            v = VE("acc", lambda e, c=c: e.tensor_copy(acc[:, 512 * c:512 * c + 512], TR[:, 4, :]),
                                   [p] + (free.get("acc") or []))
                        else:
                            v = VE("acc", lambda e, c=c, lo=lo: e.tensor_tensor(
                                acc[:, lo:512 * c + 512], acc[:, lo:512 * c + 512], TR[:, 4, lo - 512 * c:512],
                                ALU.add), [p, st8["acc"]])
                        st8["acc"] = v
                        bank_free[4] = v
                        st8["av"] = p
                        ex_av[0] = p
                        ex_av[1] = p
                    yield go

            ex_av = [st8["av"], st8["av"]]
            eready = [None, None]
            css = [0, 0]
            for jb in range(nblk):
                cs = max(0, jb * 128 - I * SUP)
                diag = jb * 128 >= I * SUP
                m2 = jb % 2
                for m in range(4):
                    slots = []
                    cost = 0
                    for q in range(4):
                        o = 4 * q + m
                        sl = st8["th"] % 6
                        st8["th"] += 1
                        lo = cs + (32 * q if diag else 0)
                        a = AC("th", lambda e, sl=sl, lo=lo, g=jb * 16 + o: e.activation(
                            TH[sl][:, lo:SUP], Fq[:, lo:SUP], ACT.Tanh, bias=Gk[:, g:g + 1]),
                            [th_free[sl], gv[jb // 4]] + fw)
                        slots.append((sl, a, lo))
                        cost += (SUP - lo) * 0.000833 + 0.3
                    if m == 0 and st8.get("exp"):
                        st8.pop("exp")()
                    for c in range(cs // 512, 4):
                        for q in range(4):
                            sl, a, lo = slots[q]
                            l = max(512 * c, lo)
                            if l >= 512 * c + 512:
                                continue
                            p = PE("s", lambda e, c=c, q=q, l=l, sl=sl, m=m: e.matmul(
                                TR[32 * q:32 * q + 32, c, l - 512 * c:512], w2b[:, m, :], TH[sl][:, l:512 * c + 512],
                                start=(m == 0), stop=(m == 3), skip_group_check=True),
                                [a] + ([st8["s"]] if m == 0 else []) + ready)
                    for sl, _, _ in slots:
                        th_free[sl] = p
                    lastth = slots[-1][1]
                    if m == 3:
                        def fin(p=p, cs=cs, m2=m2, diag=diag, jb=jb):
                            a = AC("ex", lambda e: e.activation(
                                EX[m2][:, cs:SUP],
                                TR[:, 0:4, :].rearrange("p a b -> p (a b)")[:, cs:SUP], ACT.Exp, bias=b2r[:, 0:1]),
                                [p, ex_free[m2], ex_av[m2], st8.get("esr%d" % m2)])
                            st8["s"] = a
                            r = a
                            if diag:
                                r = PO("mask", lambda e: e.affine_select(
                                    out=EX[m2][:, cs:cs + 128], in_=EX[m2][:, cs:cs + 128], compare_op=ALU.is_gt,
                                    fill=0.0, base=0, pattern=[[1, 128]], channel_multiplier=-1), [a])
                            if jb == 0:
                                g = PO("es", lambda e: e.tensor_copy(esum, EX[m2]), [r, st8.get("den")])
                            else:
                                g = PO("es", lambda e: e.tensor_tensor(
                                    esum[:, cs:SUP], esum[:, cs:SUP], EX[m2][:, cs:SUP], ALU.add),
                                    [r, st8["esum"]])
                            st8["esum"] = g
                            st8["esr%d" % m2] = g
                            eready[m2] = r
                            css[m2] = cs
                            if m2 == 1:
                                pend.extend(av_pieces(jb - 1, tuple(css), tuple(eready)))
                        st8["exp"] = fin
                    if pend:
                        pend.pop(0)()
                    yield cost
            st8.pop("exp")()
            while pend:
                pend.pop(0)()
            i = bank()
            for kk in range(16):
                p = PE("den", lambda e, i=i, kk=kk: e.matmul(TR[:, i, kk:kk + 1], esum[:, 128 * kk:128 * kk + 128],
                                                             ones[:, 0:1], start=True, stop=True),
                       [st8["esum"], bank_free[i]])
            bank_free[i] = p
            st8["den"] = p
            side.insert(0, ["epi", epilogue(b, I, st8["acc"], (i, p))])
            next(side[0][1])
            st8["thlast"] = lastth

        t0sb = {}

        def run_all(g):
            for _ in g:
                pass

        run_all(mamba(0))
        fw_prev, xt_prev = None, None
        MCOST = 4 * (3.5 * 2 + 12 + 15 + NS * 8 + 10) + 5 + 24
        for b in range(NB):
            t0sb[b] = dict(t0s)
            for kk in range(4):
                prologue(b, kk, st8.get("thlast"), st8["av"])

            def rest(b=b, xt=st8["av"], tl=st8.get("thlast")):
                for kk in range(4, 8):
                    prologue(b, kk, tl, xt)
                    yield 1
                    yield 6
            fl = None
            pro = ["pro", rest()]
            side.append(pro)
            if b + 1 < NB:
                side.append(["mamba", mamba(b + 1)])
            spent = done = 0.0
            asum = 64 * 4.2 + 128 * 7.2
            rate = (MCOST + 80) / (0.9 * asum)
            for I in range(2):
                fw = [fv[kk] for kk in range(4)] if I == 0 else [fl]
                for cost in attention(b, I, fw):
                    spent += cost * rate
                    while side and done < spent:
                        done += step_side()
                if I == 0:
                    drain_side("epi")
                    drain_side("pro")
                    for r in range(8):
                        fl = SP("fl", lambda e, r=r, b=b: e.dma_start(Fq[16 * r:16 * r + 16, :], fd[b]),
                                [st8["thlast"]] + list(fs.values()), 16)
            while side and not (len(side) == 1 and side[0][0] == "epi"):
                if side[0][0] == "epi":
                    drain_side("epi")
                else:
                    step_side()
        drain_side("epi")

        top[0] = 0
        NP = max(1, NB // 2)
        W = min(2, NB) * NE
        MT = cut(NP * L).rearrange("p (a s) -> p a s", a=NP)
        LG = [cut(L) for _ in range(2)]
        X2 = [cut(L).rearrange("p (k c) -> p k c", c=C) for _ in range(2)]
        MS = [cut(512).rearrange("p (k c) -> p k c", c=128) for _ in range(4)]
        PT = cut(NE * NB).rearrange("p (e b) -> p e b", b=NB)
        OT = cut(NE * NB).rearrange("p (e b) -> p e b", b=NB)
        OE = cut(NP * 128).rearrange("p (a c) -> p a c", a=NP)
        T8 = cut(16)
        WA = [cut(EG * NH).rearrange("p (e n) -> p e n", e=EG) for _ in range(2)]
        WB = [cut(EG * NH).rearrange("p (e k n) -> p e k n", e=EG, k=4) for _ in range(2)]
        WAb = [cut(EG * NH) for _ in range(2)]
        WBb = [t_[32:33, 0:EG * C] for t_ in WAb]
        HH = [cut(EG * 4 * NB) for _ in range(2)]
        ends = [VE.items[-1][2], AC.items[-1][2], PE.items[-1][2], PO.items[-1][2]] + [x for s_ in stores for x in s_]
        ends += [free["MOd"]]
        wfree = {}

        def load_w(gi):
            s = gi % 2
            w = [wfree.get(s)] + ends
            e0 = gi * EG
            SP("wa%d" % s, lambda e: e.dma_start(WA[s], we1[e0:e0 + EG, 0:C, :].rearrange("e p n -> p e n")), w, 16)
            SP("wa%d" % s, lambda e: e.dma_start(WB[s], we2[e0:e0 + EG, 0:NH, :].rearrange("e (p k) n -> p e k n", k=4)),
               w, 16)
            SP("wa%d" % s, lambda e: e.dma_start(WAb[s][0:1, :].rearrange("p (e n) -> p e n", e=EG),
                                                 we1[e0:e0 + EG, C:C + 1, :].rearrange("e p n -> p e n")), w, 16)
            return SP("wa%d" % s, lambda e: e.dma_start(WBb[s].rearrange("p (e n) -> p e n", e=EG),
                                                        we2[e0:e0 + EG, NH:NH + 1, :].rearrange("e p n -> p e n")),
                      w, 16)

        ldw = {}
        lgf, x2f, msf = [None, None], [None, None], [None] * 4
        tb = [0]
        tfree = {i: None for i in range(8)}

        def tbank():
            i = tb[0] % 8
            tb[0] += 1
            return i

        mtv = {}
        xl = {}

        def load_x2(b):
            xl[b] = SP("x2l%d" % (b % 2), lambda e: e.dma_start(X2[b % 2], xtd[b]), ends + [x2f[b % 2]], 16)

        for a_ in range(NP):
            l_ = SP("lgl%d" % (a_ % 2), lambda e, a_=a_: e.dma_start(
                LG[a_ % 2][0:W, :], lgd[2 * a_:2 * a_ + W // NE].rearrange("b e s -> (b e) s")),
                ends + [lgf[a_ % 2]], 16)
            Lg, M_ = LG[a_ % 2][0:W, :], MT[0:W, a_, :]
            if a_ == 0:
                for b in range(min(2, NB)):
                    load_x2(b)
                ldw[0] = load_w(0)
                ldw[1] = load_w(1)
            v = VE("g1", lambda e, Lg=Lg: e.max(T8[0:W, 0:8], Lg), [l_])
            v = VE("g2", lambda e: e.tensor_scalar(T8[0:W, 9:10], T8[0:W, 0:1], -1.0, None, ALU.mult), [v])
            a = AC("g", lambda e, Lg=Lg, M_=M_: e.activation(M_, Lg, ACT.Exp, bias=T8[0:W, 9:10],
                                                             accum_out=T8[0:W, 10:11]), [v] + ends)
            v = VE("g3", lambda e: e.reciprocal(T8[0:W, 11:12], T8[0:W, 10:11]), [a])
            v = VE("g4", lambda e, M_=M_: e.tensor_scalar(M_, M_, T8[0:W, 11:12], None, ALU.mult), [v])
            v = VE("g5", lambda e, M_=M_: e.max(T8[0:W, 0:8], M_), [v])
            v = VE("g6", lambda e, M_=M_, Lg=Lg: e.match_replace(out=Lg, in_to_replace=T8[0:W, 0:8], in_values=M_,
                                                                 imm_value=0.0), [v])
            v = VE("g7", lambda e, M_=M_, Lg=Lg: e.tensor_tensor(M_, M_, Lg, ALU.subtract), [v])
            lgf[a_ % 2] = v
            mtv[a_] = v
            pooled = [tbank(), tbank()]
            for k4 in range(8):
                i = tbank()
                while i in pooled:
                    i = tbank()
                for j in range(4):
                    kk = 4 * k4 + j
                    p = PE("mt", lambda e, i=i, j=j, kk=kk, M_=M_: e.transpose(
                        TR[:, i, 128 * j:128 * j + W], M_[:, 128 * kk:128 * kk + 128], ident[0:W, 0:W]),
                        [v, tfree[i]])
                cp = AC if k4 % 2 else VE
                fn = (lambda e, i=i, k4=k4: e.activation(MS[k4 % 4][:, :, 0:W], TR[:, i, :].rearrange(
                    "p (k c) -> p k c", c=128)[:, :, 0:W], ACT.Copy)) if k4 % 2 else (
                    lambda e, i=i, k4=k4: e.tensor_copy(MS[k4 % 4][:, :, 0:W], TR[:, i, :].rearrange(
                        "p (k c) -> p k c", c=128)[:, :, 0:W]))
                w = cp("msc", fn, [p, msf[k4 % 4]])
                tfree[i] = w
                for bb in range(W // NE):
                    for j in range(4):
                        kk = 4 * k4 + j
                        p = PE("po", lambda e, bb=bb, j=j, kk=kk, k4=k4, i=pooled[bb]: e.matmul(
                            TR[:, i, 0:NE], X2[bb][:, kk, :], MS[k4 % 4][:, j, bb * NE:bb * NE + NE],
                            start=(kk == 0), stop=(kk == 31)), [w, xl[2 * a_ + bb], tfree[pooled[bb]]])
                msf[k4 % 4] = p
            for bb in range(W // NE):
                x2f[bb] = p
                b = 2 * a_ + bb
                v = VE("poc", lambda e, b=b, i=pooled[bb]: e.tensor_copy(PT[:, :, b], TR[:, i, 0:NE]), [p])
                tfree[pooled[bb]] = v
                if b + 2 < NB:
                    load_x2(b + 2)
        ptv = v

        hf = [None, None]
        for gi in range(NE // EG):
            s = gi % 2
            i1, i2 = tbank(), tbank()
            hv = TR[:, i1, 0:EG * 4 * NB].rearrange("p (e k b) -> p e k b", e=EG, k=4)
            for e_ in range(EG):
                for k_ in range(4):
                    PE("h", lambda e, e_=e_, k_=k_, s=s, hv=hv, gi=gi: e.matmul(
                        hv[:, e_, k_, :], WA[s][:, e_, k_:NH:4], PT[:, gi * EG + e_, :], start=True, stop=False),
                        [ldw[gi], ptv, tfree[i1]])
                    p = PE("h", lambda e, e_=e_, k_=k_, s=s, hv=hv: e.matmul(
                        hv[:, e_, k_, :], WAb[s][0:1, e_ * NH + k_:e_ * NH + NH:4], ones[0:1, 0:NB],
                        start=False, stop=True))
            a = AC("gelu", lambda e, i1=i1, s=s: e.activation(HH[s], TR[:, i1, 0:EG * 4 * NB], ACT.Gelu),
                   [p, hf[s]])
            tfree[i1] = a
            ov = TR[:, i2, 0:EG * NB].rearrange("p (e b) -> p e b", e=EG)
            hs = HH[s].rearrange("p (e k b) -> p e k b", e=EG, k=4)
            for e_ in range(EG):
                for k_ in range(4):
                    PE("o", lambda e, e_=e_, k_=k_, s=s, ov=ov, hs=hs: e.matmul(
                        ov[:, e_, :], WB[s][:, e_, k_, :], hs[:, e_, k_, :], start=(k_ == 0), stop=False),
                        [a, tfree[i2]])
                p = PE("o", lambda e, e_=e_, s=s, ov=ov: e.matmul(
                    ov[:, e_, :], WBb[s][:, e_ * C:e_ * C + C], ones[32:33, 0:NB], start=False, stop=True))
            hf[s] = p
            wfree[s] = p
            v = VE("ot", lambda e, gi=gi, ov=ov: e.tensor_copy(OT[:, gi * EG:gi * EG + EG, :], ov), [p])
            tfree[i2] = v
            if gi + 2 < NE // EG:
                ldw[gi + 2] = load_w(gi + 2)
        nb2 = W // NE
        oe = []
        for a_ in range(NP):
            i = tbank()
            for bb in range(nb2):
                v2 = VE("otp", lambda e, a_=a_, bb=bb: e.tensor_copy(
                    LG[0][:, (2 * a_ + bb) * NE:(2 * a_ + bb) * NE + NE], OT[:, :, 2 * a_ + bb]), [v])
            p = PE("oe", lambda e, i=i, a_=a_: e.transpose(
                TR[0:W, i, 0:128], LG[0][:, 2 * a_ * NE:2 * a_ * NE + W], ident[:, :]), [v2, tfree[i]])
            w = VE("oe", lambda e, i=i, a_=a_: e.tensor_copy(OE[0:W, a_, :], TR[0:W, i, 0:128]), [p])
            tfree[i] = w
            oe.append(w)
        TO = X2[0].rearrange("p k c -> p (k c)"), X2[1].rearrange("p k c -> p (k c)")
        tof = {}
        fin = []
        for b in range(NB):
            t_ = TO[b % 2]
            d = SP("tl%d" % (b % 2), lambda e, b=b, t_=t_: e.dma_start(t_, t1d[b]), [tof.get(b % 2), ptv], 16)
            lo = (b % 2) * NE
            for c in range(8):
                i = tbank()
                p = PE("fo", lambda e, i=i, c=c, lo=lo, b=b: e.matmul(
                    TR[:, i, :], OE[lo:lo + NE, b // 2, :], MT[lo:lo + NE, b // 2, 512 * c:512 * c + 512],
                    start=True, stop=True), oe + [tfree[i]])
                v = VE("fo", lambda e, i=i, c=c, t_=t_: e.tensor_tensor(
                    t_[:, 512 * c:512 * c + 512], t_[:, 512 * c:512 * c + 512], TR[:, i, :], ALU.add), [p, d])
                tfree[i] = v
            d = SP("out%d" % (b % 2), lambda e, b=b, t_=t_: e.dma_start(od[b], t_), [v], 16)
            tof[b % 2] = d
            fin.append(d)
        SP("end", lambda e: None, fin)
        SP.items[-1][2].wanted = False

        emit = flush([PE, VE, AC, PO, SP], lambda n: ctx.enter_context(nc.semaphore(n)))
        ctx.enter_context(nc.allow_non_contiguous_dma(reason="small constants, strided rows"))
        block = ctx.enter_context(nc.Block())

        @block.tensor
        def _(e):
            emit(PE, e)

        @block.vector
        def _(e):
            emit(VE, e)

        @block.scalar
        def _(e):
            emit(AC, e)

        @block.gpsimd
        def _(e):
            emit(PO, e)

        @block.sync
        def _(e):
            emit(SP, e)


_INS = ["x", "L0_conv_W_in", "L0_conv_conv_w", "L0_conv_conv_b", "L0_conv_W_x", "L0_conv_W_dt", "L0_conv_b_dt",
        "L0_conv_A_log", "L0_conv_D", "L0_conv_W_out", "L0_conv_gn_gamma", "L0_conv_gn_beta", "L1_attn_W1",
        "L1_attn_b1", "L1_attn_w2", "L1_attn_b2", "L1_ffn_gate_w", "L1_ffn_gate_b", "L1_ffn_weight1",
        "L1_ffn_weight2"]


def kernel(**inputs):
    import numpy as _np
    import concourse.bacc as _bacc
    from concourse import mybir as _mybir
    from concourse.bass_utils import run_bass_kernel_spmd as _run

    nc = _bacc.Bacc("TRN2", target_bir_lowering=False, num_devices=1)
    arrays, args = {}, []
    for name in _INS:
        a = _np.ascontiguousarray(inputs[name])
        arrays[f"in_{name}_dram"] = a
        args.append(nc.dram_tensor(f"in_{name}_dram", a.shape, _mybir.dt.from_np(a.dtype), kind="ExternalInput").ap())
    shape = inputs["x"].shape
    out = nc.dram_tensor("out_0_dram", shape, _mybir.dt.float32, kind="ExternalOutput").ap()
    hybrid_kernel(nc, shape[0], *args, out)
    r = _run(nc, [arrays], core_ids=[0])
    return r.results[0]["out_0_dram"]
```

```python
from contextlib import ExitStack

import concourse.bass as bass
from concourse import mybir

ALU = mybir.AluOpType
ACT = mybir.ActivationFunctionType
F32 = mybir.dt.float32
BF16 = mybir.dt.bfloat16

C = 128
L = 4096
DI = 256
NS = 16
T = 1024
SUP = 2048
NA = 16
NE = 64
NH = 512
EG = 4
NTH = 7
ARENA = 54400


class Done:

    def __init__(self, sem, step):
        self.sem, self.step, self.wanted, self.value = sem, step, False, None


class Queue:

    def __init__(self, name):
        self.name, self.items = name, []

    def __call__(self, sem, fn, waits=(), step=1):
        waits = [w for w in waits if w is not None]
        for w in waits:
            w.wanted = True
        d = Done(f"{self.name}_{sem}", step)
        d.wanted = step == 16
        self.items.append((waits, fn, d))
        return d


def flush(queues, new_sem):
    sems, owner, count = {}, {}, {}
    for q in queues:
        for _, _, d in q.items:
            if d.wanted:
                assert owner.setdefault(d.sem, q.name) == q.name
                count[d.sem] = count.get(d.sem, 0) + d.step
                d.value = count[d.sem]
                if d.sem not in sems:
                    sems[d.sem] = new_sem(d.sem)

    def emit(q, eng):
        seen = {}
        for waits, fn, d in q.items:
            need = {}
            for w in waits:
                need[w.sem] = max(need.get(w.sem, 0), w.value)
            for s, v in need.items():
                if seen.get(s, 0) < v:
                    eng.wait_ge(sems[s], v)
                    seen[s] = v
            ins = fn(eng)
            if d.wanted:
                ins.then_inc(sems[d.sem], d.step)
    return emit


def hybrid_kernel(nc, NB, x, W_in, conv_w, conv_b, W_x, W_dt, b_dt, A_log, D, W_out, gn_gamma, gn_beta,
                  W1, b1, w2, b2, gate_w, gate_b, we1, we2, out):
    ctx = ExitStack()
    with ctx:
        def sb(name, shape, dt=F32):
            return ctx.enter_context(nc.sbuf_tensor(name, shape, dt))

        PE, VE, AC, PO, SP = (Queue(n) for n in ("pe", "ve", "ac", "po", "sp"))
        TR = ctx.enter_context(nc.psum_tensor("banks", [128, 8, 512], F32))

        def dram(name, shape):
            return nc.dram_tensor(name, shape, F32, kind="Internal").ap()
        t0d = dram("t0_scratch", (NB, C, L))
        t1d = dram("t1_scratch", (NB, C, L))
        xtd = dram("xt_scratch", (NB, 128, L // 128, C))
        lgd = dram("lg_scratch", (NB, NE, L))
        xd = x.rearrange("b c h w -> b c (h w)")
        od = out.rearrange("b c h w -> b c (h w)")

        ident = sb("ident", [128, 128])
        ones = sb("ones", [128, 8])
        WinS = sb("WinS", [128, DI])
        Wc = sb("Wc", [128, 2, DI])
        Wx = sb("Wx", [128, 2, 104])
        Wdt = sb("Wdt", [128, DI])
        Wo = sb("Wo", [128, 2, C])
        sel = sb("sel", [128, 32], BF16)
        W1f = sb("W1f", [128, 8, NA])
        W1g = sb("W1g", [128, 8, NA])
        w2b = sb("w2b", [128, 4, 32])
        gw = sb("gw", [128, NE])
        gmask = sb("gmask", [128, 4, 32])
        rmask = sb("rmask", [128, 8])
        cb = sb("cb", [128, 2])
        cbh = sb("cbh", [128, 2])
        bdt = sb("bdt", [128, 2])
        Dv = sb("Dv", [128, 2])
        An = sb("An", [128, 2, NS])
        gam = sb("gam", [128, 2])
        b1r = sb("b1r", [128, 1])
        w2r = sb("w2r", [128, 1])
        b2r = sb("b2r", [128, 1])
        gb = sb("gb", [128, 1])
        mhalf = sb("mhalf", [128, 4])
        arena = sb("arena", [128, ARENA])
        top = [0]

        def cut(n):
            a = top[0]
            top[0] += n
            assert top[0] <= ARENA, top[0]
            return arena[:, a:a + n]

        U = [cut(2 * T).rearrange("p (h t) -> p h t", h=2) for _ in range(2)]
        dA = [cut(2 * T).rearrange("p (h t) -> p h t", h=2) for _ in range(2)]
        Y = cut(2 * T).rearrange("p (h t) -> p h t", h=2)
        XC = cut(2 * T).rearrange("p (h t) -> p h t", h=2)
        DT = cut(2 * T).rearrange("p (h t) -> p h t", h=2)
        BC = cut(T // 2).bitcast(BF16)
        XS = cut(516)
        MO = cut(L)
        attn0 = top[0]
        Fq = cut(L)
        xnT = cut(28 * C).rearrange("p (k c) -> p k c", c=C)
        X0 = [cut(4 * C).rearrange("p (k c) -> p k c", c=C) for _ in range(2)]
        th0_at = top[0]
        TH = [cut(SUP) for _ in range(NTH)]
        EX = [cut(SUP) for _ in range(2)]
        esum = cut(SUP)
        acc = cut(SUP)
        Gk = cut(L // 8)
        G0 = [cut(64) for _ in range(2)]
        F0 = cut(512)
        EPa = cut(512)
        EPb = cut(512)
        EPc = cut(512)
        EPd = cut(512)
        ST = cut(2 * NS).rearrange("p (h n) -> p h n", h=2)
        BN = cut(8 * 6).rearrange("p (k s) -> p k s", s=6)
        GS = cut(16)
        B4 = cut(4 * 6).rearrange("p (k s) -> p k s", s=6)
        MV = cut(8).rearrange("p (k s) -> p k s", s=2)
        RS = cut(8)
        RD = cut(16)

        S = {}

        def load(key, dst, src):
            S[key] = SP("const", lambda e, dst=dst, src=src: e.dma_start(dst, src), step=16)

        cwrow = TH[2][:, 0:2 * DI]
        wxl = TH[3][:, 0:2 * 40].rearrange("p (k n) -> p k n", k=2)
        w1l = TH[4][:, 0:2 * NA].rearrange("p (k n) -> p k n", k=2)
        al = TH[5][:, 0:2 * NS].rearrange("p (h n) -> p h n", h=2)
        wil = TH[1][:, 0:2 * DI]
        if True:
            load("win", wil, W_in)
            load("cw", cwrow, conv_w.rearrange("d k -> (d k)").partition_broadcast(128))
            load("cb", cb[:, :], conv_b.rearrange("(h p) -> p h", p=128))
            load("wx", wxl, W_x.rearrange("(k p) n -> p k n", p=128))
            load("wdt", Wdt[96:104, :], W_dt)
            load("bdt", bdt[:, :], b_dt.rearrange("(h p) -> p h", p=128))
            load("D", Dv[:, :], D.rearrange("(h p) -> p h", p=128))
            load("al", al, A_log.rearrange("(h p) n -> p h n", p=128))
            load("wo", Wo[:, :, :], W_out.rearrange("(k p) n -> p k n", p=128))
            load("gg", gam[:, 0:1], gn_gamma.rearrange("(p a) -> p a", a=1))
            load("gb", gam[:, 1:2], gn_beta.rearrange("(p a) -> p a", a=1))
            load("w1", w1l, W1.rearrange("(k p) n -> p k n", p=128))
            for r in range(8):
                load("b1", b1r[16 * r:16 * r + 16, :], b1.rearrange("(p a) -> p a", a=1))
                load("w2", w2r[16 * r:16 * r + 16, :], w2)
            load("b2", b2r[:, :], b2.partition_broadcast(128))
            load("gw", EPa[0:NE, 0:C], gate_w)
            load("gb2", gb[0:NE, :], gate_b.rearrange("(p a) -> p a", a=1))
            load("gb2", gb[NE:2 * NE, :], gate_b.rearrange("(p a) -> p a", a=1))
        cst = S["gb2"]

        k = PO("k", lambda e: e.memset(ident[:, :], 0.0))
        k = PO("k", lambda e: e.affine_select(out=ident[:, :], in_=ident[:, :], compare_op=ALU.not_equal, fill=1.0,
                                              base=0, pattern=[[-1, 128]], channel_multiplier=1), [k])
        k_id = k
        k = PO("k", lambda e: e.memset(sel[:, :], 0.0))
        for j in range(3):
            k = PO("k", lambda e, j=j: e.affine_select(out=sel[:, :], in_=sel[:, :], compare_op=ALU.not_equal,
                                                       fill=1.0, base=-32 * j, pattern=[[-1, 32]],
                                                       channel_multiplier=1), [k])
        for t_, v in ((gmask, 1.0 / 32), (rmask, 1.0), (ones, 1.0), (mhalf, -0.5)):
            k = PO("k", lambda e, t_=t_, v=v: e.memset(t_[:], v))
        k = PO("k", lambda e: e.affine_select(out=gmask[:, :, :], in_=gmask[:, :, :], compare_op=ALU.is_ge, fill=0.0,
                                              base=0, pattern=[[-32, 4], [0, 32]], channel_multiplier=1), [k])
        k = PO("k", lambda e: e.affine_select(out=gmask[:, :, :], in_=gmask[:, :, :], compare_op=ALU.is_ge, fill=0.0,
                                              base=31, pattern=[[32, 4], [0, 32]], channel_multiplier=-1), [k])
        k = PO("k", lambda e: e.affine_select(out=rmask[:, :], in_=rmask[:, :], compare_op=ALU.is_ge, fill=0.0,
                                              base=0, pattern=[[-16, 8]], channel_multiplier=1), [k])
        k = PO("k", lambda e: e.affine_select(out=rmask[:, :], in_=rmask[:, :], compare_op=ALU.is_ge, fill=0.0,
                                              base=15, pattern=[[16, 8]], channel_multiplier=-1), [k])
        k_po = k
        v = VE("k", lambda e: e.tensor_copy(WinS[:, :], wil[:, DI:2 * DI]), [cst])
        cw2 = cwrow.rearrange("p (d k) -> p k d", k=2)
        wil_d = DI
        for j in range(2):
            v = VE("k", lambda e, j=j: e.tensor_tensor(Wc[:, j, :], wil[:, 0:wil_d], cw2[:, j, :], ALU.mult))
        for g in range(3):
            v = VE("k", lambda e, g=g: e.tensor_copy(Wx[:, :, 32 * g:32 * g + 32], wxl[:, :, 8:40]))
        v = VE("k", lambda e: e.tensor_copy(Wx[:, :, 96:104], wxl[:, :, 0:8]))
        v = VE("k", lambda e: e.tensor_scalar(cbh[:, :], cb[:, :], 0.5, None, ALU.mult))
        v = VE("k", lambda e: e.tensor_copy(W1f[:, :, :], w1l[:, 0:1, :].to_broadcast([128, 8, NA])))
        v2 = VE("k", lambda e: e.memset(w2b[:, :, :], 0.0))
        v = VE("k", lambda e: e.tensor_copy(W1g[:, :, :], w1l[:, 1:2, :].to_broadcast([128, 8, NA])))
        for m in range(4):
            v = VE("k", lambda e, m=m: e.tensor_scalar(w2b[:, m, 8 * m:8 * m + 8], rmask[:, :], w2r[:, 0:1], None,
                                                       ALU.mult), [v2, k_po])
        for j in range(4):
            v = VE("k", lambda e, j=j: e.memset(TR[:, 2 * j:2 * j + 2, :], 0.0))
        a = AC("k", lambda e: e.activation(al, al, ACT.Exp), [cst])
        v = VE("k", lambda e: e.tensor_scalar(An[:, :, :], al, -1.0, None, ALU.mult), [a])
        p = PE("k", lambda e: e.transpose(TR[:, 7, 0:NE], EPa[0:NE, 0:C], ident[0:NE, 0:NE]), [cst, k_id, v])
        v = VE("k", lambda e: e.tensor_copy(gw[:, :], TR[:, 7, 0:NE]), [p])
        ready = [v, k_po, cst]

        v0 = v
        bank_free = {i: v for i in range(4, 8)}
        turn = [0]

        def bank():
            i = 5 + turn[0] % 3
            turn[0] += 1
            f = bank_free[i]
            assert f != "open"
            bank_free[i] = "open"
            return i, f

        free = {}
        t0s, t0v = {}, {}
        xnv, fv, gv = {}, {}, {}
        stored = {b: [] for b in range(NB)}

        def mamba(b):
            xb = xd[b]

            def load_x(g0, taps):
                w = [free.get("XS")]
                if g0 == 0 and taps:
                    z = VE("xs0", lambda e: e.memset(XS[:, 0:1], 0.0), w)
                    d = SP("xs", lambda e: e.dma_start(XS[:, 1:513], xb[:, 0:512]), w, 16)
                    return [z, d]
                lo = 1 if not taps else 0
                return [SP("xs", lambda e: e.dma_start(XS[:, lo:513], xb[:, g0 - 1 + lo:g0 + 512]), w, 16)]

            uf = [free.get("U0"), free.get("U1")]
            df = [free.get("dA0"), free.get("dA1")]
            alone = b == 0
            UR = U + [TH[0].rearrange("p (h t) -> p h t", h=2), TH[1].rearrange("p (h t) -> p h t", h=2)] \
                if alone else U
            DR = dA + [TH[6].rearrange("p (h t) -> p h t", h=2)] if alone else dA
            CB = [EX[0][:, 0:T], EX[0][:, T:2 * T]]
            NU, ND = len(UR), len(DR)
            ux, dx_, cf = [cst, cst], [cst], [None, None]
            yfree = v0
            for c in range(L // T):
                for s in range(2):
                    ts = slice(s * 512, s * 512 + 512)
                    ld = load_x(c * T + s * 512, True)
                    yield 3, True
                    bk = []
                    for h in range(2):
                        i, bf = bank()
                        for kk in range(2):
                            p = PE("xh", lambda e, i=i, kk=kk, h=h: e.matmul(
                                TR[:, i, :], Wc[:, kk, h * 128:h * 128 + 128], XS[:, kk:kk + 512],
                                start=(kk == 0), stop=(kk == 1)), ld + ready + [bf])
                        bk.append((i, p))
                        yield 2, False
                    free["XS"] = p
                    th = []
                    for h, (i, p) in enumerate(bk):
                        th.append(AC("xth", lambda e, i=i, h=h, ts=ts: e.activation(
                            dA[1][:, h, ts], TR[:, i, :], ACT.Tanh, bias=cbh[:, h:h + 1], scale=0.5), [p, df[1]]))
                    yield 2, False
                    for h, (i, p) in enumerate(bk):
                        v1 = VE("xb", lambda e, i=i, h=h, ts=ts: e.tensor_scalar(
                            U[1][:, h, ts], TR[:, i, :], cb[:, h:h + 1], 0.5, ALU.add, ALU.mult), [th[h], uf[1]])
                        bank_free[i] = v1
                        vx = VE("xc", lambda e, h=h, ts=ts: e.scalar_tensor_tensor(
                            out=XC[:, h, ts], in0=dA[1][:, h, ts], scalar=1.0, in1=U[1][:, h, ts],
                            op0=ALU.add, op1=ALU.mult), [v1, free.get("XC")])
                for h in range(2):
                    vy = VE("y0", lambda e, h=h: e.tensor_scalar(Y[:, h, :], XC[:, h, :], Dv[:, h:h + 1], None,
                                                                 ALU.mult), [vx, free.get("Y")])
                yield 3, True
                for s in range(2):
                    ts = slice(s * 512, s * 512 + 512)
                    i, bf = bank()
                    for h in range(2):
                        p = PE("xdbl", lambda e, i=i, h=h, ts=ts: e.matmul(
                            TR[0:104, i, :], Wx[:, h, :], XC[:, h, ts], start=(h == 0), stop=(h == 1)), [vx, bf])
                    yield 3, False
                    R = U[1][:, 0, ts]
                    DL = U[1][:, 1, ts]
                    mid = dA[1][:, 0, s * 256:s * 256 + 256].bitcast(BF16)
                    bcs = BC[:, ts]
                    q0 = VE("dl", lambda e, i=i, DL=DL: e.tensor_copy(DL[96:104, :], TR[96:104, i, :]), [p, vx])
                    q1 = VE("s1", lambda e, i=i, bcs=bcs: e.tensor_copy(bcs[0:96, :], TR[0:96, i, :]),
                            [p, free.get("BC")])
                    q2 = VE("s2", lambda e, i=i, bcs=bcs, R=R: e.tensor_tensor(
                        R[0:96, :], TR[0:96, i, :], bcs[0:96, :], ALU.subtract), [q1])
                    bank_free[i] = q2
                    bk = []
                    for h in range(2):
                        i, bf = bank()
                        p = PE("dt", lambda e, i=i, h=h, DL=DL: e.matmul(
                            TR[:, i, :], Wdt[96:104, h * 128:h * 128 + 128], DL[96:104, :], start=True, stop=True),
                            [q0, bf])
                        bk.append((i, p))
                    q3 = VE("s3", lambda e, mid=mid, R=R: e.tensor_copy(mid[0:96, :], R[0:96, :]), [q2])
                    q4 = VE("s4", lambda e, mid=mid, R=R: e.tensor_tensor(
                        R[0:96, :], R[0:96, :], mid[0:96, :], ALU.subtract), [q3])
                    q5 = VE("s5", lambda e, mid=mid, bcs=bcs: e.tensor_copy(bcs[32:64, :], mid[32:64, :]), [q3])
                    vbc = VE("s6", lambda e, R=R, bcs=bcs: e.tensor_copy(bcs[64:96, :], R[64:96, :]), [q4])
                    yield 3, False
                    for h, (i, p) in enumerate(bk):
                        vd = VE("dtv", lambda e, i=i, h=h, ts=ts: e.tensor_scalar(
                            U[0][:, h, ts], TR[:, i, :], bdt[:, h:h + 1], None, ALU.add), [p, uf[0]])
                        bank_free[i] = vd
                    yield 1, True
                vd = VE("dtm", lambda e: e.tensor_scalar(DT, U[0], 0.0, None, ALU.max), [vd, free.get("DT")])
                vn = VE("dtn", lambda e: e.scalar_tensor_tensor(out=U[0], in0=DT, scalar=-2.0, in1=U[0],
                                                                op0=ALU.mult, op1=ALU.add), [vd])
                yield 2.5, True
                a1 = AC("sp1", lambda e: e.activation(dA[0], U[0], ACT.Exp), [vn, df[0]])
                a2 = AC("sp2", lambda e: e.activation(U[0], dA[0], ACT.Ln, bias=1.0), [a1])
                yield 3, True
                g1 = VE("sp3", lambda e: e.tensor_scalar(dA[1], dA[0], 1.0, -1.0, ALU.add, ALU.add), [a1, q5])
                g3 = PO("sp4", lambda e: e.tensor_tensor(dA[1], dA[0], dA[1], ALU.subtract), [g1])
                v3 = VE("sp5", lambda e: e.tensor_tensor(DT, DT, U[0], ALU.add), [a2, vd])
                yield 3, True
                v3 = VE("sp6", lambda e: e.tensor_tensor(DT, DT, dA[1], ALU.add), [v3, g3])
                v4 = VE("dtx", lambda e: e.tensor_tensor(XC, XC, DT, ALU.mult), [v3, vy])
                yield 4, True
                uf, df = [v3, vbc] + ux, [g3, v3] + (dx_ if alone else [])
                uf, df = uf[:NU], df[:ND]
                g = vy
                ysum = []

                def spread(col, s):
                    i, bf = bank()
                    p = PE("bc", lambda e: e.matmul(
                        TR[:, i, :], sel[0:96, col:col + 1].to_broadcast([96, 128]),
                        BC[0:96, s * 512:s * 512 + 512], start=True, stop=True), [vbc, bf])
                    return i, p

                for n in range(NS):
                    Un, En = UR[n % NU], DR[n % ND]
                    bk = [spread(n, s) for s in range(2)]
                    da = [AC("da", lambda e, h=h, n=n, En=En: e.activation(
                        En[:, h, :], DT[:, h, :], ACT.Exp, scale=An[:, h, n:n + 1]), [v3, df[n % ND]])
                        for h in range(2)]
                    for s, (i, p) in enumerate(bk):
                        w = VE("mb", lambda e, i=i, s=s, Un=Un: e.tensor_tensor(
                            Un[:, :, s * 512:s * 512 + 512], XC[:, :, s * 512:s * 512 + 512],
                            TR[:, i:i + 1, :].to_broadcast([128, 2, 512]), ALU.mult), [p, v4, uf[n % NU]])
                        bank_free[i] = w
                    yield 2.5, True
                    for h in range(2):
                        ini = 0.0 if c == 0 else ST[:, h, n:n + 1]
                        sc = VE("scan", lambda e, h=h, En=En, Un=Un, ini=ini: e.tensor_tensor_scan(
                            Un[:, h, :], En[:, h, :], Un[:, h, :], ini, ALU.mult, ALU.add),
                            [da[h], w, free.get("ST")])
                    df[n % ND] = sc
                    st = VE("st", lambda e, n=n, Un=Un: e.tensor_copy(ST[:, :, n:n + 1], Un[:, :, T - 1:T]), [sc])
                    free["ST"] = st
                    yield 2, True
                    bk = [spread(NS + n, s) for s in range(2)]
                    if alone:
                        for s, (i, p) in enumerate(bk):
                            w = AC("cb", lambda e, i=i, s=s, n=n: e.activation(
                                CB[n % 2][:, s * 512:s * 512 + 512], TR[:, i, :], ACT.Copy), [p, cf[n % 2]])
                            bank_free[i] = w
                        w = PO("mc", lambda e, n=n, Un=Un: e.tensor_tensor(
                            Un, Un, CB[n % 2].unsqueeze(1).to_broadcast([128, 2, T]), ALU.mult), [w, st])
                        cf[n % 2] = w
                        ysum.append((n, Un, w))
                        while len(ysum) > (2 if n < NS - 1 else 0):
                            n0, U0_, w = ysum.pop(0)
                            for q in range(4):
                                g = PE("y", lambda e, q=q, n0=n0, U0_=U0_: e.matmul(
                                    TR[:, q, :], ident[:, :], U0_[:, q // 2, 512 * (q % 2):512 * (q % 2) + 512],
                                    start=(n0 == 0), stop=(n0 == NS - 1)), [w, yfree])
                            uf[n0 % NU] = g
                        yield 3.5, True
                        continue
                    for s, (i, p) in enumerate(bk):
                        w = VE("mc", lambda e, i=i, s=s, Un=Un: e.tensor_tensor(
                            Un[:, :, s * 512:s * 512 + 512], Un[:, :, s * 512:s * 512 + 512],
                            TR[:, i:i + 1, :].to_broadcast([128, 2, 512]), ALU.mult), [p, st])
                        bank_free[i] = w
                    g = PO("y", lambda e, Un=Un: e.tensor_tensor(Y, Y, Un, ALU.add), [w, vy, g])
                    uf[n % NU] = g
                    yield 3.5, True
                if alone:
                    ux, dx_ = uf[2:], [df[2]]
                    for q in range(4):
                        g = VE("yp", lambda e, q=q: e.tensor_tensor(
                            Y[:, q // 2, 512 * (q % 2):512 * (q % 2) + 512],
                            Y[:, q // 2, 512 * (q % 2):512 * (q % 2) + 512], TR[:, q, :], ALU.add), [g, vy])
                    yfree = g
                free["BC"], free["XC"], free["DT"] = p, w, da[1]
                for s in range(2):
                    ts = slice(s * 512, s * 512 + 512)
                    g0 = c * T + s * 512
                    ld = load_x(g0, False)
                    yield 3, True
                    bk = []
                    for h in range(2):
                        i, bf = bank()
                        p = PE("z", lambda e, i=i, h=h: e.matmul(
                            TR[:, i, :], WinS[:, h * 128:h * 128 + 128], XS[:, 1:513], start=True, stop=True),
                            ld + [bf])
                        bk.append((i, p))
                    free["XS"] = p
                    yield 3, False
                    th = [AC("zth", lambda e, i=i, h=h, ts=ts: e.activation(
                        dA[0][:, h, ts], TR[:, i, :], ACT.Tanh, scale=0.5), [p, df[0], df[1]])
                        for h, (i, p) in enumerate(bk)]
                    yield 2, False
                    for h, (i, p) in enumerate(bk):
                        w = VE("zz", lambda e, i=i, h=h, ts=ts: e.scalar_tensor_tensor(
                            out=U[0][:, h, ts], in0=dA[0][:, h, ts], scalar=1.0, in1=TR[:, i, :],
                            op0=ALU.add, op1=ALU.mult), [th[h], uf[0]])
                        bank_free[i] = w
                    yz = VE("yz", lambda e, ts=ts: e.scalar_tensor_tensor(
                        out=U[0][:, :, ts], in0=Y[:, :, ts], scalar=0.5, in1=U[0][:, :, ts],
                        op0=ALU.mult, op1=ALU.mult), [w, g])
                    yield 3, True
                    i, bf = bank()
                    for h in range(2):
                        p = PE("mo", lambda e, i=i, h=h, ts=ts: e.matmul(
                            TR[:, i, :], Wo[:, h, :], U[0][:, h, ts], start=(h == 0), stop=(h == 1)), [yz, bf])
                    yield 3, False
                    w = VE("moc", lambda e, i=i, g0=g0: e.tensor_copy(MO[:, g0:g0 + 512], TR[:, i, :]),
                           [p, free.get("MO")])
                    vb = VE("mobn", lambda e, i=i, kk=2 * c + s: e.bn_stats(BN[:, kk, :], TR[:, i, :]), [p])
                    bank_free[i] = vb
                free["Y"] = yz
                uf, df = [p, uf[1]], [w, df[1]]
            v = VE("gn", lambda e: e.bn_aggr(GS[:, 0:2], BN.rearrange("p k s -> p (k s)")), [vb])
            v = VE("gn", lambda e: e.tensor_scalar(GS[:, 2:3], GS[:, 0:1], GS[:, 0:1], GS[:, 1:2], ALU.mult, ALU.add),
                   [v])
            v = VE("gn", lambda e: e.tensor_copy(GS[:, 1:2], GS[:, 2:3]), [v])
            yield 2, True
            i, bf = bank()
            p = PE("gn", lambda e, i=i: e.matmul(TR[:, i, 0:2], gmask[:, :, :].rearrange("p a b -> p (a b)"),
                                                 GS[:, 0:2], start=True, stop=True), [v, bf])
            v = VE("gn", lambda e, i=i: e.tensor_copy(GS[:, 4:6], TR[:, i, 0:2]), [p])
            bank_free[i] = v
            v = VE("gn", lambda e: e.tensor_tensor(GS[:, 6:7], GS[:, 4:5], GS[:, 4:5], ALU.mult), [v])
            v = VE("gn", lambda e: e.tensor_tensor(GS[:, 7:8], GS[:, 5:6], GS[:, 6:7], ALU.subtract), [v])
            v = VE("gn", lambda e: e.tensor_scalar(GS[:, 7:8], GS[:, 7:8], 1e-5, None, ALU.add), [v])
            g = PO("gn", lambda e: e.tensor_tensor(GS[:, 8:9], GS[:, 7:8], mhalf[:, 0:1], ALU.pow), [v, k_po])
            v = VE("gn", lambda e: e.tensor_tensor(GS[:, 9:10], GS[:, 8:9], gam[:, 0:1], ALU.mult), [g])
            v = VE("gn", lambda e: e.tensor_tensor(GS[:, 10:11], GS[:, 9:10], GS[:, 4:5], ALU.mult), [v])
            gnv = VE("gn", lambda e: e.tensor_tensor(GS[:, 11:12], gam[:, 1:2], GS[:, 10:11], ALU.subtract), [v])
            order = [4, 5, 6, 7, 0, 1, 2, 3]
            stage = {}

            def t0_in(n):
                kk, s = order[n], n % 2
                sl = slice(kk * 512, kk * 512 + 512)
                d = SP("t0x%d" % s, lambda e: e.dma_start(U[1][:, 0, s * 512:s * 512 + 512], xb[:, sl]),
                       [uf[1], t0_use[s]], 16)
                w = VE("t0a", lambda e: e.tensor_scalar(MO[:, sl], MO[:, sl], GS[:, 9:10], GS[:, 11:12],
                                                        ALU.mult, ALU.add), [gnv])
                stage[n] = (d, w)

            t0_use = [None, None]
            t0_in(0)
            yield 4, True
            for n, kk in enumerate(order):
                s = n % 2
                sl = slice(kk * 512, kk * 512 + 512)
                d, w = stage[n]
                a = AC("t0b", lambda e, s=s, sl=sl: e.activation(dA[1][:, 0, s * 512:s * 512 + 512], MO[:, sl],
                                                                 ACT.Tanh, scale=0.5), [w, df[1], t0_use[s]])
                if n < 7:
                    t0_in(n + 1)
                yield 1.5, True
                w = VE("t0c", lambda e, s=s, sl=sl: e.scalar_tensor_tensor(
                    out=MO[:, sl], in0=dA[1][:, 0, s * 512:s * 512 + 512], scalar=1.0, in1=MO[:, sl],
                    op0=ALU.add, op1=ALU.mult), [a, w])
                w = VE("t0d", lambda e, s=s, sl=sl: e.scalar_tensor_tensor(
                    out=MO[:, sl], in0=MO[:, sl], scalar=0.5, in1=U[1][:, 0, s * 512:s * 512 + 512],
                    op0=ALU.mult, op1=ALU.add), [w, d])
                t0_use[s] = w
                t0v[kk] = w
                t0s[b] = SP("t0s", lambda e, sl=sl: e.dma_start(t0d[b][:, sl], MO[:, sl]), [w, t0s.get(b - 1)], 16)
                yield 1.5, True
            free["U0"], free["U1"], free["dA0"], free["dA1"] = p_last(PE), w, w, w

        def p_last(q):
            return q.items[-1][2]

        def normed(src, waits, dst, dstw):
            i, bf = bank()
            for j in range(4):
                p = PE("tr", lambda e, j=j: e.transpose(TR[:, i, 128 * j:128 * j + 128],
                                                        src[:, 128 * j:128 * j + 128], ident[:, :]), waits + [bf])
            yield 3, False
            for j in range(4):
                v = VE("ln1", lambda e, j=j: e.bn_stats(B4[:, j, :], TR[:, i, 128 * j:128 * j + 128]), [p])
            for j in range(4):
                v2 = VE("ln2", lambda e, j=j: e.bn_aggr(MV[:, j, :], B4[:, j, :]), [v, free.get("MV")])
            g = PO("ln", lambda e: e.tensor_scalar(RS[:, 0:4], MV[:, :, 1], 1e-5, None, ALU.add),
                   [v2, free.get("RS")])
            g = PO("ln", lambda e: e.tensor_tensor(RS[:, 4:8], RS[:, 0:4], mhalf[:, :], ALU.pow), [g, k_po])
            yield 4, False
            for j in range(4):
                v = VE("ln3", lambda e, j=j: e.tensor_scalar(
                    dst[:, j, :], TR[:, i, 128 * j:128 * j + 128], MV[:, j, 0:1], RS[:, 4 + j:5 + j],
                    ALU.subtract, ALU.mult), [g, v2] + dstw)
            free["MV"] = free["RS"] = v
            bank_free[i] = v
            yield 2, True
            i2, bf = bank()
            for j in range(4):
                p = PE("tr2", lambda e, j=j: e.transpose(TR[:, i2, 128 * j:128 * j + 128], dst[:, j, :],
                                                         ident[:, :]), [v, bf])
            yield 2, False
            w = VE("ln4", lambda e: e.tensor_copy(EPb, TR[:, i2, :]), [p, free.get("EPb")])
            bank_free[i2] = w
            yield 1.5, True
            return v, p, w

        def prologue(b, kks, thw, avw):
            for kk in kks:
                sl = slice(kk * 512, kk * 512 + 512)
                if kk == 0:
                    dst, Fd, Gd = X0[b % 2], F0, G0[b % 2]
                else:
                    dst, Fd, Gd = xnT[:, 4 * kk - 4:4 * kk, :], Fq[:, sl], Gk[:, kk * 64:kk * 64 + 64]
                v, p, w = yield from normed(MO[:, sl], [t0v[kk]], dst, [avw])
                free["MO"] = p
                xnv[b, kk] = v
                i, bf = bank()
                p = PE("g", lambda e, i=i: e.matmul(TR[:, i, :], W1g[:, :, :].rearrange("p a b -> p (a b)"), EPb,
                                                    start=True, stop=True), [w, bf])
                i2, bf = bank()
                p2 = PE("f", lambda e, i=i2: e.matmul(TR[:, i, :], W1f[:, :, :].rearrange("p a b -> p (a b)"), EPb,
                                                      start=True, stop=True), [w, bf])
                free["EPb"] = p2
                yield 2.5, False
                v = VE("g1", lambda e, i=i: e.tensor_tensor(
                    EPc.rearrange("p (o r) -> p o r", r=8), TR[:, i, :].rearrange("p (o r) -> p o r", r=8),
                    rmask[:, :].unsqueeze(1).to_broadcast([128, 64, 8]), ALU.mult), [p, free.get("EPc")])
                bank_free[i] = v
                gv[b, kk] = VE("g2", lambda e, Gd=Gd: e.tensor_reduce(
                    Gd, EPc.rearrange("p (o r) -> p o r", r=8), mybir.AxisListType.X, ALU.add), [v, thw])
                free["EPc"] = gv[b, kk]
                v = VE("f", lambda e, i=i2, Fd=Fd: e.tensor_scalar(Fd, TR[:, i, :], b1r[:, 0:1], None, ALU.add),
                       [p2, thw, free.get("F0")])
                fv[b, kk] = v
                bank_free[i2] = v
                yield 2, True

        def epilogue(b, I, accw, esumw, state):
            i, bf = bank()
            for kk in range(16):
                p = PE("den", lambda e, i=i, kk=kk: e.matmul(TR[:, i, kk:kk + 1], esum[:, 128 * kk:128 * kk + 128],
                                                             ones[:, 0:1], start=True, stop=True), [esumw, bf])
            st8["den"] = p
            state.append("begun")
            yield 3, False
            v = VE("den", lambda e, i=i: e.tensor_scalar(RD, TR[:, i, 0:16], 1e-10, None, ALU.add),
                   [p, free.get("RD")])
            bank_free[i] = v
            vr = VE("den", lambda e: e.reciprocal(RD, RD), [v])
            yield 1, True
            last = None

            def logits(kk, w):
                gl = slice(I * SUP + kk * 512, I * SUP + kk * 512 + 512)
                i, bf = bank()
                p = PE("lg", lambda e: e.matmul(TR[0:NE, i, :], gw[:, :], EPb, start=True, stop=True), [w, bf])
                free["EPb"] = p

                def out_():
                    v = VE("lg", lambda e: e.tensor_scalar(EPc[0:NE, :], TR[0:NE, i, :], gb[0:NE, 0:1], None,
                                                           ALU.add), [p, free.get("EPc")])
                    bank_free[i] = v
                    dl = SP("lgs", lambda e: e.dma_start(lgd[b][:, gl], EPc[0:NE, :]), [v], 16)
                    free["EPc"] = dl
                    stored[b].append(dl)
                return out_

            for kk in range(4):
                sl = slice(kk * 512, kk * 512 + 512)
                gl = slice(I * SUP + kk * 512, I * SUP + kk * 512 + 512)
                i, bf = bank()
                for j in range(4):
                    p = PE("rb", lambda e, i=i, j=j, col=4 * kk + j: e.matmul(
                        TR[:, i, 128 * j:128 * j + 128], RD[:, col:col + 1].to_broadcast([128, 128]), ident[:, :],
                        start=True, stop=True), [vr, bf])
                free["RD"] = p
                lo_ = logits(kk - 1, last) if last is not None else None
                d = SP("t0l", lambda e, gl=gl: e.dma_start(EPa, t0d[b][:, gl]), [t0s[b], free.get("EPa")], 16)
                yield 2.5, False
                v = VE("t1", lambda e, i=i, sl=sl: e.tensor_tensor(acc[:, sl], acc[:, sl], TR[:, i, :], ALU.mult),
                       [p, accw])
                bank_free[i] = v
                v = VE("t1", lambda e, sl=sl: e.tensor_tensor(acc[:, sl], acc[:, sl], EPa, ALU.add), [v, d])
                free["EPa"] = v
                d = SP("t1s", lambda e, gl=gl, sl=sl: e.dma_start(t1d[b][:, gl], acc[:, sl]), [v], 16)
                stored[b].append(d)
                if lo_:
                    lo_()
                yield 1.5, True
                x2 = EPd.rearrange("p (k c) -> p k c", c=C)
                v, p, last = yield from normed(acc[:, sl], [v], x2, [free.get("EPd"), free.get("EPd2")])
                free["EPd2"] = p
                dx = SP("x2s", lambda e, kk=kk: e.dma_start(xtd[b][:, 16 * I + 4 * kk:16 * I + 4 * kk + 4, :], x2),
                        [v], 16)
                free["EPd"] = dx
                stored[b].append(dx)
                free["acc"] = [d, last]
            lo_ = logits(3, last)
            yield 2, False
            lo_()

        class Gate:
            pass

        gt = Gate()

        def gate(a_, MTa, LG, X2, MS, PT, T8, extra):
            nb2 = min(2, NB)
            W = nb2 * NE
            deps = extra + [x for bb in range(nb2) for x in stored[2 * a_ + bb]]
            Lg, M_ = LG[0:W, :], MTa[0:W, :]
            l_ = SP("lgl", lambda e: e.dma_start(Lg, lgd[2 * a_:2 * a_ + nb2].rearrange("b e s -> (b e) s")),
                    deps + [free.get("LG")], 16)
            yield 8, True
            v = VE("g3", lambda e: e.max(T8[0:W, 0:8], Lg), [l_, free.get("T8")])
            v = VE("g4", lambda e: e.tensor_scalar(T8[0:W, 9:10], T8[0:W, 0:1], -1.0, None, ALU.mult), [v])
            yield 5, True
            a = AC("g", lambda e: e.activation(M_, Lg, ACT.Exp, bias=T8[0:W, 9:10], accum_out=T8[0:W, 10:11]),
                   [v] + extra)
            yield 4, True
            v = VE("g5", lambda e: e.reciprocal(T8[0:W, 11:12], T8[0:W, 10:11]), [a])
            v = VE("g6", lambda e: e.tensor_scalar(M_, M_, T8[0:W, 11:12], None, ALU.mult), [v])
            v = VE("g7", lambda e: e.max(T8[0:W, 0:8], M_), [v])
            yield 6, True
            v = VE("g8", lambda e: e.match_replace(out=Lg, in_to_replace=T8[0:W, 0:8], in_values=M_,
                                                   imm_value=0.0), [v])
            yield 4, True
            v = VE("g9", lambda e: e.tensor_tensor(M_, M_, Lg, ALU.subtract), [v])
            free["LG"] = free["T8"] = v
            gt.m = v
            yield 5, True
            for k4 in range(8):
                xl = []
                for bb in range(nb2):
                    xl.append(SP("x2l%d" % bb, lambda e, bb=bb, k4=k4: e.dma_start(
                        X2[bb], xtd[2 * a_ + bb][:, 4 * k4:4 * k4 + 4, :]), deps + [free.get("X2%d" % bb)], 16))
                i, bf = bank()
                for j in range(4):
                    p = PE("mt", lambda e, i=i, j=j, kk=4 * k4 + j: e.transpose(
                        TR[:, i, 128 * j:128 * j + W], M_[:, 128 * kk:128 * kk + 128], ident[0:W, 0:W]), [v, bf])
                yield 3, False
                ms = MS[k4 % 2]
                w = VE("msc", lambda e, i=i, ms=ms: e.tensor_copy(ms[:, :, 0:W], TR[:, i, :].rearrange(
                    "p (k c) -> p k c", c=128)[:, :, 0:W]), [p, free.get("MS%d" % (k4 % 2))] + extra)
                bank_free[i] = w
                yield 2, True
                i, bf = bank()
                for bb in range(nb2):
                    for j in range(4):
                        p = PE("po", lambda e, i=i, bb=bb, j=j, ms=ms: e.matmul(
                            TR[:, i, bb * NE:bb * NE + NE], X2[bb][:, j, :], ms[:, j, bb * NE:bb * NE + NE],
                            start=(j == 0), stop=(j == 3)), [w, xl[bb], bf])
                    free["X2%d" % bb] = p
                free["MS%d" % (k4 % 2)] = p
                yield 2, False
                for bb in range(nb2):
                    dst = PT[:, :, 2 * a_ + bb]
                    src = lambda i=i, bb=bb: TR[:, i, bb * NE:bb * NE + NE]
                    if k4 == 0:
                        gt.pt = VE("pt", lambda e, dst=dst, src=src: e.tensor_copy(dst, src()), [p] + extra)
                    else:
                        gt.pt = VE("pt", lambda e, dst=dst, src=src: e.tensor_tensor(dst, dst, src(), ALU.add),
                                   [p, gt.pt_prev])
                bank_free[i] = gt.pt
                gt.pt_prev = gt.pt
                yield 1.5, True

        side, urgent = [], []
        safe = [True]

        def step_side():
            if urgent and safe[0]:
                side.insert(0, urgent.pop(0))
            try:
                cost, safe[0] = next(side[0])
                return cost
            except StopIteration:
                side.pop(0)
                safe[0] = True
                return 0

        def until(test):
            while not test():
                assert side or urgent
                step_side()

        th_free = [None] * NTH
        busy = [False] * NTH
        st8 = {"th": 0, "s": None, "av": None, "esum": None, "acc": None, "den": None, "exr": [None, None]}
        S4 = TR[:, 0:4, :].rearrange("p a b -> p (a b)")

        def attention(b, I, epi):
            nblk = 16 * (I + 1)
            pieces, avs = [], []
            eready, css = [None, None], [0, 0]

            def scores(m, slots, cs):
                def go(c):
                    for q in range(4):
                        tile, lo, a, _ = slots[q]
                        l = max(512 * c, lo)
                        if l >= 512 * c + 512:
                            continue
                        p = PE("s", lambda e, q=q, l=l, tile=tile, lo=lo: e.matmul(
                            TR[32 * q:32 * q + 32, c, l - 512 * c:512], w2b[:, m, :], tile[:, l - lo:512 * c + 512 - lo],
                            start=(m == 0), stop=(m == 3), skip_group_check=True),
                            [a] + ([st8["s"]] if m == 0 else []) + ready)
                    st8["sp"] = p
                    if c == 3:
                        for _, _, _, sl in slots:
                            th_free[sl] = p
                            busy[sl] = False
                return [lambda c=c: go(c) for c in range(cs // 512, 4)]

            def values(j0, css, er):
                def go(c):
                    lo = max(512 * c, css[0])
                    for m in range(2):
                        l = max(512 * c, css[m])
                        if l >= 512 * c + 512:
                            continue
                        xt = X0[b % 2][:, j0 + m, :] if j0 < 4 else xnT[:, j0 + m - 4, :]
                        last = m == 1 or css[1] >= 512 * c + 512
                        p = PE("av", lambda e, l=l, m=m, last=last, xt=xt: e.matmul(
                            TR[:, 4, l - 512 * c:512], xt, EX[m][:, l:512 * c + 512],
                            start=(m == 0), stop=last, skip_group_check=True),
                            [er[m], xnv[b, (j0 + m) // 4], bank_free[4]])
                    if j0 == 0:
                        until(lambda: "ended" in epi)
                        v = VE("acc", lambda e: e.tensor_copy(acc[:, 512 * c:512 * c + 512], TR[:, 4, :]),
                               [p] + (free.get("acc") or []))
                    else:
                        v = VE("acc", lambda e: e.tensor_tensor(
                            acc[:, lo:512 * c + 512], acc[:, lo:512 * c + 512], TR[:, 4, lo - 512 * c:512],
                            ALU.add), [p, st8["acc"]])
                    st8["acc"] = v
                    bank_free[4] = v
                    st8["av"] = p
                return [lambda c=c: go(c) for c in range(css[0] // 512, 4)]

            def finish(jb, cs, diag):
                m2 = jb % 2
                while m2 == 0 and avs:
                    avs.pop(0)()
                a = AC("ex", lambda e: e.activation(EX[m2][:, cs:SUP], S4[:, cs:SUP], ACT.Exp, bias=b2r[:, 0:1]),
                       [st8["sp"], st8["av"], st8["exr"][m2]])
                st8["s"] = r = a
                if diag:
                    r = PO("mask", lambda e: e.affine_select(
                        out=EX[m2][:, cs:cs + 128], in_=EX[m2][:, cs:cs + 128], compare_op=ALU.is_gt,
                        fill=0.0, base=0, pattern=[[1, 128]], channel_multiplier=-1), [a])
                if jb == 0:
                    until(lambda: epi)
                    g = PO("es", lambda e: e.tensor_copy(esum, EX[m2]), [r, st8["den"]])
                else:
                    g = PO("es", lambda e: e.tensor_tensor(esum[:, cs:SUP], esum[:, cs:SUP], EX[m2][:, cs:SUP],
                                                           ALU.add), [r, st8["esum"]])
                st8["esum"] = g
                st8["exr"][m2] = g
                eready[m2], css[m2] = r, cs
                if m2 == 1:
                    avs.extend(values(jb - 1, tuple(css), tuple(eready)))

            plan = [(jb, m, max(0, jb * 128 - I * SUP), jb * 128 >= I * SUP)
                    for jb in range(nblk) for m in range(4)]
            short = {}

            def gcol(jb, o):
                return G0[b % 2][:, jb * 16 + o:jb * 16 + o + 1] if jb < 4 else Gk[:, jb * 16 + o:jb * 16 + o + 1]

            def fill(n):
                jb, m, cs, _ = plan[n]
                w = SUP - cs
                k = 2 if w > 512 else 1
                s = st8["th"] % NTH
                if s + k > NTH:
                    s = 0
                if any(busy[s:s + k]):
                    return False
                st8["th"] = s + k
                tile = arena[:, th0_at + s * SUP:th0_at + (s + k) * SUP].rearrange("p (q t) -> p q t", q=4)
                for q in range(4):
                    v = VE("fill", lambda e, q=q: e.tensor_scalar(
                        tile[:, q, 0:w], Fq[:, I * SUP + cs:I * SUP + SUP], gcol(jb, 4 * q + m), None, ALU.add),
                        [th_free[x] for x in range(s, s + k)] + [gv[b, jb // 4]] + fw)
                for x in range(s, s + k):
                    busy[x] = True
                short[n] = (tile, list(range(s, s + k)), v)
                return True

            def fill_ahead(n):
                w = SUP - plan[n][2]
                for x in range(n, min(n + (4 if w <= 512 else 2), len(plan))):
                    if SUP - plan[x][2] <= 1024 and x not in short:
                        until(lambda: (b, plan[x][0] // 4) in gv)
                        if not fill(x):
                            assert x > n
                            return

            ended = None
            for n, (jb, m, cs, diag) in enumerate(plan):
                until(lambda: (b, jb // 4) in gv)
                if I == 0 and n == 0:
                    until(lambda: all((b, kk) in fv for kk in range(4)) and "copied" in f0state[b])
                fw = [fv[b, 4 * I + kk] for kk in range(4)] + ([f0state[b]["copied"]] if I == 0 else [])
                w = SUP - cs
                if w <= 1024:
                    while pieces:
                        pieces.pop(0)()
                    fill_ahead(n)
                    tile, sls, v = short.pop(n)
                    a = AC("th4", lambda e, tile=tile, w=w: e.activation(tile[:, :, 0:w], tile[:, :, 0:w], ACT.Tanh),
                           [v])
                    if m == 0 and ended:
                        finish(*ended)
                        ended = None
                    elif avs and not (jb < 4 and m < 2 and "ended" not in epi and len(avs) == 4):
                        avs.pop(0)()
                    st8["thl"] = v
                    pieces = scores(m, [(tile[:, q, :], cs, a, sls[q % len(sls)]) for q in range(4)], cs)
                    yield 4 * w * 0.000833 + 0.25
                else:
                    slots = []
                    for q in range(4):
                        sl = st8["th"] % NTH
                        assert not busy[sl]
                        busy[sl] = True
                        st8["th"] = sl + 1
                        lo = cs + (32 * q if diag else 0)
                        a = AC("th", lambda e, sl=sl, lo=lo, gc=gcol(jb, 4 * q + m): e.activation(
                            TH[sl][:, lo:SUP], Fq[:, I * SUP + lo:I * SUP + SUP], ACT.Tanh, bias=gc),
                            [th_free[sl], gv[b, jb // 4]] + fw)
                        slots.append((TH[sl][:, lo:SUP], lo, a, sl))
                        st8["thl"] = a
                        if q == 0:
                            for _ in range(2):
                                if pieces:
                                    pieces.pop(0)()
                        elif q == 1:
                            while pieces:
                                pieces.pop(0)()
                        elif q == 2:
                            if m == 0 and ended:
                                finish(*ended)
                                ended = None
                            elif avs and not (jb < 4 and m < 2 and "ended" not in epi and len(avs) == 4):
                                avs.pop(0)()
                            if n + 1 < len(plan) and SUP - plan[n + 1][2] <= 1024:
                                until(lambda: (b, plan[n + 1][0] // 4) in gv)
                                fill(n + 1)
                        else:
                            pieces = scores(m, slots, cs)
                            pieces.pop(0)()
                        yield (SUP - lo) * 0.000833 + 0.3
                if m == 3:
                    ended = (jb, cs, diag)
            while pieces:
                pieces.pop(0)()
            finish(*ended)
            while avs:
                avs.pop(0)()

        f0state = {b: {} for b in range(NB)}

        def copy_f0(b, thw):
            v = VE("f0", lambda e: e.tensor_copy(Fq[:, 0:512], F0), [fv[b, 0], thw])
            free["F0"] = v
            f0state[b]["copied"] = v
            yield 0.5, True

        def marked(gen, state):
            yield from gen
            state.append("ended")

        for _ in mamba(0):
            pass
        for _ in prologue(0, [4, 5, 6, 7, 0], None, None):
            pass
        epi = ["begun", "ended"]
        th0 = av0 = None
        AT = 1055.0
        NP = max(1, NB // 2)
        MTs = [arena[:, a_ * L:a_ * L + L] for a_ in range(min(3, NP))]
        LG = arena[:, 12288:16384]
        X2 = [arena[:, 16384 + 512 * i:16896 + 512 * i].rearrange("p (k c) -> p k c", c=C) for i in range(2)]
        MS = [arena[:, 17408 + 512 * i:17920 + 512 * i].rearrange("p (k c) -> p k c", c=C) for i in range(2)]
        PT = arena[:, 18432:18432 + NE * NB].rearrange("p (e b) -> p e b", b=NB)
        T8 = arena[:, 18432 + 512:18432 + 528]
        gated = 0
        for b in range(NB):
            side.append(prologue(b, [1, 2, 3], th0, av0))
            side.append(copy_f0(b, th0))
            total = 1.05 * (8 * 20 + 3 * 17)
            if b + 1 < NB:
                side.append(mamba(b + 1))
                total += 1.05 * (4 * (14 + 19 + 13 + 16 * 8 + 28) + 30 + 5 * 17)
            else:
                def gates():
                    yield 1, True
                    ex = [p_last(PE), p_last(VE), p_last(AC), p_last(PO), t0s[NB - 1]]
                    for a_ in range(NP - 1):
                        yield from gate(a_, MTs[a_], LG, X2, MS, PT, T8, ex)
                side.append(gates())
                total += 110 * (NP - 1)
            rate = total / AT / 0.985
            spent = done = 0.0
            for I in (1, 0):
                state = []
                for cost in attention(b, I, epi):
                    spent += cost * rate
                    while (side or urgent) and done < spent:
                        done += step_side()
                    if not side:
                        done = spent
                epi = state
                e_ = marked(epilogue(b, I, st8["acc"], st8["esum"], state), state)
                thw, avw = st8["thl"], st8["av"]
                urgent.append(e_)
                if I == 1 and b + 1 < NB:
                    side.append(prologue(b + 1, [4, 5, 6, 7, 0], thw, avw))
            th0, av0 = thw, avw
            until(lambda: not side)
        MT_a = NP - 1

        at = [attn0]

        def take(n):
            a = at[0]
            at[0] += n
            return arena[:, a:a + n]

        NG = NE // EG
        NW = 5
        MTl = take(L)
        WAB = [take(2 * EG * NH) for _ in range(NW)]
        TO0 = take(L)
        OT = TO0[:, 0:NE * NB].rearrange("p (e b) -> p e b", b=NB)
        assert at[0] <= attn0 + L + 28 * C + 8 * C + (NTH + 3) * SUP, at[0]
        MTs = MTs[:NP - 1] + [MTl]
        ends = [p_last(PE), p_last(VE), p_last(AC), p_last(PO)]
        wfree = [None] * NW
        ldw = {}
        blo = EPc

        def load_w(gi):
            s = gi % NW
            e0 = gi * EG
            SP("w%d" % s, lambda e: e.dma_start(WAB[s][:, 0:EG * NH].rearrange("p (e n) -> p e n", e=EG),
                                                we1[e0:e0 + EG, 0:C, :].rearrange("e p n -> p e n")),
               ends + [wfree[s]], 16)
            ldw[gi] = SP("w%d" % s, lambda e: e.dma_start(
                WAB[s][:, EG * NH:].rearrange("p (e k n) -> p e k n", e=EG, k=4),
                we2[e0:e0 + EG, 0:NH, :].rearrange("e (p k) n -> p e k n", k=4)), ends + [wfree[s]], 16)

        until(lambda: not side and not urgent)
        ends2 = [p_last(PE), p_last(VE)]
        nb2 = min(2, NB)
        W = nb2 * NE
        B1 = acc[0:NE, 0:NH]
        B2 = acc[0:NE, NH:NH + C]
        B1T = acc[:, 1024:1024 + 4 * NE].rearrange("p (k e) -> p k e", k=4)
        B2T = acc[:, 1280:1280 + NE]
        HB = [acc[:, 1408 + 128 * i:1408 + 128 * i + EG * 4 * NB] for i in range(2)]
        HH = [acc[:, 1664 + 128 * i:1664 + 128 * i + EG * 4 * NB] for i in range(2)]
        OE = EPd
        accw = free["acc"]
        db = SP("bias", lambda e: e.dma_start(B1, we1[:, C:C + 1, :].rearrange("e a n -> e (a n)")), accw, 16)
        db = SP("bias", lambda e: e.dma_start(B2, we2[:, NH:NH + 1, :].rearrange("e a n -> e (a n)")), accw, 16)
        g7 = gate(MT_a, MTl, LG, X2, MS, PT, T8, ends)
        next(g7)
        for gi in range(NW):
            load_w(gi)
        i, bf = bank()
        for k_ in range(4):
            p = PE("bt", lambda e, i=i, k_=k_: e.transpose(TR[:, i, NE * k_:NE * k_ + NE], B1[:, k_::4],
                                                           ident[0:NE, 0:NE]), [db, bf])
        p = PE("bt", lambda e, i=i: e.transpose(TR[:, i, 4 * NE:5 * NE], B2, ident[0:NE, 0:NE]))
        v = VE("bt", lambda e, i=i: e.tensor_copy(acc[:, 1024:1024 + 5 * NE], TR[:, i, 0:5 * NE]), [p])
        bank_free[i] = bt = v
        for _ in g7:
            pass

        hf, hbf = [None, None], [None, None]
        bank_f = {0: None, 1: None, 2: None, 3: None, 4: bank_free[4]}
        for i in range(5, 8):
            bank_f[i] = bank_free[i]
        tt = [0]

        def tbank():
            i = tt[0] % 8
            tt[0] += 1
            return i

        HR = TO0[:, 512:512 + NH]
        OR = TO0[:, 1024:1024 + C]
        hrf = orf = None
        late = None

        def out_layer(gi, a, s):
            i2 = tbank()
            hs = HH[gi % 2].rearrange("p (k e b) -> p k e b", e=EG, k=4)
            WB = WAB[s][:, EG * NH:].rearrange("p (e k n) -> p e k n", e=EG, k=4)
            for k_ in range(4):
                for e_ in range(EG):
                    p = PE("o", lambda e, e_=e_, k_=k_: e.matmul(
                        TR[32 * e_:32 * e_ + NB, i2, 0:C], hs[:, k_, e_, :], WB[:, e_, k_, :],
                        start=(k_ == 0), stop=(k_ == 3), skip_group_check=True), [a, bank_f[i2]])
            hf[gi % 2] = p
            wfree[s] = p
            v = VE("or", lambda e: e.tensor_copy(OR, TR[:, i2, 0:C]), [p, st8.get("orf")])
            i3 = tbank()
            p = PE("ot", lambda e: e.transpose(TR[:, i3, 0:128], OR, ident[:, :]), [v, bank_f[i3]])
            bank_f[i2] = v
            st8["orf"] = p
            v = VE("ot", lambda e: e.tensor_tensor(
                OT[:, gi * EG:gi * EG + EG, :], TR[:, i3, 0:128].rearrange("p (e b) -> p e b", b=32)[:, :, 0:NB],
                B2T[:, gi * EG:gi * EG + EG].unsqueeze(2).to_broadcast([128, EG, NB]), ALU.add), [p, bt])
            bank_f[i3] = v
            if gi + NW < NG:
                load_w(gi + NW)
            return v

        for gi in range(NG):
            s = gi % NW
            i1 = tbank()
            WA = WAB[s][:, 0:EG * NH].rearrange("p (e n) -> p e n", e=EG)
            for e_ in range(EG):
                p = PE("h", lambda e, e_=e_, gi=gi, i1=i1, WA=WA: e.matmul(
                    TR[32 * e_:32 * e_ + NB, i1, :], PT[:, gi * EG + e_, :], WA[:, e_, :], start=True, stop=True,
                    skip_group_check=True), [ldw[gi], gt.pt, bank_f[i1]])
            v = VE("hr", lambda e, i1=i1: e.tensor_copy(HR, TR[:, i1, :]), [p, hrf])
            bank_f[i1] = v
            if late:
                ov = out_layer(*late)
            i1 = tbank()
            for k_ in range(4):
                p = PE("ht", lambda e, k_=k_, i1=i1: e.transpose(TR[:, i1, 128 * k_:128 * k_ + 128], HR[:, k_::4],
                                                                 ident[:, :]), [v, bank_f[i1]])
            hrf = p
            hb = HB[gi % 2].rearrange("p (k e b) -> p k e b", e=EG, k=4)
            for k_ in range(4):
                v = VE("hb", lambda e, hb=hb, i1=i1, k_=k_, gi=gi: e.tensor_tensor(
                    hb[:, k_, :, :],
                    TR[:, i1, 128 * k_:128 * k_ + 128].rearrange("p (e b) -> p e b", b=32)[:, :, 0:NB],
                    B1T[:, k_, gi * EG:gi * EG + EG].unsqueeze(2).to_broadcast([128, EG, NB]), ALU.add),
                    [p, bt, hbf[gi % 2]])
            bank_f[i1] = v
            a = AC("gelu", lambda e, gi=gi: e.activation(HH[gi % 2], HB[gi % 2], ACT.Gelu), [v, hf[gi % 2]])
            hbf[gi % 2] = a
            late = (gi, a, s)
        ov = out_layer(*late)
        oe = []
        for a_ in range(NP):
            i = tbank()
            for bb in range(nb2):
                v2 = VE("otp", lambda e, a_=a_, bb=bb: e.tensor_copy(
                    acc[:, (2 * a_ + bb) * NE:(2 * a_ + bb) * NE + NE], OT[:, :, 2 * a_ + bb]), [ov, bt])
            p = PE("oe", lambda e, i=i, a_=a_: e.transpose(
                TR[0:W, i, 0:128], acc[:, 2 * a_ * NE:2 * a_ * NE + W], ident[:, :]), [v2, bank_f[i]])
            w = VE("oe", lambda e, i=i, a_=a_: e.tensor_copy(OE[0:W, 128 * a_:128 * a_ + 128], TR[0:W, i, 0:128]),
                   [p])
            bank_f[i] = w
            oe.append(w)
        tof = {}
        fin = []
        for b in range(NB):
            s = b % NW
            t_ = WAB[s]
            d = SP("tl%d" % s, lambda e, b=b, t_=t_: e.dma_start(t_, t1d[b]), [tof.get(s), wfree[s]] + stored[b], 16)
            lo = (b % 2) * NE
            for c in range(8):
                i = tbank()
                p = PE("fo", lambda e, i=i, c=c, lo=lo, b=b: e.matmul(
                    TR[:, i, :], OE[lo:lo + NE, 128 * (b // 2):128 * (b // 2) + 128],
                    MTs[b // 2][lo:lo + NE, 512 * c:512 * c + 512], start=True, stop=True),
                    oe + [bank_f[i], gt.m])
                v = VE("fo", lambda e, i=i, c=c, t_=t_: e.tensor_tensor(
                    t_[:, 512 * c:512 * c + 512], t_[:, 512 * c:512 * c + 512], TR[:, i, :], ALU.add), [p, d])
                bank_f[i] = v
            d = SP("out%d" % s, lambda e, b=b, t_=t_: e.dma_start(od[b], t_), [v], 16)
            tof[s] = d
            fin.append(d)
        SP("end", lambda e: None, fin)

        emit = flush([PE, VE, AC, PO, SP], lambda n: ctx.enter_context(nc.semaphore(n)))
        ctx.enter_context(nc.allow_non_contiguous_dma(reason="small constants, strided rows"))
        block = ctx.enter_context(nc.Block())

        @block.tensor
        def _(e):
            emit(PE, e)

        @block.vector
        def _(e):
            emit(VE, e)

        @block.scalar
        def _(e):
            emit(AC, e)

        @block.gpsimd
        def _(e):
            emit(PO, e)

        @block.sync
        def _(e):
            emit(SP, e)


_INS = ["x", "L0_conv_W_in", "L0_conv_conv_w", "L0_conv_conv_b", "L0_conv_W_x", "L0_conv_W_dt", "L0_conv_b_dt",
        "L0_conv_A_log", "L0_conv_D", "L0_conv_W_out", "L0_conv_gn_gamma", "L0_conv_gn_beta", "L1_attn_W1",
        "L1_attn_b1", "L1_attn_w2", "L1_attn_b2", "L1_ffn_gate_w", "L1_ffn_gate_b", "L1_ffn_weight1",
        "L1_ffn_weight2"]


def kernel(**inputs):
    import numpy as _np
    import concourse.bacc as _bacc
    from concourse import mybir as _mybir
    from concourse.bass_utils import run_bass_kernel_spmd as _run

    nc = _bacc.Bacc("TRN2", target_bir_lowering=False, num_devices=1, dynamic_dma_scratch_size=1024)
    arrays, args = {}, []
    for name in _INS:
        a = _np.ascontiguousarray(inputs[name])
        arrays[f"in_{name}_dram"] = a
        args.append(nc.dram_tensor(f"in_{name}_dram", a.shape, _mybir.dt.from_np(a.dtype), kind="ExternalInput").ap())
    shape = inputs["x"].shape
    out = nc.dram_tensor("out_0_dram", shape, _mybir.dt.float32, kind="ExternalOutput").ap()
    hybrid_kernel(nc, shape[0], *args, out)
    r = _run(nc, [arrays], core_ids=[0])
    return r.results[0]["out_0_dram"]
```

```python
from contextlib import ExitStack

import concourse.bass as bass
from concourse import mybir

ALU = mybir.AluOpType
ACT = mybir.ActivationFunctionType
F32 = mybir.dt.float32
BF16 = mybir.dt.bfloat16

C = 128
L = 4096
DI = 256
NS = 16
T = 1024
SUP = 2048
NA = 16
NE = 64
NH = 512
EG = 4
NTH = 7
ARENA = 54400


class Done:

    def __init__(self, sem, step):
        self.sem, self.step, self.wanted, self.value = sem, step, False, None


class Queue:

    def __init__(self, name):
        self.name, self.items = name, []

    def __call__(self, sem, fn, waits=(), step=1):
        waits = [w for w in waits if w is not None]
        for w in waits:
            w.wanted = True
        d = Done(f"{self.name}_{sem}", step)
        d.wanted = step == 16
        self.items.append((waits, fn, d))
        return d


def flush(queues, new_sem):
    sems, owner, count = {}, {}, {}
    for q in queues:
        for _, _, d in q.items:
            if d.wanted:
                assert owner.setdefault(d.sem, q.name) == q.name
                count[d.sem] = count.get(d.sem, 0) + d.step
                d.value = count[d.sem]
                if d.sem not in sems:
                    sems[d.sem] = new_sem(d.sem)

    def emit(q, eng):
        seen = {}
        for waits, fn, d in q.items:
            need = {}
            for w in waits:
                need[w.sem] = max(need.get(w.sem, 0), w.value)
            for s, v in need.items():
                if seen.get(s, 0) < v:
                    eng.wait_ge(sems[s], v)
                    seen[s] = v
            ins = fn(eng)
            if d.wanted:
                ins.then_inc(sems[d.sem], d.step)
    return emit


def hybrid_kernel(nc, NB, x, W_in, conv_w, conv_b, W_x, W_dt, b_dt, A_log, D, W_out, gn_gamma, gn_beta,
                  W1, b1, w2, b2, gate_w, gate_b, we1, we2, out):
    ctx = ExitStack()
    with ctx:
        def sb(name, shape, dt=F32):
            return ctx.enter_context(nc.sbuf_tensor(name, shape, dt))

        PE, VE, AC, PO, SP = (Queue(n) for n in ("pe", "ve", "ac", "po", "sp"))
        TR = ctx.enter_context(nc.psum_tensor("banks", [128, 8, 512], F32))

        def dram(name, shape):
            return nc.dram_tensor(name, shape, F32, kind="Internal").ap()
        t0d = dram("t0_scratch", (NB, C, L))
        t1d = dram("t1_scratch", (NB, C, L))
        xtd = dram("xt_scratch", (NB, 128, L // 128, C))
        lgd = dram("lg_scratch", (NB, NE, L))
        xd = x.rearrange("b c h w -> b c (h w)")
        od = out.rearrange("b c h w -> b c (h w)")

        ident = sb("ident", [128, 128])
        ones = sb("ones", [128, 8])
        WinS = sb("WinS", [128, DI])
        Wc = sb("Wc", [128, 2, DI])
        Wx = sb("Wx", [128, 2, 104])
        Wdt = sb("Wdt", [128, DI])
        Wo = sb("Wo", [128, 2, C])
        sel = sb("sel", [128, 32], BF16)
        W1f = sb("W1f", [128, 8, NA])
        W1g = sb("W1g", [128, 8, NA])
        w2b = sb("w2b", [128, 4, 32])
        gw = sb("gw", [128, NE])
        gmask = sb("gmask", [128, 4, 32])
        rmask = sb("rmask", [128, 8])
        cb = sb("cb", [128, 2])
        cbh = sb("cbh", [128, 2])
        bdt = sb("bdt", [128, 2])
        Dv = sb("Dv", [128, 2])
        An = sb("An", [128, 2, NS])
        gam = sb("gam", [128, 2])
        b1r = sb("b1r", [128, 1])
        w2r = sb("w2r", [128, 1])
        b2r = sb("b2r", [128, 1])
        gb = sb("gb", [128, 1])
        mhalf = sb("mhalf", [128, 4])
        arena = sb("arena", [128, ARENA])
        top = [0]

        def cut(n):
            a = top[0]
            top[0] += n
            assert top[0] <= ARENA, top[0]
            return arena[:, a:a + n]

        U = [cut(2 * T).rearrange("p (h t) -> p h t", h=2) for _ in range(2)]
        dA = [cut(2 * T).rearrange("p (h t) -> p h t", h=2) for _ in range(2)]
        Y = cut(2 * T).rearrange("p (h t) -> p h t", h=2)
        XC = cut(2 * T).rearrange("p (h t) -> p h t", h=2)
        DT = cut(2 * T).rearrange("p (h t) -> p h t", h=2)
        BC = cut(T // 2).bitcast(BF16)
        XS = cut(516)
        MO = cut(L)
        attn0 = top[0]
        Fq = cut(L)
        xnT = cut(28 * C).rearrange("p (k c) -> p k c", c=C)
        X0 = [cut(4 * C).rearrange("p (k c) -> p k c", c=C) for _ in range(2)]
        th0_at = top[0]
        TH = [cut(SUP) for _ in range(NTH)]
        EX = [cut(SUP) for _ in range(2)]
        esum = cut(SUP)
        acc = cut(SUP)
        Gk = cut(L // 8)
        G0 = [cut(64) for _ in range(2)]
        F0 = cut(512)
        EPa = cut(512)
        EPb = cut(512)
        EPc = cut(512)
        EPd = cut(512)
        ST = cut(2 * NS).rearrange("p (h n) -> p h n", h=2)
        BN = cut(8 * 6).rearrange("p (k s) -> p k s", s=6)
        GS = cut(16)
        NRM = cut(40)
        RD = cut(16)

        S = {}

        def load(key, dst, src):
            S[key] = SP("const", lambda e, dst=dst, src=src: e.dma_start(dst, src), step=16)

        cwrow = TH[2][:, 0:2 * DI]
        wxl = TH[3][:, 0:2 * 40].rearrange("p (k n) -> p k n", k=2)
        w1l = TH[4][:, 0:2 * NA].rearrange("p (k n) -> p k n", k=2)
        al = TH[5][:, 0:2 * NS].rearrange("p (h n) -> p h n", h=2)
        wil = TH[1][:, 0:2 * DI]
        if True:
            load("win", wil, W_in)
            load("cw", cwrow, conv_w.rearrange("d k -> (d k)").partition_broadcast(128))
            load("cb", cb[:, :], conv_b.rearrange("(h p) -> p h", p=128))
            load("wx", wxl, W_x.rearrange("(k p) n -> p k n", p=128))
            load("wdt", Wdt[96:104, :], W_dt)
            load("bdt", bdt[:, :], b_dt.rearrange("(h p) -> p h", p=128))
            load("D", Dv[:, :], D.rearrange("(h p) -> p h", p=128))
            load("al", al, A_log.rearrange("(h p) n -> p h n", p=128))
            load("wo", Wo[:, :, :], W_out.rearrange("(k p) n -> p k n", p=128))
            load("gg", gam[:, 0:1], gn_gamma.rearrange("(p a) -> p a", a=1))
            load("gb", gam[:, 1:2], gn_beta.rearrange("(p a) -> p a", a=1))
            load("w1", w1l, W1.rearrange("(k p) n -> p k n", p=128))
            for r in range(8):
                load("b1", b1r[16 * r:16 * r + 16, :], b1.rearrange("(p a) -> p a", a=1))
                load("w2", w2r[16 * r:16 * r + 16, :], w2)
            load("b2", b2r[:, :], b2.partition_broadcast(128))
            load("gw", EPa[0:NE, 0:C], gate_w)
            load("gb2", gb[0:NE, :], gate_b.rearrange("(p a) -> p a", a=1))
            load("gb2", gb[NE:2 * NE, :], gate_b.rearrange("(p a) -> p a", a=1))
        cst = S["gb2"]

        k = PO("k", lambda e: e.memset(ident[:, :], 0.0))
        k = PO("k", lambda e: e.affine_select(out=ident[:, :], in_=ident[:, :], compare_op=ALU.not_equal, fill=1.0,
                                              base=0, pattern=[[-1, 128]], channel_multiplier=1), [k])
        k_id = k
        k = PO("k", lambda e: e.memset(sel[:, :], 0.0))
        for j in range(3):
            k = PO("k", lambda e, j=j: e.affine_select(out=sel[:, :], in_=sel[:, :], compare_op=ALU.not_equal,
                                                       fill=1.0, base=-32 * j, pattern=[[-1, 32]],
                                                       channel_multiplier=1), [k])
        for t_, v in ((gmask, 1.0 / 32), (rmask, 1.0), (ones, 1.0), (mhalf, -0.5)):
            k = PO("k", lambda e, t_=t_, v=v: e.memset(t_[:], v))
        k = PO("k", lambda e: e.affine_select(out=gmask[:, :, :], in_=gmask[:, :, :], compare_op=ALU.is_ge, fill=0.0,
                                              base=0, pattern=[[-32, 4], [0, 32]], channel_multiplier=1), [k])
        k = PO("k", lambda e: e.affine_select(out=gmask[:, :, :], in_=gmask[:, :, :], compare_op=ALU.is_ge, fill=0.0,
                                              base=31, pattern=[[32, 4], [0, 32]], channel_multiplier=-1), [k])
        k = PO("k", lambda e: e.affine_select(out=rmask[:, :], in_=rmask[:, :], compare_op=ALU.is_ge, fill=0.0,
                                              base=0, pattern=[[-16, 8]], channel_multiplier=1), [k])
        k = PO("k", lambda e: e.affine_select(out=rmask[:, :], in_=rmask[:, :], compare_op=ALU.is_ge, fill=0.0,
                                              base=15, pattern=[[16, 8]], channel_multiplier=-1), [k])
        k_po = k
        v = VE("k", lambda e: e.tensor_copy(WinS[:, :], wil[:, DI:2 * DI]), [cst])
        cw2 = cwrow.rearrange("p (d k) -> p k d", k=2)
        wil_d = DI
        for j in range(2):
            v = VE("k", lambda e, j=j: e.tensor_tensor(Wc[:, j, :], wil[:, 0:wil_d], cw2[:, j, :], ALU.mult))
        for g in range(3):
            v = VE("k", lambda e, g=g: e.tensor_copy(Wx[:, :, 32 * g:32 * g + 32], wxl[:, :, 8:40]))
        v = VE("k", lambda e: e.tensor_copy(Wx[:, :, 96:104], wxl[:, :, 0:8]))
        v = VE("k", lambda e: e.tensor_scalar(cbh[:, :], cb[:, :], 0.5, None, ALU.mult))
        v = VE("k", lambda e: e.tensor_copy(W1f[:, :, :], w1l[:, 0:1, :].to_broadcast([128, 8, NA])))
        v2 = VE("k", lambda e: e.memset(w2b[:, :, :], 0.0))
        v = VE("k", lambda e: e.tensor_copy(W1g[:, :, :], w1l[:, 1:2, :].to_broadcast([128, 8, NA])))
        for m in range(4):
            v = VE("k", lambda e, m=m: e.tensor_scalar(w2b[:, m, 8 * m:8 * m + 8], rmask[:, :], w2r[:, 0:1], None,
                                                       ALU.mult), [v2, k_po])
        for j in range(4):
            v = VE("k", lambda e, j=j: e.memset(TR[:, 2 * j:2 * j + 2, :], 0.0))
        a = AC("k", lambda e: e.activation(al, al, ACT.Exp), [cst])
        v = VE("k", lambda e: e.tensor_scalar(An[:, :, :], al, -1.0, None, ALU.mult), [a])
        p = PE("k", lambda e: e.transpose(TR[:, 7, 0:NE], EPa[0:NE, 0:C], ident[0:NE, 0:NE]), [cst, k_id, v])
        v = VE("k", lambda e: e.tensor_copy(gw[:, :], TR[:, 7, 0:NE]), [p])
        ready = [v, k_po, cst]

        v0 = v
        bank_free = {i: v for i in range(4, 8)}
        turn, base = [0], [4]

        def bank():
            i = base[0] + turn[0] % (8 - base[0])
            turn[0] += 1
            f = bank_free[i]
            assert f != "open"
            bank_free[i] = "open"
            return i, f

        free = {}
        t0s, t0v = {}, {}
        xnv, fv, gv = {}, {}, {}
        stored = {b: [] for b in range(NB)}

        def two(t):
            return t.rearrange("p (h t) -> p h t", h=2)

        class Part:

            def __init__(self, XC, DT, BC, Y, u0, u1, d0, d1, qu, qd, XS, xs):
                self.XC, self.DT, self.BC, self.Y, self.XS, self.xs = XC, DT, BC, Y, XS, xs
                self.u0, self.u1, self.d0, self.d1, self.qu, self.qd = (
                    two(t) if len(t.shape) == 2 else t for t in (u0, u1, d0, d1, qu, qd))
                self.w, self.pw = [], []
                self.wXC = self.wDT = self.wBC = self.wY = self.vb = None

        PN = Part(XC, DT, BC, Y, U[0], U[1], dA[0], dA[1], U[0], dA[0], XS, "XS")
        X2S = arena[:, attn0 + L:attn0 + L + 516]

        def mamba(b):
            xb = xd[b]

            def load_x(XS, key, g0, taps):
                w = [free.get(key)]
                if g0 == 0 and taps:
                    z = VE("xs0", lambda e: e.memset(XS[:, 0:1], 0.0), w)
                    d = SP(key.lower(), lambda e: e.dma_start(XS[:, 1:513], xb[:, 0:512]), w, 16)
                    return [z, d]
                lo = 1 if not taps else 0
                return [SP(key.lower(), lambda e: e.dma_start(XS[:, lo:513], xb[:, g0 - 1 + lo:g0 + 512]), w, 16)]

            alone = b == 0
            UR = U + [two(TH[0]), two(TH[1])] if alone else U
            DR = dA + [two(TH[6])] if alone else dA
            CB = [EX[0][:, 0:T], EX[0][:, T:2 * T]]
            NU, ND = len(UR), len(DR)
            uf, df, cf = [cst] * NU, [cst] * ND, [None, None]
            yfree = [v0]

            def before(c, P):
                for s in range(2):
                    ts = slice(s * 512, s * 512 + 512)
                    ld = load_x(XS, "XS", c * T + s * 512, True)
                    yield 3, True
                    bk = []
                    for h in range(2):
                        i, bf = bank()
                        for kk in range(2):
                            p = PE("xh", lambda e, i=i, kk=kk, h=h: e.matmul(
                                TR[:, i, :], Wc[:, kk, h * 128:h * 128 + 128], XS[:, kk:kk + 512],
                                start=(kk == 0), stop=(kk == 1)), ld + ready + [bf])
                        bk.append((i, p))
                        yield 2, False
                    free["XS"] = p
                    th = []
                    for h, (i, p) in enumerate(bk):
                        th.append(AC("xth", lambda e, i=i, h=h, ts=ts: e.activation(
                            P.d1[:, h, ts], TR[:, i, :], ACT.Tanh, bias=cbh[:, h:h + 1], scale=0.5), [p] + P.w))
                    yield 2, False
                    for h, (i, p) in enumerate(bk):
                        v1 = VE("xb", lambda e, i=i, h=h, ts=ts: e.tensor_scalar(
                            P.u1[:, h, ts], TR[:, i, :], cb[:, h:h + 1], 0.5, ALU.add, ALU.mult), [th[h]] + P.w)
                        bank_free[i] = v1
                        vx = VE("xc", lambda e, h=h, ts=ts: e.scalar_tensor_tensor(
                            out=P.XC[:, h, ts], in0=P.d1[:, h, ts], scalar=1.0, in1=P.u1[:, h, ts],
                            op0=ALU.add, op1=ALU.mult), [v1, P.wXC])
                for h in range(2):
                    vy = VE("y0", lambda e, h=h: e.tensor_scalar(P.Y[:, h, :], P.XC[:, h, :], Dv[:, h:h + 1], None,
                                                                 ALU.mult), [vx, P.wY])
                yield 3, True
                for s in range(2):
                    ts = slice(s * 512, s * 512 + 512)
                    i, bf = bank()
                    for h in range(2):
                        p = PE("xdbl", lambda e, i=i, h=h, ts=ts: e.matmul(
                            TR[0:104, i, :], Wx[:, h, :], P.XC[:, h, ts], start=(h == 0), stop=(h == 1)), [vx, bf])
                    yield 3, False
                    R = P.u1[:, 0, ts]
                    DL = P.u1[:, 1, ts]
                    mid = P.d1[:, 0, s * 256:s * 256 + 256].bitcast(BF16)
                    bcs = P.BC[:, ts]
                    q0 = VE("dl", lambda e, i=i, DL=DL: e.tensor_copy(DL[96:104, :], TR[96:104, i, :]), [p, vx])
                    q1 = VE("s1", lambda e, i=i, bcs=bcs: e.tensor_copy(bcs[0:96, :], TR[0:96, i, :]),
                            [p, P.wBC])
                    q2 = VE("s2", lambda e, i=i, bcs=bcs, R=R: e.tensor_tensor(
                        R[0:96, :], TR[0:96, i, :], bcs[0:96, :], ALU.subtract), [q1])
                    bank_free[i] = q2
                    bk = []
                    for h in range(2):
                        i, bf = bank()
                        p = PE("dt", lambda e, i=i, h=h, DL=DL: e.matmul(
                            TR[:, i, :], Wdt[96:104, h * 128:h * 128 + 128], DL[96:104, :], start=True, stop=True),
                            [q0, bf])
                        bk.append((i, p))
                    q3 = VE("s3", lambda e, mid=mid, R=R: e.tensor_copy(mid[0:96, :], R[0:96, :]), [q2])
                    q4 = VE("s4", lambda e, mid=mid, R=R: e.tensor_tensor(
                        R[0:96, :], R[0:96, :], mid[0:96, :], ALU.subtract), [q3])
                    q5 = VE("s5", lambda e, mid=mid, bcs=bcs: e.tensor_copy(bcs[32:64, :], mid[32:64, :]), [q3])
                    vbc = VE("s6", lambda e, R=R, bcs=bcs: e.tensor_copy(bcs[64:96, :], R[64:96, :]), [q4])
                    yield 3, False
                    for h, (i, p) in enumerate(bk):
                        vd = VE("dtv", lambda e, i=i, h=h, ts=ts: e.tensor_scalar(
                            P.u0[:, h, ts], TR[:, i, :], bdt[:, h:h + 1], None, ALU.add), [p] + P.w)
                        bank_free[i] = vd
                    yield 1, True
                vd = VE("dtm", lambda e: e.tensor_scalar(P.DT, P.u0, 0.0, None, ALU.max), [vd, P.wDT])
                vn = VE("dtn", lambda e: e.scalar_tensor_tensor(out=P.u0, in0=P.DT, scalar=-2.0, in1=P.u0,
                                                                op0=ALU.mult, op1=ALU.add), [vd])
                yield 5, True
                a1 = AC("sp1", lambda e: e.activation(P.d0, P.u0, ACT.Exp), [vn] + P.w)
                a2 = AC("sp2", lambda e: e.activation(P.u0, P.d0, ACT.Ln, bias=1.0), [a1])
                yield 3, True
                g1 = VE("sp3", lambda e: e.tensor_scalar(P.d1, P.d0, 1.0, -1.0, ALU.add, ALU.add), [a1, q5])
                g3 = PO("sp4", lambda e: e.tensor_tensor(P.d1, P.d0, P.d1, ALU.subtract), [g1])
                v3 = VE("sp5", lambda e: e.tensor_tensor(P.DT, P.DT, P.u0, ALU.add), [a2, vd])
                yield 3, True
                v3 = VE("sp6", lambda e: e.tensor_tensor(P.DT, P.DT, P.d1, ALU.add), [v3, g3])
                v4 = VE("dtx", lambda e: e.tensor_tensor(P.XC, P.XC, P.DT, ALU.mult), [v3, vy])
                yield 4, True
                P.v3, P.v4, P.vbc, P.vy, P.g3 = v3, v4, vbc, vy, g3
                P.w = [v4, vbc, g3, a2]

            def states(c, P):
                if not alone:
                    uf[:], df[:] = [P.v3, P.vbc], [P.g3, P.v3]
                v3, v4, vbc, vy = P.v3, P.v4, P.vbc, P.vy
                g = vy
                ysum = []

                def spread(col, s):
                    i, bf = bank()
                    p = PE("bc", lambda e: e.matmul(
                        TR[:, i, :], sel[0:96, col:col + 1].to_broadcast([96, 128]),
                        P.BC[0:96, s * 512:s * 512 + 512], start=True, stop=True), [vbc, bf])
                    return i, p

                for n in range(NS):
                    Un, En = UR[n % NU], DR[n % ND]
                    bk = [spread(n, s) for s in range(2)]
                    da = [AC("da", lambda e, h=h, n=n, En=En: e.activation(
                        En[:, h, :], P.DT[:, h, :], ACT.Exp, scale=An[:, h, n:n + 1]), [v3, df[n % ND]])
                        for h in range(2)]
                    for s, (i, p) in enumerate(bk):
                        w = VE("mb", lambda e, i=i, s=s, Un=Un: e.tensor_tensor(
                            Un[:, :, s * 512:s * 512 + 512], P.XC[:, :, s * 512:s * 512 + 512],
                            TR[:, i:i + 1, :].to_broadcast([128, 2, 512]), ALU.mult), [p, v4, uf[n % NU]])
                        bank_free[i] = w
                    yield 2.5, True
                    for h in range(2):
                        ini = 0.0 if c == 0 else ST[:, h, n:n + 1]
                        sc = VE("scan", lambda e, h=h, En=En, Un=Un, ini=ini: e.tensor_tensor_scan(
                            Un[:, h, :], En[:, h, :], Un[:, h, :], ini, ALU.mult, ALU.add),
                            [da[h], w, free.get("ST")])
                    df[n % ND] = sc
                    st = VE("st", lambda e, n=n, Un=Un: e.tensor_copy(ST[:, :, n:n + 1], Un[:, :, T - 1:T]), [sc])
                    free["ST"] = st
                    yield 2, True
                    bk = [spread(NS + n, s) for s in range(2)]
                    if alone:
                        for s, (i, p) in enumerate(bk):
                            w = AC("cb", lambda e, i=i, s=s, n=n: e.activation(
                                CB[n % 2][:, s * 512:s * 512 + 512], TR[:, i, :], ACT.Copy), [p, cf[n % 2]])
                            bank_free[i] = w
                        w = PO("mc", lambda e, n=n, Un=Un: e.tensor_tensor(
                            Un, Un, CB[n % 2].unsqueeze(1).to_broadcast([128, 2, T]), ALU.mult), [w, st])
                        cf[n % 2] = w
                        ysum.append((n, Un, w))
                        while len(ysum) > (2 if n < NS - 1 else 0):
                            n0, U0_, w = ysum.pop(0)
                            for q in range(4):
                                g = PE("y", lambda e, q=q, n0=n0, U0_=U0_: e.matmul(
                                    TR[:, q, :], ident[:, :], U0_[:, q // 2, 512 * (q % 2):512 * (q % 2) + 512],
                                    start=(n0 == 0), stop=(n0 == NS - 1)), [w, yfree[0]])
                            uf[n0 % NU] = g
                        yield 3.5, True
                        continue
                    for s, (i, p) in enumerate(bk):
                        w = VE("mc", lambda e, i=i, s=s, Un=Un: e.tensor_tensor(
                            Un[:, :, s * 512:s * 512 + 512], Un[:, :, s * 512:s * 512 + 512],
                            TR[:, i:i + 1, :].to_broadcast([128, 2, 512]), ALU.mult), [p, st])
                        bank_free[i] = w
                    g = PO("y", lambda e, Un=Un: e.tensor_tensor(P.Y, P.Y, Un, ALU.add), [w, vy, g])
                    uf[n % NU] = g
                    yield 3.5, True
                if alone:
                    for q in range(4):
                        g = VE("yp", lambda e, q=q: e.tensor_tensor(
                            P.Y[:, q // 2, 512 * (q % 2):512 * (q % 2) + 512],
                            P.Y[:, q // 2, 512 * (q % 2):512 * (q % 2) + 512], TR[:, q, :], ALU.add), [g, vy])
                    yfree[0] = g
                P.wBC, P.wXC, P.wDT, P.y, P.sc = p, w, da[1], g, sc

            def after(c, P):
                for s in range(2):
                    ts = slice(s * 512, s * 512 + 512)
                    g0 = c * T + s * 512
                    ld = load_x(P.XS, P.xs, g0, False)
                    yield 3, True
                    bk = []
                    for h in range(2):
                        i, bf = bank()
                        p = PE("z", lambda e, i=i, h=h: e.matmul(
                            TR[:, i, :], WinS[:, h * 128:h * 128 + 128], P.XS[:, 1:513], start=True, stop=True),
                            ld + [bf])
                        bk.append((i, p))
                    free[P.xs] = p
                    yield 3, False
                    th = [AC("zth", lambda e, i=i, h=h, ts=ts: e.activation(
                        P.qd[:, h, ts], TR[:, i, :], ACT.Tanh, scale=0.5), [p] + P.pw + [P.sc])
                        for h, (i, p) in enumerate(bk)]
                    yield 2, False
                    for h, (i, p) in enumerate(bk):
                        w = VE("zz", lambda e, i=i, h=h, ts=ts: e.scalar_tensor_tensor(
                            out=P.qu[:, h, ts], in0=P.qd[:, h, ts], scalar=1.0, in1=TR[:, i, :],
                            op0=ALU.add, op1=ALU.mult), [th[h]] + P.pw + [P.y])
                        bank_free[i] = w
                    yz = VE("yz", lambda e, ts=ts: e.scalar_tensor_tensor(
                        out=P.qu[:, :, ts], in0=P.Y[:, :, ts], scalar=0.5, in1=P.qu[:, :, ts],
                        op0=ALU.mult, op1=ALU.mult), [w, P.y])
                    yield 3, True
                    i, bf = bank()
                    for h in range(2):
                        p = PE("mo", lambda e, i=i, h=h, ts=ts: e.matmul(
                            TR[:, i, :], Wo[:, h, :], P.qu[:, h, ts], start=(h == 0), stop=(h == 1)), [yz, bf])
                    yield 3, False
                    w = VE("moc", lambda e, i=i, g0=g0: e.tensor_copy(MO[:, g0:g0 + 512], TR[:, i, :]),
                           [p, free.get("MO")])
                    vb = VE("mobn", lambda e, i=i, kk=2 * c + s: e.bn_stats(BN[:, kk, :], TR[:, i, :]), [p])
                    bank_free[i] = PN.vb = vb
                P.wY = yz
                P.pw = [p, w]
                if not alone:
                    P.w = [p, w, P.y, P.sc]
                    P.pw = []

            if alone:
                P2 = [Part(XC, DT, BC, Y, TH[2], TH[3], TH[4], TH[5], Fq[:, 0:SUP], Fq[:, SUP:], X2S, "XS2"),
                      Part(two(EX[1]), two(esum), EPa.bitcast(BF16), two(acc), TH[2], TH[3], TH[4], TH[5],
                           Fq[:, 0:SUP], Fq[:, SUP:], X2S, "XS2")]
                P2[0].w = list(ready)
                yield from before(0, P2[0])
                for c in range(L // T):
                    P, O = P2[c % 2], P2[(c + 1) % 2]
                    O.w = P.w

                    def beside():
                        if c:
                            yield from after(c - 1, O)
                            P.pw = O.pw
                        if c + 1 < L // T:
                            yield from before(c + 1, O)
                    more, held, due = beside(), False, 0.0
                    rate = ((28 if c else 0) + (45 if c + 1 < L // T else 0)) / 110.0
                    for cost, _ in states(c, P):
                        due += cost * rate
                        while more and (due > 0 or held):
                            got = next(more, None)
                            if got is None:
                                more, held = None, False
                            else:
                                due -= got[0]
                                held = not got[1]
                        yield cost, True
                    if more:
                        yield from more
                yield from after(c, P)
                PN.w = [p_last(PE), p_last(VE), p_last(PO), p_last(AC)]
                PN.wXC, PN.wDT, PN.wBC, PN.wY = P2[0].wXC, P2[0].wDT, P2[0].wBC, P2[0].wY
            else:
                for c in range(L // T):
                    yield from before(c, PN)
                    yield from states(c, PN)
                    yield from after(c, PN)
            vb = PN.vb
            v = VE("gn", lambda e: e.bn_aggr(GS[:, 0:2], BN.rearrange("p k s -> p (k s)")), [vb])
            v = VE("gn", lambda e: e.tensor_scalar(GS[:, 2:3], GS[:, 0:1], GS[:, 0:1], GS[:, 1:2], ALU.mult, ALU.add),
                   [v])
            v = VE("gn", lambda e: e.tensor_copy(GS[:, 1:2], GS[:, 2:3]), [v])
            yield 2, True
            i, bf = bank()
            p = PE("gn", lambda e, i=i: e.matmul(TR[:, i, 0:2], gmask[:, :, :].rearrange("p a b -> p (a b)"),
                                                 GS[:, 0:2], start=True, stop=True), [v, bf])
            v = VE("gn", lambda e, i=i: e.tensor_copy(GS[:, 4:6], TR[:, i, 0:2]), [p])
            bank_free[i] = v
            v = VE("gn", lambda e: e.tensor_tensor(GS[:, 6:7], GS[:, 4:5], GS[:, 4:5], ALU.mult), [v])
            v = VE("gn", lambda e: e.tensor_tensor(GS[:, 7:8], GS[:, 5:6], GS[:, 6:7], ALU.subtract), [v])
            v = VE("gn", lambda e: e.tensor_scalar(GS[:, 7:8], GS[:, 7:8], 1e-5, None, ALU.add), [v])
            g = PO("gn", lambda e: e.tensor_tensor(GS[:, 8:9], GS[:, 7:8], mhalf[:, 0:1], ALU.pow), [v, k_po])
            v = VE("gn", lambda e: e.tensor_tensor(GS[:, 9:10], GS[:, 8:9], gam[:, 0:1], ALU.mult), [g])
            v = VE("gn", lambda e: e.tensor_tensor(GS[:, 10:11], GS[:, 9:10], GS[:, 4:5], ALU.mult), [v])
            gnv = VE("gn", lambda e: e.tensor_tensor(GS[:, 11:12], gam[:, 1:2], GS[:, 10:11], ALU.subtract), [v])
            order = [4, 5, 6, 7, 0, 1, 2, 3]
            stage = {}

            def t0_in(n):
                kk, s = order[n], n % 2
                sl = slice(kk * 512, kk * 512 + 512)
                d = SP("t0x%d" % s, lambda e: e.dma_start(U[1][:, 0, s * 512:s * 512 + 512], xb[:, sl]),
                       PN.w + [t0_use[s]], 16)
                w = VE("t0a", lambda e: e.tensor_scalar(MO[:, sl], MO[:, sl], GS[:, 9:10], GS[:, 11:12],
                                                        ALU.mult, ALU.add), [gnv])
                stage[n] = (d, w)

            t0_use = [None, None]
            t0_in(0)
            yield 4, True
            for n, kk in enumerate(order):
                s = n % 2
                sl = slice(kk * 512, kk * 512 + 512)
                d, w = stage[n]
                a = AC("t0b", lambda e, s=s, sl=sl: e.activation(dA[1][:, 0, s * 512:s * 512 + 512], MO[:, sl],
                                                                 ACT.Tanh, scale=0.5), [w, t0_use[s]] + PN.w)
                if n < 7:
                    t0_in(n + 1)
                yield 1.5, True
                w = VE("t0c", lambda e, s=s, sl=sl: e.scalar_tensor_tensor(
                    out=MO[:, sl], in0=dA[1][:, 0, s * 512:s * 512 + 512], scalar=1.0, in1=MO[:, sl],
                    op0=ALU.add, op1=ALU.mult), [a, w])
                w = VE("t0d", lambda e, s=s, sl=sl: e.scalar_tensor_tensor(
                    out=MO[:, sl], in0=MO[:, sl], scalar=0.5, in1=U[1][:, 0, s * 512:s * 512 + 512],
                    op0=ALU.mult, op1=ALU.add), [w, d])
                t0_use[s] = w
                t0v[kk] = w
                t0s[b] = SP("t0s", lambda e, sl=sl: e.dma_start(t0d[b][:, sl], MO[:, sl]), [w, t0s.get(b - 1)], 16)
                yield 1.5, True
            PN.w = [p_last(PE), w]

        def p_last(q):
            return q.items[-1][2]

        class Norm:

            def __init__(self, key, small, EPb, EPc):
                self.key, self.EPb, self.EPc = key, EPb, EPc
                self.B4 = small[:, 0:24].rearrange("p (k s) -> p k s", s=6)
                self.MV = small[:, 24:32].rearrange("p (k s) -> p k s", s=2)
                self.RS = small[:, 32:40]

        Z0 = Norm("", NRM, EPb, EPc)

        def normed(src, waits, dst, dstw, Z=None):
            Z = Z or Z0
            i, bf = bank()
            for j in range(4):
                p = PE("tr", lambda e, j=j: e.transpose(TR[:, i, 128 * j:128 * j + 128],
                                                        src[:, 128 * j:128 * j + 128], ident[:, :]), waits + [bf])
            yield 3, False
            for j in range(4):
                v = VE("ln1", lambda e, j=j: e.bn_stats(Z.B4[:, j, :], TR[:, i, 128 * j:128 * j + 128]), [p])
            for j in range(4):
                v2 = VE("ln2", lambda e, j=j: e.bn_aggr(Z.MV[:, j, :], Z.B4[:, j, :]), [v, free.get("MV" + Z.key)])
            g = PO("ln", lambda e: e.tensor_scalar(Z.RS[:, 0:4], Z.MV[:, :, 1], 1e-5, None, ALU.add),
                   [v2, free.get("RS" + Z.key)])
            g = PO("ln", lambda e: e.tensor_tensor(Z.RS[:, 4:8], Z.RS[:, 0:4], mhalf[:, :], ALU.pow), [g, k_po])
            yield 4, False
            for j in range(4):
                v = VE("ln3", lambda e, j=j: e.tensor_scalar(
                    dst[:, j, :], TR[:, i, 128 * j:128 * j + 128], Z.MV[:, j, 0:1], Z.RS[:, 4 + j:5 + j],
                    ALU.subtract, ALU.mult), [g, v2] + dstw)
            free["MV" + Z.key] = free["RS" + Z.key] = v
            bank_free[i] = v
            yield 2, True
            i2, bf = bank()
            for j in range(4):
                p = PE("tr2", lambda e, j=j: e.transpose(TR[:, i2, 128 * j:128 * j + 128], dst[:, j, :],
                                                         ident[:, :]), [v, bf])
            yield 2, False
            w = VE("ln4", lambda e: e.tensor_copy(Z.EPb, TR[:, i2, :]), [p, free.get("EPb" + Z.key)])
            bank_free[i2] = w
            yield 1.5, True
            return v, p, w

        def prologue(b, kks, thw, avw, Z=None):
            Z = Z or Z0
            for kk in kks:
                while kk not in t0v:
                    yield 0, True
                sl = slice(kk * 512, kk * 512 + 512)
                if kk == 0:
                    dst, Fd, Gd = X0[b % 2], F0, G0[b % 2]
                else:
                    dst, Fd, Gd = xnT[:, 4 * kk - 4:4 * kk, :], Fq[:, sl], Gk[:, kk * 64:kk * 64 + 64]
                v, p, w = yield from normed(MO[:, sl], [t0v[kk]], dst, [avw], Z)
                free["MO"] = p
                xnv[b, kk] = v
                i, bf = bank()
                p = PE("g", lambda e, i=i: e.matmul(TR[:, i, :], W1g[:, :, :].rearrange("p a b -> p (a b)"), Z.EPb,
                                                    start=True, stop=True), [w, bf])
                i2, bf = bank()
                p2 = PE("f", lambda e, i=i2: e.matmul(TR[:, i, :], W1f[:, :, :].rearrange("p a b -> p (a b)"), Z.EPb,
                                                      start=True, stop=True), [w, bf])
                free["EPb" + Z.key] = p2
                yield 2.5, False
                v = VE("g1", lambda e, i=i: e.tensor_tensor(
                    Z.EPc.rearrange("p (o r) -> p o r", r=8), TR[:, i, :].rearrange("p (o r) -> p o r", r=8),
                    rmask[:, :].unsqueeze(1).to_broadcast([128, 64, 8]), ALU.mult), [p, free.get("EPc" + Z.key)])
                bank_free[i] = v
                gv[b, kk] = VE("g2", lambda e, Gd=Gd: e.tensor_reduce(
                    Gd, Z.EPc.rearrange("p (o r) -> p o r", r=8), mybir.AxisListType.X, ALU.add), [v, thw])
                free["EPc" + Z.key] = gv[b, kk]
                v = VE("f", lambda e, i=i2, Fd=Fd: e.tensor_scalar(Fd, TR[:, i, :], b1r[:, 0:1], None, ALU.add),
                       [p2, thw, free.get("F0")])
                fv[b, kk] = v
                bank_free[i2] = v
                yield 2, True

        def epilogue(b, I, accw, esumw, state, second=None):
            i, bf = bank()
            for kk in range(16):
                p = PE("den", lambda e, i=i, kk=kk: e.matmul(TR[:, i, kk:kk + 1], esum[:, 128 * kk:128 * kk + 128],
                                                             ones[:, 0:1], start=True, stop=True), [esumw, bf])
            st8["den"] = p
            state.append("begun")
            yield 3, False
            v = VE("den", lambda e, i=i: e.tensor_scalar(RD, TR[:, i, 0:16], 1e-10, None, ALU.add),
                   [p, free.get("RD")])
            bank_free[i] = v
            vr = VE("den", lambda e: e.reciprocal(RD, RD), [v])
            yield 1, True
            accs = []

            def logits(kk, w, Z):
                gl = slice(I * SUP + kk * 512, I * SUP + kk * 512 + 512)
                i, bf = bank()
                p = PE("lg", lambda e: e.matmul(TR[0:NE, i, :], gw[:, :], Z.EPb, start=True, stop=True), [w, bf])
                free["EPb" + Z.key] = p

                def out_():
                    v = VE("lg", lambda e: e.tensor_scalar(EPc[0:NE, :], TR[0:NE, i, :], gb[0:NE, 0:1], None,
                                                           ALU.add), [p, free.get("EPc")])
                    bank_free[i] = v
                    dl = SP("lgs", lambda e: e.dma_start(lgd[b][:, gl], EPc[0:NE, :]), [v], 16)
                    free["EPc"] = dl
                    stored[b].append(dl)
                return out_

            def tiles(kks, Z, EPa, EPd):
                last = prev = None
                for kk in kks:
                    sl = slice(kk * 512, kk * 512 + 512)
                    gl = slice(I * SUP + kk * 512, I * SUP + kk * 512 + 512)
                    i, bf = bank()
                    for j in range(4):
                        p = PE("rb", lambda e, i=i, j=j, col=4 * kk + j: e.matmul(
                            TR[:, i, 128 * j:128 * j + 128], RD[:, col:col + 1].to_broadcast([128, 128]), ident[:, :],
                            start=True, stop=True), [vr, bf])
                    free["RD"] = p
                    lo_ = logits(prev, last, Z) if last is not None else None
                    d = SP("t0l" + Z.key, lambda e, gl=gl: e.dma_start(EPa, t0d[b][:, gl]), [t0s[b], free.get("EPa" + Z.key)], 16)
                    yield 2.5, False
                    v = VE("t1", lambda e, i=i, sl=sl: e.tensor_tensor(acc[:, sl], acc[:, sl], TR[:, i, :], ALU.mult),
                           [p, accw])
                    bank_free[i] = v
                    v = VE("t1", lambda e, sl=sl: e.tensor_tensor(acc[:, sl], acc[:, sl], EPa, ALU.add), [v, d])
                    free["EPa" + Z.key] = v
                    d = SP("t1s", lambda e, gl=gl, sl=sl: e.dma_start(t1d[b][:, gl], acc[:, sl]), [v], 16)
                    stored[b].append(d)
                    if lo_:
                        lo_()
                    yield 1.5, True
                    x2 = EPd.rearrange("p (k c) -> p k c", c=C)
                    v, p, last = yield from normed(acc[:, sl], [v], x2, [free.get("EPd" + Z.key), free.get("EPp" + Z.key)], Z)
                    free["EPp" + Z.key] = p
                    dx = SP("x2s" + Z.key, lambda e, kk=kk: e.dma_start(xtd[b][:, 16 * I + 4 * kk:16 * I + 4 * kk + 4, :], x2),
                            [v], 16)
                    free["EPd" + Z.key] = dx
                    stored[b].append(dx)
                    accs.extend([d, last])
                    free["acc"] = accs
                    prev = kk
                lo_ = logits(prev, last, Z)
                yield 2, False
                lo_()

            if second is None:
                yield from tiles(range(4), Z0, EPa, EPd)
                return
            streams = [tiles([0, 2], Z0, EPa, EPd), tiles([1, 3], *second)]
            held = {}
            while streams:
                for g in list(streams):
                    got = next(g, None)
                    if got is None:
                        streams.remove(g)
                        held.pop(g, None)
                        continue
                    held[g] = not got[1]
                    yield got[0], not any(held.values())

        class Gate:
            pass

        gt = Gate()

        def gate(a_, MTa, LG, X2, MS, PT, T8, extra, XR=None):
            nb2 = min(2, NB)
            W = nb2 * NE
            deps = extra + [x for bb in range(nb2) for x in stored[2 * a_ + bb]]
            Lg, M_ = LG[0:W, :], MTa[0:W, :]
            l_ = SP("lgl", lambda e: e.dma_start(Lg, lgd[2 * a_:2 * a_ + nb2].rearrange("b e s -> (b e) s")),
                    deps + [free.get("LG")], 16)
            yield 8, True
            v = VE("g3", lambda e: e.max(T8[0:W, 0:8], Lg), [l_, free.get("T8")])
            v = VE("g4", lambda e: e.tensor_scalar(T8[0:W, 9:10], T8[0:W, 0:1], -1.0, None, ALU.mult), [v])
            yield 5, True
            a = AC("g", lambda e: e.activation(M_, Lg, ACT.Exp, bias=T8[0:W, 9:10], accum_out=T8[0:W, 10:11]),
                   [v] + extra)
            yield 4, True
            v = VE("g5", lambda e: e.reciprocal(T8[0:W, 11:12], T8[0:W, 10:11]), [a])
            v = VE("g6", lambda e: e.tensor_scalar(M_, M_, T8[0:W, 11:12], None, ALU.mult), [v])
            v = VE("g7", lambda e: e.max(T8[0:W, 0:8], M_), [v])
            yield 6, True
            v = VE("g8", lambda e: e.match_replace(out=Lg, in_to_replace=T8[0:W, 0:8], in_values=M_,
                                                   imm_value=0.0), [v])
            yield 4, True
            v = VE("g9", lambda e: e.tensor_tensor(M_, M_, Lg, ALU.subtract), [v])
            free["LG"] = free["T8"] = v
            gt.m = v
            yield 5, True
            if XR is not None:
                slots = [[XR[:, 2048 * bb + 512 * i:2048 * bb + 512 * i + 512].rearrange("p (k c) -> p k c", c=C)
                          for i in range(4)] for bb in range(nb2)]
                used, xl, mt = {}, {}, {}

                def fetch(k4):
                    for bb in range(nb2):
                        xl[bb, k4] = SP("x2f%d%d" % (bb, k4 % 4), lambda e, bb=bb: e.dma_start(
                            slots[bb][k4 % 4], xtd[2 * a_ + bb][:, 4 * k4:4 * k4 + 4, :]),
                            deps + [used.get((bb, k4 - 4))], 16)

                def turned(k4):
                    i, bf = bank()
                    for j in range(4):
                        p = PE("mt", lambda e, j=j: e.transpose(
                            TR[:, i, 128 * j:128 * j + W], M_[:, 128 * (4 * k4 + j):128 * (4 * k4 + j) + 128],
                            ident[0:W, 0:W]), [v, bf])
                    src = TR[:, i, :].rearrange("p (k c) -> p k c", c=128)[:, :, 0:W]
                    w = [p, free.get("MS%d" % (k4 % 2))] + extra
                    if k4 % 2:
                        mt[k4] = AC("msc", lambda e: e.activation(MS[1][:, :, 0:W], src, ACT.Copy), w)
                    else:
                        mt[k4] = VE("msc", lambda e: e.tensor_copy(MS[0][:, :, 0:W], src), w)
                    bank_free[i] = mt[k4]

                for k4 in range(4):
                    fetch(k4)
                turned(0)
                for k4 in range(8):
                    if k4 < 7:
                        turned(k4 + 1)
                    for bb in range(nb2):
                        for j in range(4):
                            p = PE("po", lambda e, bb=bb, j=j, k4=k4: e.matmul(
                                TR[:, bb, 0:NE], slots[bb][k4 % 4][:, j, :],
                                MS[k4 % 2][:, j, bb * NE:bb * NE + NE],
                                start=(k4 == 0 and j == 0), stop=(k4 == 7 and j == 3)),
                                [mt[k4], xl[bb, k4]] + st8["s"])
                        used[bb, k4] = p
                    free["MS%d" % (k4 % 2)] = p
                    if k4 < 4:
                        fetch(k4 + 4)
                for bb in range(nb2):
                    gt.pt = VE("pt", lambda e, bb=bb: e.tensor_copy(PT[:, :, 2 * a_ + bb], TR[:, bb, 0:NE]),
                               [p] + extra)
                return
            for k4 in range(8):
                xl = []
                for bb in range(nb2):
                    xl.append(SP("x2l%d" % bb, lambda e, bb=bb, k4=k4: e.dma_start(
                        X2[bb], xtd[2 * a_ + bb][:, 4 * k4:4 * k4 + 4, :]), deps + [free.get("X2%d" % bb)], 16))
                i, bf = bank()
                for j in range(4):
                    p = PE("mt", lambda e, i=i, j=j, kk=4 * k4 + j: e.transpose(
                        TR[:, i, 128 * j:128 * j + W], M_[:, 128 * kk:128 * kk + 128], ident[0:W, 0:W]), [v, bf])
                yield 3, False
                ms = MS[k4 % 2]
                w = VE("msc", lambda e, i=i, ms=ms: e.tensor_copy(ms[:, :, 0:W], TR[:, i, :].rearrange(
                    "p (k c) -> p k c", c=128)[:, :, 0:W]), [p, free.get("MS%d" % (k4 % 2))] + extra)
                bank_free[i] = w
                yield 2, True
                i, bf = bank()
                for bb in range(nb2):
                    for j in range(4):
                        p = PE("po", lambda e, i=i, bb=bb, j=j, ms=ms: e.matmul(
                            TR[:, i, bb * NE:bb * NE + NE], X2[bb][:, j, :], ms[:, j, bb * NE:bb * NE + NE],
                            start=(j == 0), stop=(j == 3)), [w, xl[bb], bf])
                    free["X2%d" % bb] = p
                free["MS%d" % (k4 % 2)] = p
                yield 2, False
                for bb in range(nb2):
                    dst = PT[:, :, 2 * a_ + bb]
                    src = lambda i=i, bb=bb: TR[:, i, bb * NE:bb * NE + NE]
                    if k4 == 0:
                        gt.pt = VE("pt", lambda e, dst=dst, src=src: e.tensor_copy(dst, src()), [p] + extra)
                    else:
                        gt.pt = VE("pt", lambda e, dst=dst, src=src: e.tensor_tensor(dst, dst, src(), ALU.add),
                                   [p, gt.pt_prev])
                bank_free[i] = gt.pt
                gt.pt_prev = gt.pt
                yield 1.5, True

        side, urgent = [], []
        safe = [True]

        def step_side():
            if urgent and safe[0]:
                side.insert(0, urgent.pop(0))
            try:
                cost, safe[0] = next(side[0])
                return cost
            except StopIteration:
                side.pop(0)
                safe[0] = True
                return 0

        def until(test):
            while not test():
                assert side or urgent
                step_side()

        th_free = [None] * NTH
        busy = [False] * NTH
        st8 = {"th": 0, "s": [None, None], "av": None, "esum": None, "acc": None, "den": None, "exr": [None, None]}
        S4 = TR[:, 0:4, :].rearrange("p a b -> p (a b)")

        def attention(b, I, epi):
            nblk = 16 * (I + 1)
            pieces, avs = [], []
            eready, css = [None, None], [0, 0]

            def low(jb, cs):
                return 2 if SUP - cs <= 1024 and jb % 2 == 0 else 0

            def scores(m, slots, cs, jb):
                sh = low(jb, cs)

                def go(c):
                    for q in range(4):
                        tile, lo, a, _ = slots[q]
                        l = max(512 * c, lo)
                        if l >= 512 * c + 512:
                            continue
                        p = PE("s", lambda e, q=q, l=l, tile=tile, lo=lo: e.matmul(
                            TR[32 * q:32 * q + 32, c - sh, l - 512 * c:512], w2b[:, m, :], tile[:, l - lo:512 * c + 512 - lo],
                            start=(m == 0), stop=(m == 3), skip_group_check=True),
                            [a] + ([st8["s"][(c - sh) // 2]] if m == 0 else []) + ready)
                    if m == 3:
                        st8["sp"] = p
                    if c == 3:
                        for _, _, _, sl in slots:
                            th_free[sl] = p
                            busy[sl] = False
                return [lambda c=c: go(c) for c in range(cs // 512, 4)]

            def values(j0, css, er):
                def go(c):
                    lo = max(512 * c, css[0])
                    for m in range(2):
                        l = max(512 * c, css[m])
                        if l >= 512 * c + 512:
                            continue
                        xt = X0[b % 2][:, j0 + m, :] if j0 < 4 else xnT[:, j0 + m - 4, :]
                        last = m == 1 or css[1] >= 512 * c + 512
                        p = PE("av", lambda e, l=l, m=m, last=last, xt=xt: e.matmul(
                            TR[:, 4, l - 512 * c:512], xt, EX[m][:, l:512 * c + 512],
                            start=(m == 0), stop=last, skip_group_check=True),
                            [er[m], xnv[b, (j0 + m) // 4], bank_free[4]])
                    if j0 == 0:
                        until(lambda: "ended" in epi)
                        v = VE("acc", lambda e: e.tensor_copy(acc[:, 512 * c:512 * c + 512], TR[:, 4, :]),
                               [p] + (free.get("acc") or []))
                    else:
                        v = VE("acc", lambda e: e.tensor_tensor(
                            acc[:, lo:512 * c + 512], acc[:, lo:512 * c + 512], TR[:, 4, lo - 512 * c:512],
                            ALU.add), [p, st8["acc"]])
                    st8["acc"] = v
                    bank_free[4] = v
                    st8["av"] = p
                return [lambda c=c: go(c) for c in range(css[0] // 512, 4)]

            def finish(jb, cs, diag):
                m2 = jb % 2
                while m2 == 0 and avs:
                    avs.pop(0)()
                sh = 512 * low(jb, cs)
                a = AC("ex", lambda e: e.activation(EX[m2][:, cs:SUP], S4[:, cs - sh:SUP - sh], ACT.Exp,
                                                    bias=b2r[:, 0:1]),
                       [st8["sp"], st8["av"], st8["exr"][m2]])
                r = a
                for h in range((cs - sh) // 1024, (SUP - sh) // 1024):
                    st8["s"][h] = a
                if diag:
                    r = PO("mask", lambda e: e.affine_select(
                        out=EX[m2][:, cs:cs + 128], in_=EX[m2][:, cs:cs + 128], compare_op=ALU.is_gt,
                        fill=0.0, base=0, pattern=[[1, 128]], channel_multiplier=-1), [a])
                if jb == 0:
                    until(lambda: epi)
                    g = PO("es", lambda e: e.tensor_copy(esum, EX[m2]), [r, st8["den"]])
                else:
                    g = PO("es", lambda e: e.tensor_tensor(esum[:, cs:SUP], esum[:, cs:SUP], EX[m2][:, cs:SUP],
                                                           ALU.add), [r, st8["esum"]])
                st8["esum"] = g
                st8["exr"][m2] = g
                eready[m2], css[m2] = r, cs
                if m2 == 1:
                    avs.extend(values(jb - 1, tuple(css), tuple(eready)))

            plan = [(jb, m, max(0, jb * 128 - I * SUP), jb * 128 >= I * SUP)
                    for jb in range(nblk) for m in range(4)]
            short = {}

            def gcol(jb, o):
                return G0[b % 2][:, jb * 16 + o:jb * 16 + o + 1] if jb < 4 else Gk[:, jb * 16 + o:jb * 16 + o + 1]

            def fill(n):
                jb, m, cs, _ = plan[n]
                w = SUP - cs
                k = 2 if w > 512 else 1
                s = st8["th"] % NTH
                if s + k > NTH:
                    s = 0
                if any(busy[s:s + k]):
                    return False
                st8["th"] = s + k
                tile = arena[:, th0_at + s * SUP:th0_at + (s + k) * SUP].rearrange("p (q t) -> p q t", q=4)
                for q in range(4):
                    v = VE("fill", lambda e, q=q: e.tensor_scalar(
                        tile[:, q, 0:w], Fq[:, I * SUP + cs:I * SUP + SUP], gcol(jb, 4 * q + m), None, ALU.add),
                        [th_free[x] for x in range(s, s + k)] + [gv[b, jb // 4]] + fw)
                for x in range(s, s + k):
                    busy[x] = True
                short[n] = (tile, list(range(s, s + k)), v)
                return True

            def fill_ahead(n):
                w = SUP - plan[n][2]
                for x in range(n, min(n + (4 if w <= 512 else 2), len(plan))):
                    if SUP - plan[x][2] <= 1024 and x not in short:
                        until(lambda: (b, plan[x][0] // 4) in gv)
                        if not fill(x):
                            assert x > n
                            return

            ended = None
            for n, (jb, m, cs, diag) in enumerate(plan):
                until(lambda: (b, jb // 4) in gv)
                if I == 0 and n == 0:
                    until(lambda: all((b, kk) in fv for kk in range(4)) and "copied" in f0state[b])
                fw = [fv[b, 4 * I + kk] for kk in range(4)] + ([f0state[b]["copied"]] if I == 0 else [])
                w = SUP - cs
                if w <= 1024:
                    while pieces:
                        pieces.pop(0)()
                    fill_ahead(n)
                    tile, sls, v = short.pop(n)
                    a = AC("th4", lambda e, tile=tile, w=w: e.activation(tile[:, :, 0:w], tile[:, :, 0:w], ACT.Tanh),
                           [v])
                    if ended and m == (1 if SUP - ended[1] <= 1024 else 0):
                        finish(*ended)
                        ended = None
                    elif avs and not (jb < 4 and m < 2 and "ended" not in epi and len(avs) == 4):
                        avs.pop(0)()
                    st8["thl"] = v
                    pieces = scores(m, [(tile[:, q, :], cs, a, sls[q % len(sls)]) for q in range(4)], cs, jb)
                    yield (4 * w * 0.000833 + 0.25) * 0.3
                else:
                    slots = []
                    for q in range(4):
                        sl = st8["th"] % NTH
                        assert not busy[sl]
                        busy[sl] = True
                        st8["th"] = sl + 1
                        lo = cs + (32 * q if diag else 0)
                        a = AC("th", lambda e, sl=sl, lo=lo, gc=gcol(jb, 4 * q + m): e.activation(
                            TH[sl][:, lo:SUP], Fq[:, I * SUP + lo:I * SUP + SUP], ACT.Tanh, bias=gc),
                            [th_free[sl], gv[b, jb // 4]] + fw)
                        slots.append((TH[sl][:, lo:SUP], lo, a, sl))
                        st8["thl"] = a
                        if q == 0:
                            for _ in range(4 if m == 0 else 2):
                                if pieces:
                                    pieces.pop(0)()
                        elif q == 1:
                            while pieces:
                                pieces.pop(0)()
                        elif q == 2:
                            if m == 0 and ended:
                                finish(*ended)
                                ended = None
                            elif avs and not (jb < 4 and m < 2 and "ended" not in epi and len(avs) == 4):
                                avs.pop(0)()
                            if n + 1 < len(plan) and SUP - plan[n + 1][2] <= 1024:
                                until(lambda: (b, plan[n + 1][0] // 4) in gv)
                                fill(n + 1)
                        else:
                            pieces = scores(m, slots, cs, jb)
                            pieces.pop(0)()
                        yield (SUP - lo) * 0.000833 + 0.3
                if m == 3:
                    ended = (jb, cs, diag)
            while pieces:
                pieces.pop(0)()
            finish(*ended)
            while avs:
                avs.pop(0)()

        f0state = {b: {} for b in range(NB)}

        def copy_f0(b, thw):
            v = VE("f0", lambda e: e.tensor_copy(Fq[:, 0:512], F0), [fv[b, 0], thw])
            free["F0"] = v
            f0state[b]["copied"] = v
            yield 0.5, True

        def marked(gen, state):
            yield from gen
            state.append("ended")

        first = mamba(0)
        while 4 not in t0v:
            next(first)
        Z1 = Norm("1", TH[5], EPd, TH[4][:, 0:512])
        streams = [first, prologue(0, [4, 6, 0], None, None), prologue(0, [5, 7], None, None, Z1)]
        while streams:
            for g in list(streams):
                if next(g, None) is None:
                    streams.remove(g)
        base[0] = 5
        epi = ["begun", "ended"]
        th0 = av0 = None
        AT = 950.0
        NP = max(1, NB // 2)
        MTs = [arena[:, a_ * L:a_ * L + L] for a_ in range(min(3, NP))]
        LG = arena[:, 12288:16384]
        X2 = [arena[:, 16384 + 512 * i:16896 + 512 * i].rearrange("p (k c) -> p k c", c=C) for i in range(2)]
        MS = [arena[:, 17408 + 512 * i:17920 + 512 * i].rearrange("p (k c) -> p k c", c=C) for i in range(2)]
        PT = arena[:, 18432:18432 + NE * NB].rearrange("p (e b) -> p e b", b=NB)
        T8 = arena[:, 18432 + 512:18432 + 528]
        gated = 0
        for b in range(NB):
            side.append(prologue(b, [1, 2, 3], th0, av0))
            side.append(copy_f0(b, th0))
            total = 1.05 * (8 * 20 + 3 * 17)
            if b + 1 < NB:
                side.append(mamba(b + 1))
                total += 1.05 * (4 * (14 + 19 + 15.5 + 16 * 8 + 28) + 30 + 5 * 17)
            else:
                def gates():
                    yield 1, True
                    ex = [p_last(PE), p_last(VE), p_last(AC), p_last(PO), t0s[NB - 1]]
                    for a_ in range(NP - 1):
                        yield from gate(a_, MTs[a_], LG, X2, MS, PT, T8, ex)
                side.append(gates())
                total += 110 * (NP - 1)
            rate = total / AT / 0.985
            spent = done = 0.0
            for I in (1, 0):
                state = []
                for cost in attention(b, I, epi):
                    spent += cost * (rate if "ended" in epi else rate if b + 1 < NB else max(rate, 1.0))
                    while (side or urgent) and done < spent:
                        done += step_side()
                    if not side:
                        done = spent
                epi = state
                second = None
                if b == NB - 1 and I == 0:
                    base[0] = 4
                    free["EPa2"] = p_last(AC)
                    second = (Norm("2", arena[:, 18960:19000], esum[:, 1536:SUP], EPc), Gk, F0)
                e_ = marked(epilogue(b, I, st8["acc"], st8["esum"], state, second), state)
                thw, avw = st8["thl"], st8["av"]
                urgent.append(e_)
                if I == 1 and b + 1 < NB:
                    side.append(prologue(b + 1, [4, 5, 6, 7, 0], thw, avw))
            th0, av0 = thw, avw
            until(lambda: not side)
        MT_a = NP - 1

        at = [attn0]

        def take(n):
            a = at[0]
            at[0] += n
            return arena[:, a:a + n]

        NG = NE // EG
        NW = 5
        MTl = take(L)
        WAB = [take(2 * EG * NH) for _ in range(NW)]
        TO0 = take(L)
        OT = TO0[:, 0:NE * NB].rearrange("p (e b) -> p e b", b=NB)
        assert at[0] <= attn0 + L + 28 * C + 8 * C + (NTH + 3) * SUP, at[0]
        MTs = MTs[:NP - 1] + [MTl]
        ends = [p_last(PE), p_last(VE), p_last(AC), p_last(PO)]
        wfree = [None] * NW
        ldw = {}
        blo = EPc

        def load_w(gi):
            s = gi % NW
            e0 = gi * EG
            SP("w%d" % s, lambda e: e.dma_start(WAB[s][:, 0:EG * NH].rearrange("p (e n) -> p e n", e=EG),
                                                we1[e0:e0 + EG, 0:C, :].rearrange("e p n -> p e n")),
               ends + [wfree[s]], 16)
            ldw[gi] = SP("w%d" % s, lambda e: e.dma_start(
                WAB[s][:, EG * NH:].rearrange("p (e k n) -> p e k n", e=EG, k=4),
                we2[e0:e0 + EG, 0:NH, :].rearrange("e (p k) n -> p e k n", k=4)), ends + [wfree[s]], 16)

        until(lambda: not side and not urgent)
        ends2 = [p_last(PE), p_last(VE)]
        nb2 = min(2, NB)
        W = nb2 * NE
        B1 = acc[0:NE, 0:NH]
        B2 = acc[0:NE, NH:NH + C]
        B1T = acc[:, 1024:1024 + 4 * NE].rearrange("p (k e) -> p k e", k=4)
        B2T = acc[:, 1280:1280 + NE]
        HB = [acc[:, 1408 + 128 * i:1408 + 128 * i + EG * 4 * NB] for i in range(2)]
        HH = [acc[:, 1664 + 128 * i:1664 + 128 * i + EG * 4 * NB] for i in range(2)]
        OE = EPd
        accw = free["acc"]
        db = SP("bias", lambda e: e.dma_start(B1, we1[:, C:C + 1, :].rearrange("e a n -> e (a n)")), accw, 16)
        db = SP("bias", lambda e: e.dma_start(B2, we2[:, NH:NH + 1, :].rearrange("e a n -> e (a n)")), accw, 16)
        g7 = gate(MT_a, MTl, LG, X2, MS, PT, T8, ends, TO0)
        next(g7)
        for gi in range(NW):
            load_w(gi)
        i, bf = bank()
        for k_ in range(4):
            p = PE("bt", lambda e, i=i, k_=k_: e.transpose(TR[:, i, NE * k_:NE * k_ + NE], B1[:, k_::4],
                                                           ident[0:NE, 0:NE]), [db, bf])
        p = PE("bt", lambda e, i=i: e.transpose(TR[:, i, 4 * NE:5 * NE], B2, ident[0:NE, 0:NE]))
        v = VE("bt", lambda e, i=i: e.tensor_copy(acc[:, 1024:1024 + 5 * NE], TR[:, i, 0:5 * NE]), [p])
        bank_free[i] = bt = v
        for _ in g7:
            pass

        hf, hbf = [None, None], [None, None]
        bank_f = {0: gt.pt, 1: gt.pt, 2: None, 3: None, 4: bank_free[4]}
        for i in range(5, 8):
            bank_f[i] = bank_free[i]
        tt = [0]

        def tbank():
            i = tt[0] % 8
            tt[0] += 1
            return i

        HR = TO0[:, 512:512 + NH]
        OR = TO0[:, 1024:1024 + C]
        hrf = orf = None
        late = None

        def out_layer(gi, a, s):
            i2 = tbank()
            hs = HH[gi % 2].rearrange("p (k e b) -> p k e b", e=EG, k=4)
            WB = WAB[s][:, EG * NH:].rearrange("p (e k n) -> p e k n", e=EG, k=4)
            for k_ in range(4):
                for e_ in range(EG):
                    p = PE("o", lambda e, e_=e_, k_=k_: e.matmul(
                        TR[32 * e_:32 * e_ + NB, i2, 0:C], hs[:, k_, e_, :], WB[:, e_, k_, :],
                        start=(k_ == 0), stop=(k_ == 3), skip_group_check=True), [a, bank_f[i2]])
            hf[gi % 2] = p
            wfree[s] = p
            v = VE("or", lambda e: e.tensor_copy(OR, TR[:, i2, 0:C]), [p, st8.get("orf")])
            i3 = tbank()
            p = PE("ot", lambda e: e.transpose(TR[:, i3, 0:128], OR, ident[:, :]), [v, bank_f[i3]])
            bank_f[i2] = v
            st8["orf"] = p
            v = VE("ot", lambda e: e.tensor_tensor(
                OT[:, gi * EG:gi * EG + EG, :], TR[:, i3, 0:128].rearrange("p (e b) -> p e b", b=32)[:, :, 0:NB],
                B2T[:, gi * EG:gi * EG + EG].unsqueeze(2).to_broadcast([128, EG, NB]), ALU.add), [p, bt])
            bank_f[i3] = v
            if gi + NW < NG:
                load_w(gi + NW)
            return v

        for gi in range(NG):
            s = gi % NW
            i1 = tbank()
            WA = WAB[s][:, 0:EG * NH].rearrange("p (e n) -> p e n", e=EG)
            for e_ in range(EG):
                p = PE("h", lambda e, e_=e_, gi=gi, i1=i1, WA=WA: e.matmul(
                    TR[32 * e_:32 * e_ + NB, i1, :], PT[:, gi * EG + e_, :], WA[:, e_, :], start=True, stop=True,
                    skip_group_check=True), [ldw[gi], gt.pt, bank_f[i1]])
            v = VE("hr", lambda e, i1=i1: e.tensor_copy(HR, TR[:, i1, :]), [p, hrf])
            bank_f[i1] = v
            if late:
                ov = out_layer(*late)
            i1 = tbank()
            for k_ in range(4):
                p = PE("ht", lambda e, k_=k_, i1=i1: e.transpose(TR[:, i1, 128 * k_:128 * k_ + 128], HR[:, k_::4],
                                                                 ident[:, :]), [v, bank_f[i1]])
            hrf = p
            hb = HB[gi % 2].rearrange("p (k e b) -> p k e b", e=EG, k=4)
            for k_ in range(4):
                v = VE("hb", lambda e, hb=hb, i1=i1, k_=k_, gi=gi: e.tensor_tensor(
                    hb[:, k_, :, :],
                    TR[:, i1, 128 * k_:128 * k_ + 128].rearrange("p (e b) -> p e b", b=32)[:, :, 0:NB],
                    B1T[:, k_, gi * EG:gi * EG + EG].unsqueeze(2).to_broadcast([128, EG, NB]), ALU.add),
                    [p, bt, hbf[gi % 2]])
            bank_f[i1] = v
            a = AC("gelu", lambda e, gi=gi: e.activation(HH[gi % 2], HB[gi % 2], ACT.Gelu), [v, hf[gi % 2]])
            hbf[gi % 2] = a
            late = (gi, a, s)
        ov = out_layer(*late)
        oe = []
        for a_ in range(NP):
            i = tbank()
            for bb in range(nb2):
                v2 = VE("otp", lambda e, a_=a_, bb=bb: e.tensor_copy(
                    acc[:, (2 * a_ + bb) * NE:(2 * a_ + bb) * NE + NE], OT[:, :, 2 * a_ + bb]), [ov, bt])
            p = PE("oe", lambda e, i=i, a_=a_: e.transpose(
                TR[0:W, i, 0:128], acc[:, 2 * a_ * NE:2 * a_ * NE + W], ident[:, :]), [v2, bank_f[i]])
            w = VE("oe", lambda e, i=i, a_=a_: e.tensor_copy(OE[0:W, 128 * a_:128 * a_ + 128], TR[0:W, i, 0:128]),
                   [p])
            bank_f[i] = w
            oe.append(w)
        tof = {}
        fin = []
        for b in range(NB):
            s = b % NW
            t_ = WAB[s]
            d = SP("tl%d" % s, lambda e, b=b, t_=t_: e.dma_start(t_, t1d[b]), [tof.get(s), wfree[s]] + stored[b], 16)
            lo = (b % 2) * NE
            for c in range(8):
                i = tbank()
                p = PE("fo", lambda e, i=i, c=c, lo=lo, b=b: e.matmul(
                    TR[:, i, :], OE[lo:lo + NE, 128 * (b // 2):128 * (b // 2) + 128],
                    MTs[b // 2][lo:lo + NE, 512 * c:512 * c + 512], start=True, stop=True),
                    oe + [bank_f[i], gt.m])
                v = VE("fo", lambda e, i=i, c=c, t_=t_: e.tensor_tensor(
                    t_[:, 512 * c:512 * c + 512], t_[:, 512 * c:512 * c + 512], TR[:, i, :], ALU.add), [p, d])
                bank_f[i] = v
            d = SP("out%d" % s, lambda e, b=b, t_=t_: e.dma_start(od[b], t_), [v], 16)
            tof[s] = d
            fin.append(d)
        SP("end", lambda e: None, fin)

        emit = flush([PE, VE, AC, PO, SP], lambda n: ctx.enter_context(nc.semaphore(n)))
        ctx.enter_context(nc.allow_non_contiguous_dma(reason="small constants, strided rows"))
        block = ctx.enter_context(nc.Block())

        @block.tensor
        def _(e):
            emit(PE, e)

        @block.vector
        def _(e):
            emit(VE, e)

        @block.scalar
        def _(e):
            emit(AC, e)

        @block.gpsimd
        def _(e):
            emit(PO, e)

        @block.sync
        def _(e):
            emit(SP, e)


_INS = ["x", "L0_conv_W_in", "L0_conv_conv_w", "L0_conv_conv_b", "L0_conv_W_x", "L0_conv_W_dt", "L0_conv_b_dt",
        "L0_conv_A_log", "L0_conv_D", "L0_conv_W_out", "L0_conv_gn_gamma", "L0_conv_gn_beta", "L1_attn_W1",
        "L1_attn_b1", "L1_attn_w2", "L1_attn_b2", "L1_ffn_gate_w", "L1_ffn_gate_b", "L1_ffn_weight1",
        "L1_ffn_weight2"]


def kernel(**inputs):
    import numpy as _np
    import concourse.bacc as _bacc
    from concourse import mybir as _mybir
    from concourse.bass_utils import run_bass_kernel_spmd as _run

    nc = _bacc.Bacc("TRN2", target_bir_lowering=False, num_devices=1, dynamic_dma_scratch_size=1024)
    arrays, args = {}, []
    for name in _INS:
        a = _np.ascontiguousarray(inputs[name])
        arrays[f"in_{name}_dram"] = a
        args.append(nc.dram_tensor(f"in_{name}_dram", a.shape, _mybir.dt.from_np(a.dtype), kind="ExternalInput").ap())
    shape = inputs["x"].shape
    out = nc.dram_tensor("out_0_dram", shape, _mybir.dt.float32, kind="ExternalOutput").ap()
    hybrid_kernel(nc, shape[0], *args, out)
    r = _run(nc, [arrays], core_ids=[0])
    return r.results[0]["out_0_dram"]
```
